# Optimizing a Trainium2 kernel written in Bass

```python
import numpy as np
import jax
import jax.numpy as jnp

def _softmax(x, axis=-1):
    return jax.nn.softmax(x, axis=axis)

def _gelu(x):
    return jax.nn.gelu(x, approximate=True)

def _silu(x):
    return jax.nn.silu(x)

def _sigmoid(x):
    return jax.nn.sigmoid(x)

def _layernorm(x, axis=-1, eps=1e-05):
    m = jnp.mean(x, axis=axis, keepdims=True)
    v = jnp.var(x, axis=axis, keepdims=True)
    return (x - m) / jnp.sqrt(v + eps)

def _scatter_add(tgt, idx, src, axis=0):
    return tgt.at[idx].add(src)

def _segment_sum(src, seg, n):
    return jax.ops.segment_sum(src, seg, n)
kernel_name = 'mk_sandwich_d1_jaxref_r8_2f03ac'

def setup_inputs(seed: int=0):
    np.random.seed(seed)
    _w = jnp.asarray

    def _L0_attn_setup():
        import jax, jax.numpy as jnp
        import numpy as np
        D_MODEL = 128
        D_STATE = 16
        D_CONV = 4
        EXPAND = 2
        D_INNER = EXPAND * D_MODEL
        DT_RANK = (D_MODEL + 15) // 16
        BATCH = 2
        SEQ = 256
        EPS = 1e-05

        def _mamba_params(key, scale=0.02):
            ks = jax.random.split(key, 8)
            n = lambda k, s: jax.random.normal(k, s, jnp.float32) * scale
            return {'Win': n(ks[0], (2 * D_INNER, D_MODEL)), 'convw': n(ks[1], (D_INNER, 1, D_CONV)), 'convb': n(ks[2], (D_INNER,)), 'Wx': n(ks[3], (DT_RANK + 2 * D_STATE, D_INNER)), 'Wdt': n(ks[4], (D_INNER, DT_RANK)), 'bdt': n(ks[5], (D_INNER,)), 'Alog': jnp.log(jnp.tile(jnp.arange(1, D_STATE + 1, dtype=jnp.float32), (D_INNER, 1))), 'D': jnp.ones((D_INNER,), jnp.float32), 'Wout': n(ks[6], (D_MODEL, D_INNER))}

        def _mamba(x, Win, convw, convb, Wx, Wdt, bdt, Alog, Dp, Wout):
            B, L, _ = x.shape
            xz = jnp.einsum('bld,ed->ble', x, Win)
            u, z = jnp.split(xz, 2, axis=-1)
            uc = jnp.transpose(u, (0, 2, 1))
            uc = jnp.pad(uc, ((0, 0), (0, 0), (D_CONV - 1, 0)))
            uc = jax.lax.conv_general_dilated(uc, convw, (1,), 'VALID', feature_group_count=D_INNER)
            uc = uc + convb[None, :, None]
            u = jax.nn.silu(jnp.transpose(uc, (0, 2, 1)))
            xdbl = jnp.einsum('bld,ed->ble', u, Wx)
            dtr, Bm, Cm = jnp.split(xdbl, [DT_RANK, DT_RANK + D_STATE], axis=-1)
            dt = jax.nn.softplus(jnp.einsum('blr,dr->bld', dtr, Wdt) + bdt)
            A = -jnp.exp(Alog)

            def step(h, ins):
                dt_t, u_t, B_t, C_t = ins
                h = jnp.exp(dt_t[..., None] * A) * h + (dt_t * u_t)[..., None] * B_t[:, None, :]
                y_t = jnp.einsum('bdn,bn->bd', h, C_t)
                return (h, y_t)
            h0 = jnp.zeros((B, D_INNER, D_STATE), jnp.float32)
            xs = (jnp.moveaxis(dt, 1, 0), jnp.moveaxis(u, 1, 0), jnp.moveaxis(Bm, 1, 0), jnp.moveaxis(Cm, 1, 0))
            _, ys = jax.lax.scan(step, h0, xs)
            y = jnp.moveaxis(ys, 0, 1) + u * Dp
            y = y * jax.nn.silu(z)
            return jnp.einsum('bld,ed->ble', y, Wout)
        key = jax.random.key(seed)
        kx, kf, kb = jax.random.split(key, 3)
        inp = {'x': jax.random.normal(kx, (BATCH, SEQ, D_MODEL), jnp.float32), 'norm_g': jnp.ones((D_MODEL,), jnp.float32), 'norm_b': jnp.zeros((D_MODEL,), jnp.float32)}
        for pfx, k in (('f', kf), ('b', kb)):
            for name, v in _mamba_params(k).items():
                inp[f'{pfx}_{name}'] = v
        return inp
    _L0_attn_in = _L0_attn_setup()

    def _L0_ffn_setup():
        import jax, jax.numpy as jnp
        import numpy as np
        HID = 128
        NH = 16
        NKV = 4
        HD = HID // NH
        E = 8
        TOPK = 2
        FFN = 256
        EPS = 1e-05
        THETA = 10000.0

        def _rmsnorm(x, w):
            var = jnp.mean(x * x, axis=-1, keepdims=True)
            return x * jax.lax.rsqrt(var + EPS) * w

        def _rope_tables(S):
            inv_freq = 1.0 / THETA ** (jnp.arange(0, HD, 2, dtype=jnp.float32) / HD)
            freqs = jnp.arange(S, dtype=jnp.float32)[:, None] * inv_freq[None, :]
            emb = jnp.concatenate([freqs, freqs], axis=-1)
            return (jnp.cos(emb), jnp.sin(emb))

        def _apply_rope(t, cos, sin):
            t1, t2 = jnp.split(t, 2, axis=-1)
            rot = jnp.concatenate([-t2, t1], axis=-1)
            return t * cos[None, :, None, :] + rot * sin[None, :, None, :]
        key = jax.random.key(seed)
        ks = jax.random.split(key, 6)
        B, S = (1, 256)
        x = jax.random.normal(ks[0], (B, S, HID), dtype=jnp.float32)
        wqkv = jax.random.normal(ks[1], ((NH + 2 * NKV) * HD, HID), dtype=jnp.float32) * 0.02
        wo = jax.random.normal(ks[2], (HID, NH * HD), dtype=jnp.float32) * 0.02
        gate_w = jax.random.normal(ks[3], (E, HID), dtype=jnp.float32) * 0.02
        w13 = jax.random.normal(ks[4], (E, 2 * FFN, HID), dtype=jnp.float32) * 0.02
        w2 = jax.random.normal(ks[5], (E, HID, FFN), dtype=jnp.float32) * 0.02
        return {'x': x, 'ln1_w': jnp.ones((HID,), jnp.float32), 'ln2_w': jnp.ones((HID,), jnp.float32), 'wqkv': wqkv, 'wo': wo, 'gate_w': gate_w, 'w13': w13, 'w2': w2}
    _L0_ffn_in = _L0_ffn_setup()
    _d = {'L0_attn_x': _L0_attn_in['x'], 'L0_attn_norm_g': _L0_attn_in['norm_g'], 'L0_attn_norm_b': _L0_attn_in['norm_b'], 'L0_attn_f_Win': _L0_attn_in['f_Win'], 'L0_attn_f_convw': _L0_attn_in['f_convw'], 'L0_attn_f_convb': _L0_attn_in['f_convb'], 'L0_attn_f_Wx': _L0_attn_in['f_Wx'], 'L0_attn_f_Wdt': _L0_attn_in['f_Wdt'], 'L0_attn_f_bdt': _L0_attn_in['f_bdt'], 'L0_attn_f_Alog': _L0_attn_in['f_Alog'], 'L0_attn_f_D': _L0_attn_in['f_D'], 'L0_attn_f_Wout': _L0_attn_in['f_Wout'], 'L0_attn_b_Win': _L0_attn_in['b_Win'], 'L0_attn_b_convw': _L0_attn_in['b_convw'], 'L0_attn_b_convb': _L0_attn_in['b_convb'], 'L0_attn_b_Wx': _L0_attn_in['b_Wx'], 'L0_attn_b_Wdt': _L0_attn_in['b_Wdt'], 'L0_attn_b_bdt': _L0_attn_in['b_bdt'], 'L0_attn_b_Alog': _L0_attn_in['b_Alog'], 'L0_attn_b_D': _L0_attn_in['b_D'], 'L0_attn_b_Wout': _L0_attn_in['b_Wout'], 'L0_ffn_ln1_w': _L0_ffn_in['ln1_w'], 'L0_ffn_ln2_w': _L0_ffn_in['ln2_w'], 'L0_ffn_wqkv': _L0_ffn_in['wqkv'], 'L0_ffn_wo': _L0_ffn_in['wo'], 'L0_ffn_gate_w': _L0_ffn_in['gate_w'], 'L0_ffn_w13': _L0_ffn_in['w13'], 'L0_ffn_w2': _L0_ffn_in['w2']}
    _x0 = _d['L0_attn_x']
    _d['L0_attn_x'] = jax.random.normal(jax.random.fold_in(jax.random.key(seed), 1), (8, 512, 128), dtype=_x0.dtype)
    del _x0
    return _d

def reference(L0_attn_x, L0_attn_norm_g, L0_attn_norm_b, L0_attn_f_Win, L0_attn_f_convw, L0_attn_f_convb, L0_attn_f_Wx, L0_attn_f_Wdt, L0_attn_f_bdt, L0_attn_f_Alog, L0_attn_f_D, L0_attn_f_Wout, L0_attn_b_Win, L0_attn_b_convw, L0_attn_b_convb, L0_attn_b_Wx, L0_attn_b_Wdt, L0_attn_b_bdt, L0_attn_b_Alog, L0_attn_b_D, L0_attn_b_Wout, L0_ffn_ln1_w, L0_ffn_ln2_w, L0_ffn_wqkv, L0_ffn_wo, L0_ffn_gate_w, L0_ffn_w13, L0_ffn_w2):

    def _L0_attn_ref(x, norm_g, norm_b, f_Win, f_convw, f_convb, f_Wx, f_Wdt, f_bdt, f_Alog, f_D, f_Wout, b_Win, b_convw, b_convb, b_Wx, b_Wdt, b_bdt, b_Alog, b_D, b_Wout):
        import jax, jax.numpy as jnp
        import numpy as np
        D_MODEL = 128
        D_STATE = 16
        D_CONV = 4
        EXPAND = 2
        D_INNER = EXPAND * D_MODEL
        DT_RANK = (D_MODEL + 15) // 16
        BATCH = 2
        SEQ = 256
        EPS = 1e-05

        def _mamba_params(key, scale=0.02):
            ks = jax.random.split(key, 8)
            n = lambda k, s: jax.random.normal(k, s, jnp.float32) * scale
            return {'Win': n(ks[0], (2 * D_INNER, D_MODEL)), 'convw': n(ks[1], (D_INNER, 1, D_CONV)), 'convb': n(ks[2], (D_INNER,)), 'Wx': n(ks[3], (DT_RANK + 2 * D_STATE, D_INNER)), 'Wdt': n(ks[4], (D_INNER, DT_RANK)), 'bdt': n(ks[5], (D_INNER,)), 'Alog': jnp.log(jnp.tile(jnp.arange(1, D_STATE + 1, dtype=jnp.float32), (D_INNER, 1))), 'D': jnp.ones((D_INNER,), jnp.float32), 'Wout': n(ks[6], (D_MODEL, D_INNER))}

        def _mamba(x, Win, convw, convb, Wx, Wdt, bdt, Alog, Dp, Wout):
            B, L, _ = x.shape
            xz = jnp.einsum('bld,ed->ble', x, Win)
            u, z = jnp.split(xz, 2, axis=-1)
            uc = jnp.transpose(u, (0, 2, 1))
            uc = jnp.pad(uc, ((0, 0), (0, 0), (D_CONV - 1, 0)))
            uc = jax.lax.conv_general_dilated(uc, convw, (1,), 'VALID', feature_group_count=D_INNER)
            uc = uc + convb[None, :, None]
            u = jax.nn.silu(jnp.transpose(uc, (0, 2, 1)))
            xdbl = jnp.einsum('bld,ed->ble', u, Wx)
            dtr, Bm, Cm = jnp.split(xdbl, [DT_RANK, DT_RANK + D_STATE], axis=-1)
            dt = jax.nn.softplus(jnp.einsum('blr,dr->bld', dtr, Wdt) + bdt)
            A = -jnp.exp(Alog)

            def step(h, ins):
                dt_t, u_t, B_t, C_t = ins
                h = jnp.exp(dt_t[..., None] * A) * h + (dt_t * u_t)[..., None] * B_t[:, None, :]
                y_t = jnp.einsum('bdn,bn->bd', h, C_t)
                return (h, y_t)
            h0 = jnp.zeros((B, D_INNER, D_STATE), jnp.float32)
            xs = (jnp.moveaxis(dt, 1, 0), jnp.moveaxis(u, 1, 0), jnp.moveaxis(Bm, 1, 0), jnp.moveaxis(Cm, 1, 0))
            _, ys = jax.lax.scan(step, h0, xs)
            y = jnp.moveaxis(ys, 0, 1) + u * Dp
            y = y * jax.nn.silu(z)
            return jnp.einsum('bld,ed->ble', y, Wout)
        mu = jnp.mean(x, axis=-1, keepdims=True)
        var = jnp.var(x, axis=-1, keepdims=True)
        xn = (x - mu) * jax.lax.rsqrt(var + EPS) * norm_g + norm_b
        y_fwd = _mamba(xn, f_Win, f_convw, f_convb, f_Wx, f_Wdt, f_bdt, f_Alog, f_D, f_Wout)
        y_bwd = _mamba(jnp.flip(xn, axis=1), b_Win, b_convw, b_convb, b_Wx, b_Wdt, b_bdt, b_Alog, b_D, b_Wout)
        y_bwd = jnp.flip(y_bwd, axis=1)
        return x + y_fwd + y_bwd

    def _L0_ffn_ref(x, ln1_w, ln2_w, wqkv, wo, gate_w, w13, w2):
        import jax, jax.numpy as jnp
        import numpy as np
        HID = 128
        NH = 16
        NKV = 4
        HD = HID // NH
        E = 8
        TOPK = 2
        FFN = 256
        EPS = 1e-05
        THETA = 10000.0

        def _rmsnorm(x, w):
            var = jnp.mean(x * x, axis=-1, keepdims=True)
            return x * jax.lax.rsqrt(var + EPS) * w

        def _rope_tables(S):
            inv_freq = 1.0 / THETA ** (jnp.arange(0, HD, 2, dtype=jnp.float32) / HD)
            freqs = jnp.arange(S, dtype=jnp.float32)[:, None] * inv_freq[None, :]
            emb = jnp.concatenate([freqs, freqs], axis=-1)
            return (jnp.cos(emb), jnp.sin(emb))

        def _apply_rope(t, cos, sin):
            t1, t2 = jnp.split(t, 2, axis=-1)
            rot = jnp.concatenate([-t2, t1], axis=-1)
            return t * cos[None, :, None, :] + rot * sin[None, :, None, :]
        B, S, _ = x.shape
        h = _rmsnorm(x, ln1_w)
        qkv = jnp.einsum('bsh,oh->bso', h, wqkv)
        q = qkv[..., :NH * HD].reshape(B, S, NH, HD)
        k = qkv[..., NH * HD:(NH + NKV) * HD].reshape(B, S, NKV, HD)
        v = qkv[..., (NH + NKV) * HD:].reshape(B, S, NKV, HD)
        cos, sin = _rope_tables(S)
        q = _apply_rope(q, cos, sin)
        k = _apply_rope(k, cos, sin)
        groups = NH // NKV
        k = jnp.repeat(k, groups, axis=2)
        v = jnp.repeat(v, groups, axis=2)
        scale = HD ** (-0.5)
        scores = jnp.einsum('bqhd,bkhd->bhqk', q, k) * scale
        causal = jnp.tril(jnp.ones((S, S), dtype=bool))
        scores = jnp.where(causal[None, None], scores, jnp.finfo(scores.dtype).min)
        probs = jax.nn.softmax(scores, axis=-1)
        attn = jnp.einsum('bhqk,bkhd->bqhd', probs, v).reshape(B, S, NH * HD)
        x = x + jnp.einsum('bso,ho->bsh', attn, wo)
        h = _rmsnorm(x, ln2_w).reshape(-1, HID)
        T = h.shape[0]
        logits = jnp.einsum('th,eh->te', h, gate_w)
        rprobs = jax.nn.softmax(logits.astype(jnp.float32), axis=-1)
        topw, topi = jax.lax.top_k(rprobs, TOPK)
        topw = topw / jnp.sum(topw, axis=-1, keepdims=True)
        wfull = jnp.zeros((T, E), jnp.float32).at[jnp.arange(T)[:, None], topi].set(topw)
        wfull = wfull.astype(h.dtype)
        out = jnp.zeros((T, HID), h.dtype)
        for e in range(E):
            w1 = w13[e, :FFN]
            w3 = w13[e, FFN:]
            g = jax.nn.silu(h @ w1.T) * (h @ w3.T)
            out = out + jnp.einsum('tf,hf->th', g, w2[e]) * wfull[:, e:e + 1]
        return x + out.reshape(B, S, HID)
    x = L0_attn_x
    x = x + _layernorm(_L0_attn_ref(_layernorm(x, axis=-1), L0_attn_norm_g, L0_attn_norm_b, L0_attn_f_Win, L0_attn_f_convw, L0_attn_f_convb, L0_attn_f_Wx, L0_attn_f_Wdt, L0_attn_f_bdt, L0_attn_f_Alog, L0_attn_f_D, L0_attn_f_Wout, L0_attn_b_Win, L0_attn_b_convw, L0_attn_b_convb, L0_attn_b_Wx, L0_attn_b_Wdt, L0_attn_b_bdt, L0_attn_b_Alog, L0_attn_b_D, L0_attn_b_Wout), axis=-1)
    x = x + _layernorm(_L0_ffn_ref(_layernorm(x, axis=-1), L0_ffn_ln1_w, L0_ffn_ln2_w, L0_ffn_wqkv, L0_ffn_wo, L0_ffn_gate_w, L0_ffn_w13, L0_ffn_w2), axis=-1)
    return x

_drawn_inputs = setup_inputs


def setup_inputs(seed=0):
    import zlib

    import numpy as np

    out = dict(_drawn_inputs(seed))
    spreads = {'L0_attn_norm_g': (1.0, 0.6),
     'L0_attn_norm_b': (0.0, 0.8),
     'L0_attn_f_D': (1.0, 0.6),
     'L0_attn_b_D': (1.0, 0.6),
     'L0_ffn_ln1_w': (1.0, 0.6),
     'L0_ffn_ln2_w': (1.0, 0.6)}
    factors = {'L0_attn_f_Win': 8.0,
     'L0_attn_f_convw': 8.0,
     'L0_attn_f_convb': 8.0,
     'L0_attn_f_Wx': 8.0,
     'L0_attn_f_Wdt': 8.0,
     'L0_attn_f_bdt': 8.0,
     'L0_attn_f_Alog': 8.0,
     'L0_attn_f_Wout': 8.0,
     'L0_attn_b_Win': 8.0,
     'L0_attn_b_convw': 8.0,
     'L0_attn_b_convb': 8.0,
     'L0_attn_b_Wx': 8.0,
     'L0_attn_b_Wdt': 8.0,
     'L0_attn_b_bdt': 8.0,
     'L0_attn_b_Alog': 8.0,
     'L0_attn_b_Wout': 8.0,
     'L0_ffn_wqkv': 8.0,
     'L0_ffn_wo': 8.0,
     'L0_ffn_gate_w': 8.0,
     'L0_ffn_w13': 8.0,
     'L0_ffn_w2': 8.0}
    for name, (base, spread) in spreads.items():
        noise = np.random.default_rng([zlib.crc32(name.encode()), seed]).standard_normal(out[name].shape)
        drawn = base * np.exp(spread * noise) if base else spread * noise
        out[name] = jnp.asarray(drawn.astype(out[name].dtype))
    for name, factor in factors.items():
        out[name] = (out[name] * factor).astype(out[name].dtype)
    return out
```

```python
from contextlib import ExitStack

import numpy as np

import concourse.bass as bass
from concourse import mybir

ALU = mybir.AluOpType
ACT = mybir.ActivationFunctionType
F32 = mybir.dt.float32
BF16 = mybir.dt.bfloat16

P = 128
NB = 8
SEQ = 512
DM = 128
TC = SEQ // P
DI = 256
NH2 = DI // P
NS = 16
NTAP = 4
DTR = 8
NDIR = 2
STEPS = NS * NH2
EPS = 1e-5
SPLIT_ROWS = 3 * 32
DT_ROW = 96


class Counts:

    def __init__(self):
        self.per, self.ahead = {}, {}

    def add(self, sem, per, credited):
        self.per[sem.name], self.ahead[sem.name] = per, per if credited else 0

    def __call__(self, sem, b, c):
        per, ahead = self.per[sem.name], self.ahead[sem.name]
        assert c >= 1 or (ahead and c > -per), (sem.name, c)
        value = b * per + c + ahead
        assert not isinstance(value, int) or value > 0, (sem.name, b, c)
        return value

    def in_register(self, eng, sem, b, c):
        value = self(sem, b, c)
        return value if isinstance(value, int) else eng.to_reg(value)


def is_first(b):
    return isinstance(b, int) and b == 0


def mamba_phase(nc, sems, x, x1, cscr, w):
    with ExitStack() as ctx:
        def sb(name, shape, dt=F32):
            return ctx.enter_context(nc.sbuf_tensor(name, shape, dt))

        def pb(name, shape):
            return ctx.enter_context(nc.psum_tensor(name, shape, F32))

        count = Counts()
        credited = {e: [] for e in ("sync", "tensor", "scalar", "vector", "gpsimd")}

        def sig(name, per, producer=None):
            s = sems.enter_context(nc.semaphore(name))
            count.add(s, per, producer is not None)
            if producer is not None:
                credited[producer].append((s, per))
            return s

        ident = sb("ident", [P, P])
        win_u = sb("win_u", [P, NDIR, DI])
        win_z = sb("win_z", [P, NDIR, DI])
        wu = sb("wu", [P, NDIR, NTAP, DI])
        wx = sb("wx", [P, NDIR, NH2, P])
        wdt = sb("wdt", [P, NDIR, DI])
        wout = sb("wout", [P, NDIR, NH2, DM])
        col = sb("col", [P, NDIR, NH2, 3])
        a_neg = sb("a_neg", [P, NDIR, NH2, NS])
        ncol = sb("ncol", [P, 2])
        sel = sb("sel", [SPLIT_ROWS, NS, P], BF16)
        mhalf = sb("mhalf", [P, TC])
        eps = sb("eps", [P, TC])
        xin = sb("xin", [P, TC, DM])
        xln = sb("xln", [P, TC, DM])
        xres = sb("xres", [P, 2, TC, DM])
        xn = sb("xn", [P, TC, DM])
        stats = sb("stats", [P, 2, TC, 6])
        mv = sb("mv", [P, 2, TC, 2])
        rstd = sb("rstd", [P, 2, 2, TC])
        xpad = sb("xpad", [P, NDIR, NTAP - 1 + SEQ])
        u = sb("u", [P, NH2, SEQ])
        sz = sb("sz", [P, NDIR, TC, DI])
        xd = sb("xd", [P, SEQ])
        st = sb("st", [SPLIT_ROWS, NDIR, SEQ], BF16)
        rem = sb("rem", [SPLIT_ROWS, SEQ])
        mid2 = sb("mid2", [SPLIT_ROWS, SEQ], BF16)
        t_abs = sb("t_abs", [P, SEQ])
        t_exp = sb("t_exp", [P, SEQ])
        t_ln = sb("t_ln", [P, NH2, SEQ])
        t_relu = sb("t_relu", [P, NH2, SEQ])
        dt = sb("dt", [P, NDIR, NH2, SEQ])
        dtu = sb("dtu", [P, NDIR, NH2, SEQ])
        ud = sb("ud", [P, NH2, SEQ])
        cb = sb("cb", [P, NDIR, NS, SEQ])
        yg = sb("yg", [P, TC, DI])
        ygt = sb("ygt", [P, NDIR, NH2, SEQ])
        res = sb("res", [P, TC, DM])
        x1t = sb("x1t", [P, TC, DM])
        NDA, NHB, NHC = 8, 4, 4
        da = sb("da", [P, NDA, SEQ])
        sel32 = da[0:SPLIT_ROWS, 0:NS * P // SEQ, :].rearrange("r a (n p) -> r (a n) p", p=P)
        hb = sb("hb", [P, NHB, SEQ])
        hc = sb("hc", [P, NHC, SEQ])
        bp = pb("bp", [P, 2, SEQ])
        dbu = pb("dbu", [P, 2, SEQ])
        yp = pb("yp", [P, TC, DI])
        wp = pb("wp", [P, 2, SEQ])

        weights_loaded = sems.enter_context(nc.semaphore("weights_loaded"))
        taps_folded = sems.enter_context(nc.semaphore("taps_folded"))
        sel_cast = sems.enter_context(nc.semaphore("sel_cast"))
        a_ready = sems.enter_context(nc.semaphore("a_ready"))
        consts_set = sems.enter_context(nc.semaphore("consts_set"))

        x_loaded = sig("x_loaded", 16)
        x_kept = sig("x_kept", 32, "sync")
        c_written = sig("c_written", 32, "sync")
        c_bcast = sig("c_bcast", 32, "sync")
        x1_stored = sig("x1_stored", 16, "sync")

        xt_ready = sig("xt_ready", 1, "tensor")
        u_ready = sig("u_ready", 4)
        z_ready = sig("z_ready", 4, "tensor")
        xd_ready = sig("xd_ready", 2, "tensor")
        dtp_ready = sig("dtp_ready", 4, "tensor")
        b_ready = sig("b_ready", NDIR * NS, "tensor")
        y_added = sig("y_added", NDIR * (STEPS + 1), "tensor")
        ygt_ready = sig("ygt_ready", 4, "tensor")
        out_ready = sig("out_ready", 1, "tensor")

        xpad_done = sig("xpad_done", 2)
        silu_done = sig("silu_done", 8)
        xd_done = sig("xd_done", 8, "scalar")
        soft_done = sig("soft_done", 16, "scalar")
        ud_done = sig("ud_done", 4)
        da_done = sig("da_done", NDIR * STEPS, "scalar")
        ygt_done = sig("ygt_done", 4, "scalar")

        ln_step = sig("ln_step", 24, "vector")
        end_step = sig("end_step", 12, "vector")
        part_done = sig("part_done", 2, "vector")
        dt_done = sig("dt_done", 4, "vector")
        dbu_done = sig("dbu_done", NDIR * STEPS, "vector")
        scan_done = sig("scan_done", NDIR * STEPS, "vector")
        yg_done = sig("yg_done", 2, "vector")
        res_done = sig("res_done", 1, "vector")
        x1_done = sig("x1_done", 1, "vector")

        rstd_done = sig("rstd_done", 4)
        end_rstd = sig("end_rstd", 2)
        rem_done = sig("rem_done", 2, "gpsimd")
        hc_done = sig("hc_done", NDIR * STEPS, "gpsimd")

        block = ctx.enter_context(nc.Block())
        weights = ((ident, "ident"), (win_u, "win_u"), (win_z, "win_z"), (wu, "tap_w"), (wx, "wx"),
                   (wdt, "wdt"), (wout, "wout"), (col, "col"), (a_neg, "alog"), (ncol, "ncol"), (sel32, "sel"))
        n_weights = 16 * len(weights)

        def y_count(d, s):
            return (STEPS + 1) * d + s + (2 if s >= 0 else 1)

        def sp_x_load(sp, b, first=False):
            if not first:
                sp.wait_ge(ln_step, count(ln_step, b, 12 - 24))
                sp.wait_ge(x_kept, count(x_kept, b, 0))
            sp.dma_start(xin[:, :, :].rearrange("p (a c) m -> p a c m", a=1),
                         x[bass.ds(b, 1)].rearrange("a (c p) m -> p a c m", p=P)).then_inc(x_loaded, 16)

        def sp_keep(sp, b):
            sp.wait_ge(ln_step, count(ln_step, b, 12))
            sp.wait_ge(x1_done, count(x1_done, b, 0))
            sp.dma_start(xres[:, 0], xin[:, :, :]).then_inc(x_kept, 16)
            sp.dma_start(xres[:, 1], xln[:, :, :]).then_inc(x_kept, 16)

        def sp_c(sp, b, d):
            xd_now = count.in_register(sp, xd_done, b, 4 * d + 2)
            c_before = count.in_register(sp, c_bcast, b, 16 * d - 16)
            sp.wait_ge(xd_done, xd_now)
            sp.wait_ge(c_bcast, c_before)
            sp.dma_start(cscr[d], xd[NS:2 * NS, :]).then_inc(c_written, 16)
            written = count.in_register(sp, c_written, b, 16 * d + 16)
            hc_before = count.in_register(sp, hc_done, b, STEPS * (d - 1))
            sp.wait_ge(c_written, written)
            sp.wait_ge(hc_done, hc_before)
            sp.dma_start(cb[:, d], cscr[d:d + 1].to_broadcast([P, NS, SEQ])).then_inc(c_bcast, 16)

        def sp_store(sp, b):
            sp.wait_ge(x1_done, count(x1_done, b, 1))
            sp.dma_start(x1[bass.ds(b, 1)].rearrange("a (c p) m -> p a c m", p=P),
                         x1t[:, :, :].rearrange("p (a c) m -> p a c m", a=1)).then_inc(x1_stored, 16)

        @block.sync
        def _(sp):
            for s, per in credited["sync"]:
                sp.sem_inc(s, per)
            sp_x_load(sp, 0, first=True)
            for dst, name in weights:
                sp.dma_start(dst[...], w[name]).then_inc(weights_loaded, 16)
            sp_c(sp, 0, 0)
            sp_keep(sp, 0)
            sp_c(sp, 0, 1)
            with sp.Fori(0, NB - 1) as b:
                sp_x_load(sp, b + 1)
                sp_c(sp, b + 1, 0)
                sp_store(sp, b)
                sp_keep(sp, b + 1)
                sp_c(sp, b + 1, 1)
            sp_store(sp, NB - 1)
            sp.wait_ge(x1_stored, count(x1_stored, NB - 1, 16))

        def pe_xt(pe, b, first=False):
            pe.wait_ge(ln_step, count(ln_step, b, 24))
            if not first:
                pe.wait_ge(ygt_done, count(ygt_done, b - 1, 2))
            for c in range(TC):
                last = nc.tensor.transpose(wp[:, 1, c * P:(c + 1) * P], xn[:, c, :], ident[:, :])
            last.then_inc(xt_ready, 1)

        def pe_u(pe, b, d, h, first=False):
            pe.wait_ge(xpad_done, count(xpad_done, b, 2))
            if not first and h == 0:
                if d:
                    pe.wait_ge(res_done, count(res_done, b, 0))
                    pe.wait_ge(ygt_done, count(ygt_done, b, 0))
                else:
                    pe.wait_ge(ygt_done, count(ygt_done, b - 1, 2))
            for j in range(NTAP):
                last = nc.tensor.matmul(wp[:, h, :], wu[:, d, j, h * P:(h + 1) * P], xpad[:, d, j:j + SEQ],
                                        start=(j == 0), stop=(j == NTAP - 1))
            last.then_inc(u_ready, 1)

        def pe_z(pe, b, d, k):
            pe.wait_ge(silu_done, count(silu_done, b, 4 * d + k + 1))
            for c in (2 * k, 2 * k + 1):
                last = nc.tensor.matmul(wp[:, k, (c % 2) * DI:(c % 2 + 1) * DI],
                                        xpad[:, d, NTAP - 1 + c * P:NTAP - 1 + (c + 1) * P], win_z[:, d, :],
                                        start=True, stop=True)
            last.then_inc(z_ready, 1)

        def pe_xd(pe, b, d):
            pe.wait_ge(silu_done, count(silu_done, b, 4 * d + 3))
            for h in range(NH2):
                last = nc.tensor.matmul(wp[:, 0, :], wx[:, d, h, :], u[:, h, :], start=(h == 0), stop=(h == 1))
            last.then_inc(xd_ready, 1)

        def pe_dt(pe, b, d, h):
            if h == 0:
                pe.wait_ge(silu_done, count(silu_done, b, 4 * d + 4))
                pe.wait_ge(xd_done, count(xd_done, b, 4 * d + 2))
            nc.tensor.matmul(wp[:, 1 - h, :], wdt[:, d, h * P:(h + 1) * P], xd[:, :],
                             start=True, stop=True).then_inc(dtp_ready, 1)

        def pe_b(pe, b, d, n):
            if n == 0:
                pe.wait_ge(part_done, count(part_done, b, d + 1))
                pe.wait_ge(xd_done, count(xd_done, b, 4 * d + 3))
            pe.wait_ge(dbu_done, count(dbu_done, b, STEPS * d + 2 * (n - 1)))
            nc.tensor.matmul(bp[:, n % 2, :], sel[:, n, :], st[:, d, :], start=True, stop=True).then_inc(b_ready, 1)

        def pe_y(pe, b, d, s):
            if s < 0:
                pe.wait_ge(ud_done, count(ud_done, b, 2 * d + 2))
                pe.wait_ge(yg_done, count(yg_done, b, d))
            else:
                pe.wait_ge(hc_done, count(hc_done, b, STEPS * d + s + 1))
            for h in (range(NH2) if s < 0 else (s % 2,)):
                src = ud[:, h, :] if s < 0 else hc[:, s % NHC, :]
                for c in range(TC):
                    last = nc.tensor.matmul(yp[:, c, h * P:(h + 1) * P], src[:, c * P:(c + 1) * P], ident[:, :],
                                            is_transpose=True, start=(s < 0 and h == 0 and c % 2 == 0),
                                            stop=(s == STEPS - 1), skip_group_check=True)
            last.then_inc(y_added, 1)

        def pe_ygt(pe, b, d, last_unit=False):
            pe.wait_ge(yg_done, count(yg_done, b, d + 1))
            if last_unit:
                pe.wait_ge(ygt_done, count(ygt_done, b, 2))
                pe.wait_ge(res_done, count(res_done, b, 0))
            elif d:
                pe.wait_ge(soft_done, count(soft_done, b + 1, 8))
            else:
                pe.wait_ge(soft_done, count(soft_done, b, 16))
            for h in range(NH2):
                for c in range(TC):
                    last = nc.tensor.transpose(wp[:, h, c * P:(c + 1) * P], yg[:, c, h * P:(h + 1) * P], ident[:, :])
                last.then_inc(ygt_ready, 1)

        def pe_out(pe, b, c):
            pe.wait_ge(ygt_done, count(ygt_done, b, 4))
            for k in range(NDIR * NH2):
                last = nc.tensor.matmul(wp[:, 0, c * P:(c + 1) * P], ygt[:, k // 2, k % 2, c * P:(c + 1) * P],
                                        wout[:, k // 2, k % 2, :], start=(k == 0), stop=(k == 3))
            if c == TC - 1:
                last.then_inc(out_ready, 1)

        def pe_unit(pe, b, d, front=None, tail=None, after=None):
            for s in range(STEPS):
                if s % 2 == 0 and s // 2 + 1 < NS:
                    pe_b(pe, b, d, s // 2 + 1)
                if s == STEPS - 2 and after:
                    pe_b(pe, *after, 0)
                if s == 2:
                    pe_y(pe, b, d, -1)
                if s >= 2:
                    pe_y(pe, b, d, s - 2)
                if tail and s == 3:
                    pe_ygt(pe, *tail)
                if tail and tail[1] == 1 and 6 <= s < 6 + TC:
                    pe_out(pe, tail[0], s - 6)
                if front:
                    if s == 10 and front[1] == 0:
                        pe_xt(pe, front[0])
                    if s in (12, 14):
                        pe_u(pe, *front, (s - 12) // 2)
                    if s in (17, 18):
                        pe_z(pe, *front, s - 17)
                    if s == 20:
                        pe_xd(pe, *front)
                    if s in (22, 23):
                        pe_dt(pe, *front, s - 22)
            pe_y(pe, b, d, STEPS - 2)
            pe_y(pe, b, d, STEPS - 1)

        @block.tensor
        def _(pe):
            for s, per in credited["tensor"]:
                pe.sem_inc(s, per)
            pe.wait_ge(weights_loaded, n_weights)
            pe.wait_ge(taps_folded, NDIR)
            pe.wait_ge(sel_cast, 1)
            pe_xt(pe, 0, first=True)
            pe_u(pe, 0, 0, 0, first=True)
            pe_u(pe, 0, 0, 1, first=True)
            pe_z(pe, 0, 0, 0)
            pe_z(pe, 0, 0, 1)
            pe_xd(pe, 0, 0)
            pe_dt(pe, 0, 0, 0)
            pe_dt(pe, 0, 0, 1)
            pe_b(pe, 0, 0, 0)
            pe_unit(pe, 0, 0, front=(0, 1), after=(0, 1))
            with pe.Fori(0, NB - 1) as b:
                pe_unit(pe, b, 1, front=(b + 1, 0), tail=(b, 0), after=(b + 1, 0))
                pe_unit(pe, b + 1, 0, front=(b + 1, 1), tail=(b, 1), after=(b + 1, 1))
            pe_unit(pe, NB - 1, 1, tail=(NB - 1, 0))
            pe_ygt(pe, NB - 1, 1, last_unit=True)
            for c in range(TC):
                pe_out(pe, NB - 1, c)

        def act_xpad(act, b, r):
            if r == 0:
                act.wait_ge(xt_ready, count(xt_ready, b, 1))
                act.wait_ge(z_ready, count(z_ready, b, 0))
            out = xpad[:, r, NTAP - 1:]
            nc.scalar.activation(out[:, ::-1] if r else out, wp[:, 1, :], ACT.Identity,
                                 bias=ncol[:, 1:2], scale=ncol[:, 0:1]).then_inc(xpad_done, 1)

        def act_silu_u(act, b, d, h):
            act.wait_ge(u_ready, count(u_ready, b, 2 * d + h + 1))
            if h == 0:
                act.wait_ge(xd_ready, count(xd_ready, b, d))
                act.wait_ge(dt_done, count(dt_done, b, 2 * d))
                if d:
                    act.wait_ge(ud_done, count(ud_done, b, 2))
                elif not is_first(b):
                    act.wait_ge(ud_done, count(ud_done, b - 1, 4))
            nc.scalar.activation(u[:, h, :], wp[:, h, :], ACT.Silu, bias=col[:, d, h, 0:1]).then_inc(silu_done, 1)

        def act_silu_z(act, b, d, k):
            act.wait_ge(z_ready, count(z_ready, b, 2 * d + k + 1))
            if k == 0:
                act.wait_ge(yg_done, count(yg_done, b, d - 1))
            nc.scalar.activation(sz[:, d, 2 * k:2 * k + 2, :], wp[:, k, :].rearrange("p (c n) -> p c n", c=2),
                                 ACT.Silu).then_inc(silu_done, 1)

        def act_xd(act, b, d, k):
            if k == 0:
                act.wait_ge(xd_ready, count(xd_ready, b, d + 1))
                act.wait_ge(b_ready, count(b_ready, b, NS * (d - 1)))
                nc.scalar.activation(st[:, d, :], wp[0:SPLIT_ROWS, 0, :], ACT.Copy).then_inc(xd_done, 1)
            elif k == 1:
                act.wait_ge(c_written, count(c_written, b, 16 * d))
                act.wait_ge(dtp_ready, count(dtp_ready, b, 2 * d))
                act.wait_ge(rem_done, count(rem_done, b, d))
                nc.scalar.activation(xd[:, :], wp[:, 0, :], ACT.Copy).then_inc(xd_done, 1)
            elif k == 2:
                act.wait_ge(rem_done, count(rem_done, b, d + 1))
                act.wait_ge(part_done, count(part_done, b, d))
                nc.scalar.activation(st[32:64, d, :], rem[32:64, :], ACT.Copy).then_inc(xd_done, 1)
            else:
                nc.scalar.activation(mid2[64:96, :], rem[64:96, :], ACT.Copy).then_inc(xd_done, 1)

        def act_soft(act, b, d, h, k):
            n = 8 * d + 4 * h
            bias = col[:, d, h, 1:2]
            if k == 0:
                act.wait_ge(dtp_ready, count(dtp_ready, b, 2 * d + h + 1))
                if h == 0:
                    act.wait_ge(dt_done, count(dt_done, b, 2 * d))
                act.wait_ge(soft_done, count(soft_done, b, n))
                nc.scalar.activation(t_abs[:, :], wp[:, 1 - h, :], ACT.Abs, bias=bias).then_inc(soft_done, 1)
            elif k == 1:
                nc.scalar.activation(t_relu[:, h, :], wp[:, 1 - h, :], ACT.Relu, bias=bias).then_inc(soft_done, 1)
            elif k == 2:
                act.wait_ge(soft_done, count(soft_done, b, n + 1))
                nc.scalar.activation(t_exp[:, :], t_abs[:, :], ACT.Exp, scale=-1.0).then_inc(soft_done, 1)
            else:
                act.wait_ge(soft_done, count(soft_done, b, n + 3))
                nc.scalar.activation(t_ln[:, h, :], t_exp[:, :], ACT.Ln, bias=1.0).then_inc(soft_done, 1)

        def act_ud(act, b, d, h):
            if h == 0:
                act.wait_ge(y_added, count(y_added, b, y_count(d - 1, 0)))
            nc.scalar.activation(ud[:, h, :], u[:, h, :], ACT.Copy, scale=col[:, d, h, 2:3]).then_inc(ud_done, 1)

        def act_da(act, b, d, s):
            n, h = s // 2, s % 2
            if s == 0:
                act.wait_ge(dt_done, count(dt_done, b, 2 * d + 1))
            act.wait_ge(scan_done, count(scan_done, b, STEPS * d + s + 1 - NDA))
            nc.scalar.activation(da[:, s % NDA, :], dt[:, d, h, :], ACT.Exp,
                                 scale=a_neg[:, d, h, n:n + 1]).then_inc(da_done, 1)

        def act_ygt(act, b, d, h):
            act.wait_ge(ygt_ready, count(ygt_ready, b, 2 * d + h + 1))
            if h == 0:
                act.wait_ge(out_ready, count(out_ready, b, 0))
            out = ygt[:, d, h, :]
            nc.scalar.activation(out[:, ::-1] if d else out, wp[:, h, :], ACT.Copy).then_inc(ygt_done, 1)

        def act_front(act, b, d, at, first=False):
            if at == 12 and d == 0:
                act_xpad(act, b, 0)
            if at == 13 and d == 0:
                act_xpad(act, b, 1)
            if at == 19:
                act_silu_u(act, b, d, 0)
                act_silu_u(act, b, d, 1)
                act_silu_z(act, b, d, 0)
                act_silu_z(act, b, d, 1)
                act.preload_act_table_set("natural_log_exp_and_others")
            if at in (21, 22, 24, 25):
                act_xd(act, b, d, {21: 0, 22: 1, 24: 2, 25: 3}[at])
            if 26 <= at <= 29:
                for k in (0, 1) if at % 2 == 0 else (2, 3):
                    act_soft(act, b, d, (at - 26) // 2, k)
            if at in (30, 31):
                act_ud(act, b, d, at - 30)

        def act_unit(act, b, d, front=None, tail=None):
            for s in range(STEPS):
                act_da(act, b, d, s)
                if tail and s in (5, 6):
                    act_ygt(act, *tail, s - 5)
                if front:
                    act_front(act, *front, s)

        @block.scalar
        def _(act):
            for s, per in credited["scalar"]:
                act.sem_inc(s, per)
            act.preload_act_table_set("natural_log_exp_and_others")
            act.wait_ge(weights_loaded, n_weights)
            nc.scalar.activation(a_neg[...], a_neg[...], ACT.Exp).then_inc(a_ready, 1)
            act.wait_ge(a_ready, 1)
            nc.scalar.activation(a_neg[...], a_neg[...], ACT.Copy, scale=-1.0).then_inc(a_ready, 1)
            for at in range(12, STEPS):
                act_front(act, 0, 0, at)
            act.wait_ge(a_ready, 2)
            act.wait_ge(sel_cast, 1)
            act_unit(act, 0, 0, front=(0, 1))
            with act.Fori(0, NB - 1) as b:
                act_unit(act, b, 1, front=(b + 1, 0), tail=(b, 0))
                act_unit(act, b + 1, 0, front=(b + 1, 1), tail=(b, 1))
            act_unit(act, NB - 1, 1, tail=(NB - 1, 0))
            act_ygt(act, NB - 1, 1, 0)
            act_ygt(act, NB - 1, 1, 1)

        def dve_ln(dve, b, k):
            base, part = 12 * (k // 3), k % 3
            src, dst = (xin, xln) if k < 3 else (xln, xn)
            if k == 0:
                dve.wait_ge(x_loaded, count(x_loaded, b, 16))
                dve.wait_ge(ln_step, count(ln_step, b, 0))
            if k == 3:
                dve.wait_ge(ln_step, count(ln_step, b, 12))
            if part == 2:
                dve.wait_ge(rstd_done, count(rstd_done, b, 2 * (k // 3) + 2))
                if k == 2:
                    dve.wait_ge(x_kept, count(x_kept, b, 0))
                else:
                    dve.wait_ge(xt_ready, count(xt_ready, b, 0))
            for c in range(TC):
                if part == 0:
                    i = nc.vector.bn_stats(stats[:, 0, c, :], src[:, c, :])
                elif part == 1:
                    i = nc.vector.bn_aggr(mv[:, 0, c, :], stats[:, 0, c, :])
                else:
                    i = nc.vector.tensor_scalar(dst[:, c, :], src[:, c, :], mv[:, 0, c, 0:1], rstd[:, 0, 1, c:c + 1],
                                                ALU.subtract, ALU.mult)
                i.then_inc(ln_step, 1)

        def dve_ln_stats_wait(dve, b, k):
            dve.wait_ge(ln_step, count(ln_step, b, 12 * (k // 3) + 4))

        def dve_part(dve, b, d):
            dve.wait_ge(xd_done, count(xd_done, b, 4 * d + 4))
            nc.vector.tensor_tensor(st[64:96, d, :], rem[64:96, :], mid2[64:96, :],
                                    ALU.subtract).then_inc(part_done, 1)

        def dve_dt(dve, b, d, k):
            if k == 0:
                dve.wait_ge(soft_done, count(soft_done, b, 8 * d + 8))
                dve.wait_ge(da_done, count(da_done, b, STEPS * (d - 1)))
                nc.vector.tensor_tensor(dt[:, d], t_ln[:, :, :], t_relu[:, :, :], ALU.add).then_inc(dt_done, 1)
            else:
                dve.wait_ge(dt_done, count(dt_done, b, 2 * d + 1))
                dve.wait_ge(dbu_done, count(dbu_done, b, STEPS * (d - 1)))
                nc.vector.tensor_tensor(dtu[:, d], dt[:, d], u[:, :, :], ALU.mult).then_inc(dt_done, 1)

        def dve_dbu(dve, b, d, s):
            n, h = s // 2, s % 2
            if s == 0:
                dve.wait_ge(dt_done, count(dt_done, b, 2 * d + 2))
            if h == 0:
                dve.wait_ge(b_ready, count(b_ready, b, NS * d + n + 1))
            dve.wait_ge(scan_done, count(scan_done, b, STEPS * d + s - 1))
            nc.vector.tensor_tensor(dbu[:, s % 2, :], dtu[:, d, h, :], bp[:, n % 2, :],
                                    ALU.mult).then_inc(dbu_done, 1)

        def dve_scan(dve, b, d, s):
            dve.wait_ge(dbu_done, count(dbu_done, b, STEPS * d + s + 1))
            dve.wait_ge(da_done, count(da_done, b, STEPS * d + s + 1))
            dve.wait_ge(hc_done, count(hc_done, b, STEPS * d + s + 1 - NHB))
            nc.vector.tensor_tensor_scan(hb[:, s % NHB, :], da[:, s % NDA, :], dbu[:, s % 2, :], 0.0,
                                         ALU.mult, ALU.add).then_inc(scan_done, 1)

        def dve_yg(dve, b, d):
            dve.wait_ge(y_added, count(y_added, b, y_count(d, STEPS - 1)))
            dve.wait_ge(silu_done, count(silu_done, b, 4 * d + 4))
            dve.wait_ge(ygt_ready, count(ygt_ready, b, 2 * d))
            nc.vector.tensor_tensor(yg[:, :, :], yp[:, :, :], sz[:, d], ALU.mult).then_inc(yg_done, 1)

        def dve_end(dve, b, k):
            if k == 0:
                dve.wait_ge(out_ready, count(out_ready, b, 1))
                dve.wait_ge(x_kept, count(x_kept, b, 32))
                dve.wait_ge(end_step, count(end_step, b, 0))
                nc.vector.tensor_tensor(res[:, :, :], wp[:, 0, :].rearrange("p (c m) -> p c m", c=TC), xres[:, 1],
                                        ALU.add).then_inc(res_done, 1)
            elif k == 4:
                dve.wait_ge(end_step, count(end_step, b, 12))
                nc.vector.tensor_tensor(x1t[:, :, :], x1t[:, :, :], xres[:, 0], ALU.add).then_inc(x1_done, 1)
            else:
                if k == 1:
                    dve.wait_ge(res_done, count(res_done, b, 1))
                if k == 3:
                    dve.wait_ge(end_rstd, count(end_rstd, b, 2))
                    dve.wait_ge(x1_stored, count(x1_stored, b, 0))
                for c in range(TC):
                    if k == 1:
                        i = nc.vector.bn_stats(stats[:, 1, c, :], res[:, c, :])
                    elif k == 2:
                        i = nc.vector.bn_aggr(mv[:, 1, c, :], stats[:, 1, c, :])
                    else:
                        i = nc.vector.tensor_scalar(x1t[:, c, :], res[:, c, :], mv[:, 1, c, 0:1],
                                                    rstd[:, 1, 1, c:c + 1], ALU.subtract, ALU.mult)
                    i.then_inc(end_step, 1)

        def dve_unit(dve, b, d, front=None, tail=None):
            dve_dbu(dve, b, d, 0)
            for s in range(STEPS):
                if front and front[1] == 0 and s in (2, 6):
                    dve_ln_stats_wait(dve, front[0], {2: 1, 6: 4}[s])
                if tail and tail[1] == 1 and s == 13:
                    dve.wait_ge(end_step, count(end_step, tail[0], 4))
                if s + 1 < STEPS:
                    dve_dbu(dve, b, d, s + 1)
                dve_scan(dve, b, d, s)
                if tail and s == 2:
                    dve_yg(dve, *tail)
                if tail and tail[1] == 1 and s in (11, 12, 13, 15, 16):
                    dve_end(dve, tail[0], {11: 0, 12: 1, 13: 2, 15: 3, 16: 4}[s])
                if front and front[1] == 0 and s in (1, 2, 4, 5, 6, 8):
                    dve_ln(dve, front[0], {1: 0, 2: 1, 4: 2, 5: 3, 6: 4, 8: 5}[s])
                if front and s == 27:
                    dve_part(dve, *front)
                if front and s in (29, 30):
                    dve_dt(dve, *front, s - 29)

        @block.vector
        def _(dve):
            for s, per in credited["vector"]:
                dve.sem_inc(s, per)
            for k in range(6):
                if k % 3 == 1:
                    dve_ln_stats_wait(dve, 0, k)
                dve_ln(dve, 0, k)
            dve.wait_ge(weights_loaded, n_weights)
            for d in range(NDIR):
                nc.vector.tensor_tensor(wu[:, d], win_u[:, d:d + 1, :].to_broadcast([P, NTAP, DI]), wu[:, d],
                                        ALU.mult).then_inc(taps_folded, 1)
            dve_part(dve, 0, 0)
            dve_dt(dve, 0, 0, 0)
            dve_dt(dve, 0, 0, 1)
            dve_unit(dve, 0, 0, front=(0, 1))
            with dve.Fori(0, NB - 1) as b:
                dve_unit(dve, b, 1, front=(b + 1, 0), tail=(b, 0))
                dve_unit(dve, b + 1, 0, front=(b + 1, 1), tail=(b, 1))
            dve_unit(dve, NB - 1, 1, tail=(NB - 1, 0))
            dve_yg(dve, NB - 1, 1)
            for k in range(5):
                if k == 2:
                    dve.wait_ge(end_step, count(end_step, NB - 1, 4))
                dve_end(dve, NB - 1, k)

        def pool_rstd(pool, b, k, done, steps, after):
            pool.wait_ge(steps, count(steps, b, after))
            side = 0 if done is rstd_done else 1
            nc.gpsimd.tensor_tensor(rstd[:, side, 0, :], mv[:, side, :, 1], eps[:, :], ALU.add).then_inc(done, 1)
            pool.wait_ge(done, count(done, b, 2 * k + 1))
            nc.gpsimd.tensor_tensor(rstd[:, side, 1, :], rstd[:, side, 0, :], mhalf[:, :], ALU.pow).then_inc(done, 1)

        def pool_rem(pool, b, d):
            pool.wait_ge(xd_done, count(xd_done, b, 4 * d + 2))
            pool.wait_ge(part_done, count(part_done, b, d))
            nc.gpsimd.tensor_tensor(rem[:, :], xd[0:SPLIT_ROWS, :], st[:, d, :],
                                    ALU.subtract).then_inc(rem_done, 1)

        def pool_hc(pool, b, d, s):
            if s == 0:
                pool.wait_ge(c_bcast, count(c_bcast, b, 16 * d + 16))
            pool.wait_ge(scan_done, count(scan_done, b, STEPS * d + s + 1))
            pool.wait_ge(y_added, count(y_added, b, y_count(d, s - NHC)))
            nc.gpsimd.tensor_tensor(hc[:, s % NHC, :], hb[:, s % NHB, :], cb[:, d, s // 2, :],
                                    ALU.mult).then_inc(hc_done, 1)

        def pool_unit(pool, b, d, front=None, tail=None):
            for s in range(STEPS):
                if front and front[1] == 0 and s == 3:
                    pool_rstd(pool, front[0], 0, rstd_done, ln_step, 8)
                if front and front[1] == 0 and s == 7:
                    pool_rstd(pool, front[0], 1, rstd_done, ln_step, 20)
                if tail and tail[1] == 1 and s == 14:
                    pool_rstd(pool, tail[0], 0, end_rstd, end_step, 8)
                if front and s == 23:
                    pool_rem(pool, *front)
                pool_hc(pool, b, d, s)

        @block.gpsimd
        def _(pool):
            for s, per in credited["gpsimd"]:
                pool.sem_inc(s, per)
            nc.gpsimd.memset(mhalf[:, :], -0.5).then_inc(consts_set, 1)
            nc.gpsimd.memset(eps[:, :], EPS).then_inc(consts_set, 1)
            nc.gpsimd.memset(xpad[:, :, 0:NTAP - 1], 0.0).then_inc(consts_set, 1)
            pool.wait_ge(weights_loaded, n_weights)
            nc.gpsimd.tensor_copy(sel[:, :, :], sel32).then_inc(sel_cast, 1)
            pool.wait_ge(consts_set, 3)
            pool_rstd(pool, 0, 0, rstd_done, ln_step, 8)
            pool_rstd(pool, 0, 1, rstd_done, ln_step, 20)
            pool_rem(pool, 0, 0)
            pool_unit(pool, 0, 0, front=(0, 1))
            with pool.Fori(0, NB - 1) as b:
                pool_unit(pool, b, 1, front=(b + 1, 0), tail=(b, 0))
                pool_unit(pool, b + 1, 0, front=(b + 1, 1), tail=(b, 1))
            pool_unit(pool, NB - 1, 1, tail=(NB - 1, 0))
            pool_rstd(pool, NB - 1, 0, end_rstd, end_step, 8)


NHEAD, NKV, HD = 16, 4, 8
GH = 8
NE, FF = 8, 256
NF = FF // P
PART_ROWS = 9 * HD
QK_ROWS = PART_ROWS + 3
SCALE = HD ** -0.5
PAIRS = NHEAD // 2
PAIR_TILES = (((0, 0, 0),), ((0, 1, 0), (0, 3, 384)), ((0, 2, 0), (1, 2, 256)), ((1, 0, 0),), ((1, 1, 0), (1, 3, 384)))
NPT = len(PAIR_TILES)
ST_TILES = PAIRS * NPT
MAX_TILES = [(c, h, n) for c, n in ((0, 4), (1, 2), (2, 1), (3, 1)) for h in range(0, NHEAD, n)]
MT = len(MAX_TILES)


def ffn_phase(nc, sems, x1, out, qscr, kscr, mscr, w):
    with ExitStack() as ctx:
        def sb(name, shape, dt=F32):
            return ctx.enter_context(nc.sbuf_tensor(name, shape, dt))

        def pb(name, shape):
            return ctx.enter_context(nc.psum_tensor(name, shape, F32))

        count = Counts()
        credited = {e: [] for e in ("sync", "tensor", "scalar", "vector", "gpsimd")}

        def sig(name, per, producer=None):
            s = sems.enter_context(nc.semaphore(name))
            count.add(s, per, producer is not None)
            if producer is not None:
                credited[producer].append((s, per))
            return s

        ident = sb("ident2", [P, P])
        identb = sb("identb", [P, P], BF16)
        mask32 = sb("mask32", [P, 2, P])
        mask = sb("mask", [P, 2, P], BF16)
        trig = sb("trig", [P, 2, SEQ])
        wq = sb("wq", [P, 2, P])
        wk = sb("wk", [P, 2 * NKV * HD])
        wv = sb("wv", [P, NKV * HD])
        wo = sb("wo", [P, DM])
        gate = sb("gate", [P, NE])
        w13 = sb("w13", [P, NE, 2 * FF])
        w2 = sb("w2", [P, NE, NF, DM])
        lnw = sb("lnw", [P, 2])
        tri = sb("tri", [P, NE, NE])
        sel32 = sb("sel32e", [SPLIT_ROWS, NE, P])
        sel = sb("sel_e", [SPLIT_ROWS, NE, P], BF16)
        mhalf = sb("mhalf2", [P, TC])
        eps = sb("eps2", [P, TC])
        xa = sb("xa", [P, TC, DM])
        h0 = sb("h0", [P, TC, DM])
        hres = sb("hres", [P, TC, DM])
        hn = sb("hn", [P, TC, DM])
        stats = sb("stats2", [P, 3, TC, 6])
        mv = sb("mv2", [P, 3, TC, 2])
        rt = sb("rt", [P, 3, 4, TC])
        ht = sb("ht", [P, SEQ])
        rot = sb("rot", [P, 2, SEQ])
        qf = sb("qf", [P, SEQ])
        rotk = sb("rotk", [NKV * HD, 2, SEQ])
        kf = sb("kf", [NKV * HD, SEQ])
        qp = sb("qp", [P, 3, SEQ], BF16)
        kp = sb("kp", [NKV * HD, 3, SEQ], BF16)
        vst = sb("vst", [P, TC, NKV, HD])
        vpad = sb("vpad", [P, TC, NHEAD, P])
        q9 = sb("q9", [QK_ROWS, NHEAD, SEQ], BF16)
        k9 = sb("k9", [QK_ROWS, NKV, SEQ], BF16)
        mx = sb("mx", [P, TC, NHEAD])
        nm = sb("nm", [NHEAD, 3, SEQ], BF16)
        nmr = sb("nmr", [NHEAD, SEQ])
        NPR = 4
        pt = sb("pt", [P, NPR, SEQ])
        rec = sb("rec", [64, SEQ])
        ot = sb("ot", [P, SEQ])
        x2 = sb("x2", [P, TC, DM])
        h2n = sb("h2n", [P, TC, DM])
        h2t = sb("h2t", [P, SEQ])
        lg = sb("lg", [P, TC, NE])
        lmax = sb("lmax", [P, TC])
        ex = sb("ex", [P, TC, NE])
        gtm = sb("gtm", [P, TC, NE, NE])
        eqm = sb("eqm", [P, TC, NE, NE])
        rank = sb("rank", [P, TC, NE])
        wsum = sb("wsum", [P, 2, TC])
        wrep = sb("wrep", [P, TC, 3, 32])
        wst = sb("wst", [SPLIT_ROWS, SEQ], BF16)
        wrem = sb("wrem", [SPLIT_ROWS, SEQ])
        wmid = sb("wmid", [SPLIT_ROWS, SEQ], BF16)
        h2e = sb("h2e", [P, 2, SEQ])
        th = sb("th", [P, 2, SEQ])
        ga = sb("ga", [P, 2, SEQ])
        g = sb("g", [P, 2, SEQ])
        ots = sb("ots", [P, SEQ])
        ye = sb("ye", [P, TC, DM])
        xr = sb("xr", [P, TC, DM])
        yo = sb("yo", [P, TC, DM])
        sp_ = pb("scores", [P, 2, SEQ])
        og = pb("og", [P, SEQ])
        pa = pb("pa", [P, SEQ])
        pbk = pb("pbk", [P, SEQ])
        po = pb("po", [P, SEQ])
        m0 = pb("m0", [P, SEQ])
        m1 = pb("m1", [P, SEQ])

        loaded = sems.enter_context(nc.semaphore("weights2_loaded"))
        consts = sems.enter_context(nc.semaphore("consts2_set"))
        casts = sems.enter_context(nc.semaphore("casts2_done"))

        xa_loaded = sig("xa_loaded", 16)
        qk_written = sig("qk_written", 96, "sync")
        qk_loaded = sig("qk_loaded", 64, "sync")
        m_written = sig("m_written", 16, "sync")
        m_loaded = sig("m_loaded", 16, "sync")
        xr_loaded = sig("xr_loaded", 16)
        out_stored = sig("out_stored", 16, "sync")

        ht_ready = sig("ht_ready", 1, "tensor")
        proj_ready = sig("proj_ready", 4, "tensor")
        max_ready = sig("max_ready", MT, "tensor")
        nm_ready = sig("nm_ready", 1)
        st_ready = sig("st_ready", ST_TILES, "tensor")
        pv_done = sig("pv_done", ST_TILES, "tensor")
        wo_ready = sig("wo_ready", 1, "tensor")
        x2t_ready = sig("x2t_ready", 1, "tensor")
        gate_ready = sig("gate_ready", 1)
        wt_ready = sig("wt_ready", 1, "tensor")
        wbc_ready = sig("wbc_ready", NE, "tensor")
        a_ready = sig("a_ready2", NE * NF, "tensor")
        b_ready = sig("b_ready2", NE * NF, "tensor")
        down_done = sig("down_done", NE * NF, "tensor")
        ot_ready = sig("ot_ready", 1, "tensor")

        ht_done = sig("ht_done", 1)
        part_act = sig("part_act", 4, "scalar")
        v_done = sig("v_done", 1, "scalar")
        exp_done = sig("exp_done", ST_TILES, "scalar")
        nm_act = sig("nm_act", 2, "scalar")
        th_done = sig("th_done", NE * NF, "scalar")
        h2t_done = sig("h2t_done", 1, "scalar")
        ex_done = sig("ex_done", 1)
        wpart_act = sig("wpart_act", 3, "scalar")
        ots_done = sig("ots_done", 1, "scalar")

        in_step = sig("in_step", 24, "vector")
        rope_mul = sig("rope_mul", 4, "vector")
        max_done = sig("max_done", MT, "vector")
        nm_rem = sig("nm_rem", 1, "vector")
        og_step = sig("og_step", 4, "vector")
        x2_done = sig("x2_done", 1, "vector")
        post_step = sig("post_step", 12, "vector")
        gate_step = sig("gate_step", 12, "vector")
        wpart_dve = sig("wpart_dve", 2, "vector")
        h2e_done = sig("h2e_done", NE, "vector")
        ga_done = sig("ga_done", NE * NF, "vector")
        g_done = sig("g_done", NE * NF, "vector")
        ye_done = sig("ye_done", 1, "vector")
        end_step = sig("end_step2", 12, "vector")
        out_done = sig("out_done", 1, "vector")

        in_rstd = sig("in_rstd", 6, "gpsimd")
        post_rstd = sig("post_rstd", 4, "gpsimd")
        end_rstd = sig("end_rstd2", 2, "gpsimd")
        rope_add = sig("rope_add", 2, "gpsimd")
        part_pool = sig("part_pool", 4, "gpsimd")
        kept = sig("kept", 1, "scalar")
        vpad_done = sig("vpad_done", 8, "scalar")
        nm_pool = sig("nm_pool", 1, "gpsimd")

        block = ctx.enter_context(nc.Block())
        weights = ((ident, "ident"), (mask32, "mask"), (trig, "trig"), (wq, "wq"), (wk, "wk"), (wv, "wv"), (wo, "wo"),
                   (gate, "gate"), (lnw, "lnw"), (tri, "tri"), (sel32, "sel_e"), (w13, "w13"), (w2, "w2"))
        n_weights = 16 * len(weights)

        def rows(t, b):
            return t[bass.ds(b, 1)].rearrange("a (c p) m -> p a c m", p=P)

        def flat(t):
            return t[:, :, :].rearrange("p (a c) m -> p a c m", a=1)

        def sp_xa(sp, b, first=False):
            if not first:
                sp.wait_ge(in_step, count(in_step, b, -12))
            sp.dma_start(flat(xa), rows(x1, b)).then_inc(xa_loaded, 16)

        def sp_xr(sp, b):
            sp.wait_ge(out_done, count(out_done, b, 0))
            sp.dma_start(flat(xr), rows(x1, b)).then_inc(xr_loaded, 16)

        def sp_parts_out(sp, b):
            sp.wait_ge(part_act, count(part_act, b, 4))
            sp.wait_ge(part_pool, count(part_pool, b, 4))
            sp.wait_ge(qk_loaded, count(qk_loaded, b, 0))
            for a in range(3):
                sp.dma_start(qscr[a].rearrange("d h s -> h d s"), qp[:, a, :]).then_inc(qk_written, 16)
                sp.dma_start(kscr[a].rearrange("d h s -> h d s"), kp[:, a, :]).then_inc(qk_written, 16)

        def sp_parts_in(sp, b):
            sp.wait_ge(qk_written, count(qk_written, b, 96))
            sp.wait_ge(st_ready, count(st_ready, b, 0))
            for a in range(3):
                sp.dma_start(q9[a * 3 * HD:(a + 1) * 3 * HD].rearrange("r h s -> r (h s)"),
                             qscr[a:a + 1].rearrange("a d h s -> a d (h s)").to_broadcast([3, HD, NHEAD * SEQ])
                             ).then_inc(qk_loaded, 16)
            sp.dma_start(k9[0:PART_ROWS].rearrange("r h s -> r (h s)"),
                         kscr.rearrange("b d h s -> (b d) (h s)").unsqueeze(0).to_broadcast([3, 3 * HD, NKV * SEQ])
                         ).then_inc(qk_loaded, 16)

        def sp_max(sp, b):
            parts_act, parts_pool, before = (count.in_register(sp, nm_act, b, 2), count.in_register(sp, nm_pool, b, 1),
                                             count.in_register(sp, m_loaded, b, 0))
            sp.wait_ge(nm_act, parts_act)
            sp.wait_ge(nm_pool, parts_pool)
            sp.wait_ge(m_loaded, before)
            sp.dma_start(mscr.rearrange("a h s -> h a s"), nm[:, :, :]).then_inc(m_written, 16)
            sp.wait_ge(m_written, count(m_written, b, 16))
            sp.wait_ge(st_ready, count(st_ready, b, 0))
            sp.dma_start(q9[PART_ROWS:QK_ROWS].rearrange("r h s -> r (h s)"),
                         mscr.rearrange("a h s -> a (h s)")).then_inc(m_loaded, 16)

        def sp_out(sp, b):
            sp.wait_ge(out_done, count(out_done, b, 1))
            sp.dma_start(rows(out, b), flat(yo)).then_inc(out_stored, 16)

        @block.sync
        def _(sp):
            for s, per in credited["sync"]:
                sp.sem_inc(s, per)
            sp_xa(sp, 0, first=True)
            for dst, name in weights:
                sp.dma_start(dst[...], w[name]).then_inc(loaded, 16)
            sp_parts_out(sp, 0)
            sp.wait_ge(consts, 6)
            sp_parts_in(sp, 0)
            sp_max(sp, 0)
            sp_xa(sp, 1)
            sp_parts_out(sp, 1)
            sp_parts_in(sp, 1)
            sp_max(sp, 1)
            with sp.Fori(1, NB - 1) as b:
                sp_xa(sp, b + 1)
                sp_xr(sp, b - 1)
                sp_parts_out(sp, b + 1)
                sp_parts_in(sp, b + 1)
                sp_out(sp, b - 1)
                sp_max(sp, b + 1)
            sp_xr(sp, NB - 2)
            sp_out(sp, NB - 2)
            sp_xr(sp, NB - 1)
            sp_out(sp, NB - 1)
            sp.wait_ge(out_stored, count(out_stored, NB - 1, 16))

        def pe_ht(pe, b):
            pe.wait_ge(in_step, count(in_step, b, 24))
            if not is_first(b):
                pe.wait_ge(wpart_act, count(wpart_act, b - 1, 0))
                pe.wait_ge(wpart_dve, count(wpart_dve, b - 1, 0))
            for c in range(TC):
                last = nc.tensor.transpose(m0[:, c * P:(c + 1) * P], hn[:, c, :], ident[:, :])
            last.then_inc(ht_ready, 1)

        def pe_proj(pe, b, k):
            if k == 0:
                pe.wait_ge(ht_done, count(ht_done, b, 1))
                nc.tensor.matmul(m0[:, :], wq[:, 0, :], ht[:, :], start=True, stop=True).then_inc(proj_ready, 1)
            elif k == 1:
                pe.wait_ge(rope_mul, count(rope_mul, b, 1))
                nc.tensor.matmul(m0[:, :], wq[:, 1, :], ht[:, :], start=True, stop=True).then_inc(proj_ready, 1)
            elif k == 2:
                pe.wait_ge(rope_mul, count(rope_mul, b, 2))
                nc.tensor.matmul(m0[0:64, :], wk[:, :], ht[:, :], start=True, stop=True).then_inc(proj_ready, 1)
            else:
                pe.wait_ge(rope_mul, count(rope_mul, b, 4))
                for c in range(TC):
                    last = nc.tensor.matmul(m0[:, c * 32:(c + 1) * 32], ht[:, c * P:(c + 1) * P], wv[:, :],
                                            start=True, stop=True)
                last.then_inc(proj_ready, 1)

        def pe_max(pe, b, t):
            c, h0_, n = MAX_TILES[t]
            if t == 0:
                pe.wait_ge(qk_loaded, count(qk_loaded, b, 64))
                pe.wait_ge(exp_done, count(exp_done, b, 0))
            if t >= 2:
                pe.wait_ge(max_done, count(max_done, b, t - 1))
            width = (c + 1) * P
            for i in range(n):
                at = i * width
                nc.tensor.matmul(sp_[:, t % 2, at + c * P:at + width], identb[:, :], mask[:, 0, :],
                                 start=(i == 0), stop=False, skip_group_check=True)
                last = nc.tensor.matmul(sp_[:, t % 2, at:at + width],
                                        q9[0:PART_ROWS, h0_ + i, c * P:(c + 1) * P],
                                        k9[0:PART_ROWS, (h0_ + i) // 4, 0:width],
                                        start=False, stop=True, skip_group_check=True)
            last.then_inc(max_ready, 1)

        def pe_nm(pe, b):
            pe.wait_ge(max_done, count(max_done, b, MT))
            if not is_first(b):
                pe.wait_ge(h2e_done, count(h2e_done, b - 1, 0))
                pe.wait_ge(ye_done, count(ye_done, b - 1, 0))
            for c in range(TC):
                last = nc.tensor.transpose(m1[0:NHEAD, c * P:(c + 1) * P], mx[:, c, :], ident[:, :])
            last.then_inc(nm_ready, 1)

        def pieces(t):
            i, j = t // NPT, t % NPT
            return [(2 * i + hh, kc, at) for hh, kc, at in PAIR_TILES[j]]

        def pe_st(pe, b, t):
            if t == 0:
                pe.wait_ge(m_loaded, count(m_loaded, b, 16))
                pe.wait_ge(max_done, count(max_done, b, MT))
            if t >= 2:
                pe.wait_ge(exp_done, count(exp_done, b, t - 1))
            for i, (h, kc, at) in enumerate(pieces(t)):
                nc.tensor.matmul(sp_[:, t % 2, at:at + P], identb[:, :], mask[:, 1, :],
                                 start=(i == 0), stop=False, skip_group_check=True)
                last = nc.tensor.matmul(sp_[:, t % 2, at:at + SEQ - kc * P],
                                        k9[:, h // 4, kc * P:(kc + 1) * P], q9[:, h, kc * P:],
                                        start=False, stop=True, skip_group_check=True)
            last.then_inc(st_ready, 1)

        def pe_pv(pe, b, t):
            pe.wait_ge(exp_done, count(exp_done, b, t + 1))
            if t == 0:
                pe.wait_ge(vpad_done, count(vpad_done, b, 8))
                pe.wait_ge(og_step, count(og_step, b, 0))
            if t == ST_TILES // 2:
                pe.wait_ge(og_step, count(og_step, b, 2))
            ps = pieces(t)
            for i, (h, kc, at) in enumerate(ps):
                first = t % (ST_TILES // 2) == 0
                final = t % (ST_TILES // 2) == ST_TILES // 2 - 1 and i == len(ps) - 1
                last = nc.tensor.matmul(og[:, kc * P:], vpad[:, kc, h, :], pt[:, t % NPR, at:at + SEQ - kc * P],
                                        start=first, stop=final, skip_group_check=True)
            last.then_inc(pv_done, 1)

        def pe_wo(pe, b, final=False):
            pe.wait_ge(og_step, count(og_step, b, 4))
            if final:
                pe.wait_ge(wpart_act, count(wpart_act, b, 0))
                pe.wait_ge(wpart_dve, count(wpart_dve, b, 0))
            else:
                pe.wait_ge(v_done, count(v_done, b + 1, 1))
            for c in range(TC):
                last = nc.tensor.matmul(m0[:, c * P:(c + 1) * P], ot[:, c * P:(c + 1) * P], wo[:, :],
                                        start=True, stop=True)
            last.then_inc(wo_ready, 1)

        def pe_x2t(pe, b):
            pe.wait_ge(post_step, count(post_step, b, 12))
            pe.wait_ge(x2_done, count(x2_done, b, 1))
            for c in range(TC):
                last = nc.tensor.transpose(m0[:, c * P:(c + 1) * P], h2n[:, c, :], ident[:, :])
            last.then_inc(x2t_ready, 1)

        def pe_gate(pe, b):
            pe.wait_ge(h2t_done, count(h2t_done, b, 1))
            for c in range(TC):
                last = nc.tensor.matmul(m0[:, c * NE:(c + 1) * NE], h2t[:, c * P:(c + 1) * P], gate[:, :],
                                        start=True, stop=True)
            last.then_inc(gate_ready, 1)

        def pe_wt(pe, b):
            pe.wait_ge(gate_step, count(gate_step, b, 12))
            for c in range(TC):
                last = nc.tensor.transpose(m0[0:SPLIT_ROWS, c * P:(c + 1) * P],
                                           wrep[:, c, :, :].rearrange("p a b -> p (a b)"), ident[:, :])
            last.then_inc(wt_ready, 1)

        def pe_wbc(pe, b, e, final=False):
            if e == 0:
                pe.wait_ge(wpart_act, count(wpart_act, b, 3))
                pe.wait_ge(wpart_dve, count(wpart_dve, b, 2))
                if final:
                    pe.wait_ge(ye_done, count(ye_done, b, 0))
                else:
                    pe.wait_ge(nm_rem, count(nm_rem, b + 1, 1))
                    pe.wait_ge(nm_act, count(nm_act, b + 1, 1))
            else:
                pe.wait_ge(h2e_done, count(h2e_done, b, e))
            nc.tensor.matmul(m1[:, :], sel[:, e, :], wst[:, :], start=True, stop=True).then_inc(wbc_ready, 1)

        def pe_a(pe, b, e, f):
            n = NF * e + f
            pe.wait_ge(ga_done, count(ga_done, b, n))
            if n == 0:
                pe.wait_ge(h2t_done, count(h2t_done, b, 1))
            nc.tensor.matmul(pa[:, :], w13[:, e, f * P:(f + 1) * P], h2t[:, :],
                             start=True, stop=True).then_inc(a_ready, 1)

        def pe_bm(pe, b, e, f):
            pe.wait_ge(g_done, count(g_done, b, NF * e + f))
            pe.wait_ge(h2e_done, count(h2e_done, b, e + 1))
            nc.tensor.matmul(pbk[:, :], w13[:, e, FF + f * P:FF + (f + 1) * P], h2e[:, e % 2, :],
                             start=True, stop=True).then_inc(b_ready, 1)

        def pe_down(pe, b, n):
            pe.wait_ge(g_done, count(g_done, b, n + 1))
            if n == 0:
                pe.wait_ge(ots_done, count(ots_done, b, 0))
            nc.tensor.matmul(po[:, :], w2[:, n // NF, n % NF, :], g[:, n % 2, :], start=(n == 0),
                             stop=(n == NE * NF - 1), skip_group_check=True).then_inc(down_done, 1)

        def pe_ot(pe, b):
            pe.wait_ge(ots_done, count(ots_done, b, 1))
            pe.wait_ge(h2e_done, count(h2e_done, b, NE))
            for c in range(TC):
                last = nc.tensor.transpose(m1[:, c * P:(c + 1) * P], ots[:, c * P:(c + 1) * P], ident[:, :])
            last.then_inc(ot_ready, 1)

        def pe_main(pe, att=None, moe=None, front=None):
            if moe is not None:
                pe_wbc(pe, moe, 0, final=att is None)
            for t in range(ST_TILES):
                i, j = t // NPT, t % NPT
                if att is not None:
                    pe_st(pe, att, t)
                    if t >= 2:
                        pe_pv(pe, att, t - 2)
                if moe is not None:
                    if j == 0:
                        pe_a(pe, moe, i, 0)
                    if j == 1:
                        pe_bm(pe, moe, i, 0)
                        if i > 0:
                            pe_down(pe, moe, 2 * i - 1)
                    if j == 2:
                        if i + 1 < NE:
                            pe_wbc(pe, moe, i + 1)
                        pe_a(pe, moe, i, 1)
                    if j == 3:
                        pe_bm(pe, moe, i, 1)
                    if j == 4:
                        pe_down(pe, moe, 2 * i)
                if front is not None:
                    if t == 14:
                        pe_ht(pe, front)
                    if t in (18, 21, 24, 27):
                        pe_proj(pe, front, (t - 18) // 3)
            if att is not None:
                pe_pv(pe, att, ST_TILES - 2)
                pe_pv(pe, att, ST_TILES - 1)
            if moe is not None:
                pe_down(pe, moe, NE * NF - 1)

        def pe_turn(pe, post=None, end=None, top=None):
            if post is not None:
                pe_wo(pe, post, final=top is None)
            if end is not None:
                pe_ot(pe, end)
            for t in range(MT):
                if top is not None:
                    pe_max(pe, top, t)
                if post is not None:
                    if t == 12:
                        pe_x2t(pe, post)
                    if t == 16:
                        pe_gate(pe, post)
                    if t == 34:
                        pe_wt(pe, post)
            if top is not None:
                pe_nm(pe, top)

        @block.tensor
        def _(pe):
            for s, per in credited["tensor"]:
                pe.sem_inc(s, per)
            pe.wait_ge(loaded, n_weights)
            pe.wait_ge(casts, 3)
            pe_ht(pe, 0)
            for k in range(4):
                pe_proj(pe, 0, k)
            pe_turn(pe, top=0)
            pe_main(pe, att=0, front=1)
            pe_turn(pe, post=0, top=1)
            with pe.Fori(1, NB - 1) as b:
                pe_main(pe, att=b, moe=b - 1, front=b + 1)
                pe_turn(pe, post=b, end=b - 1, top=b + 1)
            pe_main(pe, att=NB - 1, moe=NB - 2)
            pe_turn(pe, post=NB - 1, end=NB - 2)
            pe_main(pe, moe=NB - 1)
            pe_turn(pe, end=NB - 1)

        def vpad_diag(c, gi):
            a = vpad[:, c, gi * GH:(gi + 1) * GH, 0:HD].rearrange("p (k r) d -> p k r d", k=2)
            step = P + HD
            ap = [list(x) for x in a.ap]
            ap[1][0], ap[2][0] = 4 * step, step
            return bass.AP(tensor=a.tensor, offset=a.offset, ap=ap)

        def act_keep(act, b):
            act.wait_ge(in_step, count(in_step, b, 24))
            act.wait_ge(x2_done, count(x2_done, b, 0))
            nc.scalar.activation(hres[:, :, :], h0[:, :, :], ACT.Copy).then_inc(kept, 1)

        def act_vpad(act, b):
            act.wait_ge(v_done, count(v_done, b, 1))
            act.wait_ge(pv_done, count(pv_done, b, 0))
            for c in range(TC):
                for gi in range(2):
                    nc.scalar.activation(vpad_diag(c, gi),
                                         vst[:, c, 2 * gi:2 * gi + 2, :].unsqueeze(2).to_broadcast([P, 2, 4, HD]),
                                         ACT.Copy).then_inc(vpad_done, 1)

        def act_ht(act, b):
            act.wait_ge(ht_ready, count(ht_ready, b, 1))
            act.wait_ge(proj_ready, count(proj_ready, b, 0))
            nc.scalar.activation(ht[:, :], m0[:, :], ACT.Copy, scale=lnw[:, 0:1]).then_inc(ht_done, 1)

        def act_v(act, b):
            act.wait_ge(proj_ready, count(proj_ready, b, 4))
            act.wait_ge(vpad_done, count(vpad_done, b, 0))
            nc.scalar.activation(vst[:, :, :, :].rearrange("p c h d -> p (c h d)"), m0[:, 0:TC * NKV * HD],
                                 ACT.Copy).then_inc(v_done, 1)

        def act_part(act, b, k):
            src, first, rem = ((qf, qp, rot), (kf, kp, rotk))[k // 2]
            if k % 2 == 0:
                act.wait_ge(rope_add, count(rope_add, b, k // 2 + 1))
                act.wait_ge(qk_written, count(qk_written, b, 0))
                act.wait_ge(part_pool, count(part_pool, b, 0))
                nc.scalar.activation(first[:, 0, :], src[:, :], ACT.Copy).then_inc(part_act, 1)
            else:
                act.wait_ge(part_pool, count(part_pool, b, 2 * (k // 2) + 1))
                nc.scalar.activation(first[:, 1, :], rem[:, 0, :], ACT.Copy).then_inc(part_act, 1)

        def act_exp(act, b, t):
            act.wait_ge(st_ready, count(st_ready, b, t + 1))
            act.wait_ge(pv_done, count(pv_done, b, t + 1 - NPR))
            width = sum(SEQ - kc * P for _, kc, _ in pieces(t))
            nc.scalar.activation(pt[:, t % NPR, 0:width], sp_[:, t % 2, 0:width], ACT.Exp,
                                 scale=SCALE).then_inc(exp_done, 1)

        def act_nm(act, b, k):
            if k == 0:
                act.wait_ge(nm_ready, count(nm_ready, b, 1))
                act.wait_ge(m_written, count(m_written, b, 0))
                act.wait_ge(nm_pool, count(nm_pool, b, 0))
                nc.scalar.activation(nm[:, 0, :], m1[0:NHEAD, :], ACT.Copy, scale=-1.0).then_inc(nm_act, 1)
            else:
                act.wait_ge(nm_rem, count(nm_rem, b, 1))
                nc.scalar.activation(nm[:, 1, :], nmr[:, :], ACT.Copy).then_inc(nm_act, 1)

        def act_th(act, b, n):
            act.wait_ge(a_ready, count(a_ready, b, n + 1))
            act.wait_ge(ga_done, count(ga_done, b, n - 1))
            nc.scalar.activation(th[:, n % 2, :], pa[:, :], ACT.Tanh, scale=0.5).then_inc(th_done, 1)

        def act_h2t(act, b):
            act.wait_ge(x2t_ready, count(x2t_ready, b, 1))
            act.wait_ge(a_ready, count(a_ready, b, 0))
            act.wait_ge(h2e_done, count(h2e_done, b, 0))
            nc.scalar.activation(h2t[:, :], m0[:, :], ACT.Copy, scale=lnw[:, 1:2]).then_inc(h2t_done, 1)

        def act_ex(act, b):
            act.wait_ge(gate_step, count(gate_step, b, 3))
            nc.scalar.activation(ex[:, :, :], ex[:, :, :], ACT.Exp).then_inc(ex_done, 1)

        def act_wpart(act, b, k):
            if k == 0:
                act.wait_ge(wt_ready, count(wt_ready, b, 1))
                act.wait_ge(wbc_ready, count(wbc_ready, b, 0))
                nc.scalar.activation(wst[:, :], m0[0:SPLIT_ROWS, :], ACT.Copy).then_inc(wpart_act, 1)
            elif k == 1:
                act.wait_ge(wpart_dve, count(wpart_dve, b, 1))
                nc.scalar.activation(wst[32:64, :], wrem[32:64, :], ACT.Copy).then_inc(wpart_act, 1)
            else:
                nc.scalar.activation(wmid[64:96, :], wrem[64:96, :], ACT.Copy).then_inc(wpart_act, 1)

        def act_ots(act, b):
            act.wait_ge(down_done, count(down_done, b, NE * NF))
            act.wait_ge(ot_ready, count(ot_ready, b, 0))
            nc.scalar.activation(ots[:, :], po[:, :], ACT.Copy).then_inc(ots_done, 1)

        def act_main(act, att=None, moe=None, front=None):
            for t in range(ST_TILES):
                i, j = t // NPT, t % NPT
                if att is not None:
                    act_exp(act, att, t)
                if moe is not None and j in (1, 3):
                    act_th(act, moe, 2 * i + j // 2)
                if front is not None:
                    if t == 15:
                        act_ht(act, front)
                    if t in (26, 28, 30, 32):
                        act_part(act, front, (0, 2, 1, 3)[(t - 26) // 2])
                    if t == 29:
                        act_v(act, front)

        def act_turn(act, post=None, end=None, top=None):
            if end is not None:
                act_ots(act, end)
            if post is not None:
                act_h2t(act, post)
            if top is not None:
                act_keep(act, top)
                act_vpad(act, top)
            if post is not None:
                act_ex(act, post)
                for k in range(3):
                    act_wpart(act, post, k)
            if top is not None:
                act_nm(act, top, 0)
                act_nm(act, top, 1)

        @block.scalar
        def _(act):
            for s, per in credited["scalar"]:
                act.sem_inc(s, per)
            act.wait_ge(loaded, n_weights)
            act.wait_ge(consts, 6)
            act_ht(act, 0)
            for k in (0, 2, 1, 3):
                act_part(act, 0, k)
            act_v(act, 0)
            act_turn(act, top=0)
            act_main(act, att=0, front=1)
            act_turn(act, post=0, top=1)
            with act.Fori(1, NB - 1) as b:
                act_main(act, att=b, moe=b - 1, front=b + 1)
                act_turn(act, post=b, end=b - 1, top=b + 1)
            act_main(act, att=NB - 1, moe=NB - 2)
            act_turn(act, post=NB - 1, end=NB - 2)
            act_main(act, moe=NB - 1)
            act_turn(act, end=NB - 1)

        def dve_stats(side, src, sem):
            for c in range(TC):
                nc.vector.bn_stats(stats[:, side, c, :], src[:, c, :]).then_inc(sem, 1)

        def dve_aggr(side, sem):
            for c in range(TC):
                nc.vector.bn_aggr(mv[:, side, c, :], stats[:, side, c, :]).then_inc(sem, 1)

        def dve_norm(side, dst, src, sem, rms):
            for c in range(TC):
                r = rt[:, side, 3, c:c + 1]
                if rms:
                    nc.vector.tensor_scalar(dst[:, c, :], src[:, c, :], r, None, ALU.mult).then_inc(sem, 1)
                else:
                    nc.vector.tensor_scalar(dst[:, c, :], src[:, c, :], mv[:, side, c, 0:1], r,
                                            ALU.subtract, ALU.mult).then_inc(sem, 1)

        def dve_in(dve, b, k):
            s = in_step
            if k == 0:
                dve.wait_ge(xa_loaded, count(xa_loaded, b, 16))
                dve.wait_ge(s, count(s, b, 0))
                dve_stats(0, xa, s)
            elif k == 1:
                dve_aggr(0, s)
            elif k == 2:
                dve.wait_ge(in_rstd, count(in_rstd, b, 2))
                dve.wait_ge(kept, count(kept, b, 0))
                dve_norm(0, h0, xa, s, False)
            elif k == 3:
                dve.wait_ge(s, count(s, b, 12))
                dve_stats(0, h0, s)
            elif k == 4:
                dve_aggr(0, s)
            else:
                dve.wait_ge(in_rstd, count(in_rstd, b, 6))
                dve.wait_ge(ht_ready, count(ht_ready, b, 0))
                dve_norm(0, hn, h0, s, True)

        def dve_rope(dve, b, k):
            dve.wait_ge(proj_ready, count(proj_ready, b, (1, 2, 3, 3)[k]))
            if k == 0:
                dve.wait_ge(rope_add, count(rope_add, b, 0))
                dve.wait_ge(part_act, count(part_act, b, 0))
                dve.wait_ge(part_pool, count(part_pool, b, 0))
            if k < 2:
                nc.vector.tensor_tensor(rot[:, k, :], m0[:, :], trig[:, k, :], ALU.mult).then_inc(rope_mul, 1)
            else:
                at = 32 * (k - 2)
                nc.vector.tensor_tensor(rotk[:, k - 2, :], m0[at:at + 32, :], trig[0:32, k - 2, :],
                                        ALU.mult).then_inc(rope_mul, 1)

        def dve_max(dve, b, t):
            c, h, n = MAX_TILES[t]
            dve.wait_ge(max_ready, count(max_ready, b, t + 1))
            if t == 0:
                dve.wait_ge(nm_act, count(nm_act, b, 0))
            nc.vector.reduce_max(mx[:, c, h:h + n],
                                 sp_[:, t % 2, 0:n * (c + 1) * P].rearrange("p (n k) -> p n k", n=n),
                                 mybir.AxisListType.X).then_inc(max_done, 1)

        def dve_nm(dve, b):
            dve.wait_ge(nm_act, count(nm_act, b, 1))
            dve.wait_ge(nm_pool, count(nm_pool, b, 0))
            nc.vector.scalar_tensor_tensor(nmr[:, :], m1[0:NHEAD, :], -1.0, nm[:, 0, :],
                                           ALU.mult, ALU.subtract).then_inc(nm_rem, 1)

        def dve_og(dve, b, k):
            dve.wait_ge(pv_done, count(pv_done, b, (k + 1) * ST_TILES // 2))
            dve.wait_ge(og_step, count(og_step, b, 2 * k))
            nc.vector.reciprocal(rec[:, :], og[64:128, :]).then_inc(og_step, 1)
            dve.wait_ge(og_step, count(og_step, b, 2 * k + 1))
            if k == 0:
                dve.wait_ge(wo_ready, count(wo_ready, b, 0))
            nc.vector.tensor_tensor(ot[64 * k:64 * k + 64, :], og[0:64, :], rec[:, :], ALU.mult).then_inc(og_step, 1)

        def dve_post(dve, b, k):
            if k == 0:
                dve.wait_ge(wo_ready, count(wo_ready, b, 1))
                dve.wait_ge(kept, count(kept, b, 1))
                dve.wait_ge(ye_done, count(ye_done, b, 0))
                dve.wait_ge(post_step, count(post_step, b, 0))
                nc.vector.tensor_tensor(x2[:, :, :], m0[:, :].rearrange("p (c m) -> p c m", c=TC), hres[:, :, :],
                                        ALU.add).then_inc(x2_done, 1)
            elif k == 1:
                dve.wait_ge(x2_done, count(x2_done, b, 1))
                dve_stats(1, x2, post_step)
            elif k == 2:
                dve_aggr(1, post_step)
            else:
                dve.wait_ge(post_rstd, count(post_rstd, b, 4))
                dve.wait_ge(x2t_ready, count(x2t_ready, b, 0))
                dve_norm(1, h2n, x2, post_step, True)

        def over(a, axis):
            return a[:, :, :].unsqueeze(axis).to_broadcast([P, TC, NE, NE])

        def dve_gate(dve, b, k):
            s = gate_step
            v = nc.vector
            if k == 0:
                dve.wait_ge(gate_ready, count(gate_ready, b, 1))
                dve.wait_ge(s, count(s, b, 0))
                i = v.tensor_copy(lg[:, :, :].rearrange("p c e -> p (c e)"), m0[:, 0:TC * NE])
            else:
                dve.wait_ge(s, count(s, b, k))
            if k == 1:
                i = v.reduce_max(lmax[:, :], lg[:, :, :], mybir.AxisListType.X)
            if k == 2:
                i = v.tensor_tensor(ex[:, :, :], lg[:, :, :], lmax[:, :].unsqueeze(2).to_broadcast([P, TC, NE]),
                                    ALU.subtract)
            if k == 3:
                i = v.tensor_tensor(gtm[:, :, :, :], over(lg, 2), over(lg, 3), ALU.is_gt)
            if k == 4:
                i = v.tensor_tensor(eqm[:, :, :, :], over(lg, 2), over(lg, 3), ALU.is_equal)
            if k == 5:
                i = v.tensor_tensor(eqm[:, :, :, :], eqm[:, :, :, :],
                                    tri[:, :, :].unsqueeze(1).to_broadcast([P, TC, NE, NE]), ALU.mult)
            if k == 6:
                i = v.tensor_tensor(gtm[:, :, :, :], gtm[:, :, :, :], eqm[:, :, :, :], ALU.add)
            if k == 7:
                i = v.reduce_sum(rank[:, :, :], gtm[:, :, :, :], mybir.AxisListType.X)
            if k == 8:
                dve.wait_ge(ex_done, count(ex_done, b, 1))
                i = v.scalar_tensor_tensor(rank[:, :, :], rank[:, :, :], 1.5, ex[:, :, :], ALU.is_lt, ALU.mult)
            if k == 9:
                i = v.reduce_sum(wsum[:, 0, :], rank[:, :, :], mybir.AxisListType.X)
            if k == 10:
                i = v.reciprocal(wsum[:, 1, :], wsum[:, 0, :])
            if k == 11:
                dve.wait_ge(wt_ready, count(wt_ready, b, 0))
                i = v.tensor_tensor(wrep[:, :, :, 0:NE], rank[:, :, :].unsqueeze(2).to_broadcast([P, TC, 3, NE]),
                                    wsum[:, 1, :].unsqueeze(2).unsqueeze(3).to_broadcast([P, TC, 3, NE]), ALU.mult)
            i.then_inc(s, 1)

        def dve_wpart(dve, b, k):
            if k == 0:
                dve.wait_ge(wpart_act, count(wpart_act, b, 1))
                dve.wait_ge(wpart_dve, count(wpart_dve, b, 0))
                nc.vector.tensor_tensor(wrem[:, :], m0[0:SPLIT_ROWS, :], wst[:, :],
                                        ALU.subtract).then_inc(wpart_dve, 1)
            else:
                dve.wait_ge(wpart_act, count(wpart_act, b, 3))
                nc.vector.tensor_tensor(wst[64:96, :], wrem[64:96, :], wmid[64:96, :],
                                        ALU.subtract).then_inc(wpart_dve, 1)

        def dve_h2e(dve, b, e):
            dve.wait_ge(wbc_ready, count(wbc_ready, b, e + 1))
            dve.wait_ge(b_ready, count(b_ready, b, NF * (e - 1)))
            nc.vector.tensor_tensor(h2e[:, e % 2, :], h2t[:, :], m1[:, :], ALU.mult).then_inc(h2e_done, 1)

        def dve_ga(dve, b, n):
            dve.wait_ge(th_done, count(th_done, b, n + 1))
            dve.wait_ge(g_done, count(g_done, b, n - 1))
            nc.vector.scalar_tensor_tensor(ga[:, n % 2, :], th[:, n % 2, :], 1.0, pa[:, :],
                                           ALU.add, ALU.mult).then_inc(ga_done, 1)

        def dve_g(dve, b, n):
            dve.wait_ge(b_ready, count(b_ready, b, n + 1))
            dve.wait_ge(ga_done, count(ga_done, b, n + 1))
            dve.wait_ge(down_done, count(down_done, b, n - 1))
            nc.vector.scalar_tensor_tensor(g[:, n % 2, :], ga[:, n % 2, :], 0.5, pbk[:, :],
                                           ALU.mult, ALU.mult).then_inc(g_done, 1)

        def dve_end(dve, b, k):
            if k == 0:
                dve.wait_ge(ot_ready, count(ot_ready, b, 1))
                dve.wait_ge(end_step, count(end_step, b, 0))
                nc.vector.tensor_tensor(ye[:, :, :], m1[:, :].rearrange("p (c m) -> p c m", c=TC), x2[:, :, :],
                                        ALU.add).then_inc(ye_done, 1)
            elif k == 1:
                dve.wait_ge(ye_done, count(ye_done, b, 1))
                dve_stats(2, ye, end_step)
            elif k == 2:
                dve_aggr(2, end_step)
            elif k == 3:
                dve.wait_ge(end_rstd, count(end_rstd, b, 2))
                dve.wait_ge(out_stored, count(out_stored, b, 0))
                dve_norm(2, yo, ye, end_step, False)
            else:
                dve.wait_ge(end_step, count(end_step, b, 12))
                dve.wait_ge(xr_loaded, count(xr_loaded, b, 16))
                nc.vector.tensor_tensor(yo[:, :, :], yo[:, :, :], xr[:, :, :], ALU.add).then_inc(out_done, 1)

        def dve_main(dve, att=None, moe=None, front=None):
            if moe is not None:
                dve_h2e(dve, moe, 0)
            for t in range(ST_TILES):
                i, j = t // NPT, t % NPT
                if front is not None and t in (3, 8):
                    dve.wait_ge(in_step, count(in_step, front, {3: 4, 8: 16}[t]))
                if moe is not None:
                    if j == 1:
                        dve_ga(dve, moe, 2 * i)
                    if j == 2:
                        dve_g(dve, moe, 2 * i)
                        if i + 1 < NE:
                            dve_h2e(dve, moe, i + 1)
                    if j == 3:
                        dve_ga(dve, moe, 2 * i + 1)
                    if j == 4:
                        dve_g(dve, moe, 2 * i + 1)
                if att is not None and t == 21:
                    dve_og(dve, att, 0)
                if front is not None:
                    if t in (1, 3, 5, 7, 8, 11):
                        dve_in(dve, front, (1, 3, 5, 7, 8, 11).index(t))
                    if t in (19, 22, 25, 26):
                        dve_rope(dve, front, (19, 22, 25, 26).index(t))
            if att is not None:
                dve_og(dve, att, 1)

        def dve_turn(dve, post=None, end=None, top=None):
            if end is not None:
                dve_end(dve, end, 0)
            if post is not None:
                dve_post(dve, post, 0)
                dve_post(dve, post, 1)
            for t in range(MT):
                if post is not None and t == 0:
                    dve.wait_ge(post_step, count(post_step, post, 4))
                if end is not None and t == 7:
                    dve.wait_ge(end_step, count(end_step, end, 4))
                if top is not None:
                    dve_max(dve, top, t)
                if post is not None:
                    if t == 0:
                        dve_post(dve, post, 2)
                    if t == 5:
                        dve_post(dve, post, 3)
                    if 18 <= t < 30:
                        dve_gate(dve, post, t - 18)
                    if t in (36, 40):
                        dve_wpart(dve, post, (t - 36) // 4)
                if end is not None and t in (6, 7, 10, 11):
                    dve_end(dve, end, {6: 1, 7: 2, 10: 3, 11: 4}[t])
            if top is not None:
                dve_nm(dve, top)

        @block.vector
        def _(dve):
            for s, per in credited["vector"]:
                dve.sem_inc(s, per)
            for k in range(6):
                if k in (1, 4):
                    dve.wait_ge(in_step, count(in_step, 0, {1: 4, 4: 16}[k]))
                dve_in(dve, 0, k)
            dve.wait_ge(loaded, n_weights)
            for k in range(4):
                dve_rope(dve, 0, k)
            dve_turn(dve, top=0)
            dve.wait_ge(consts, 6)
            dve_main(dve, att=0, front=1)
            dve_turn(dve, post=0, top=1)
            with dve.Fori(1, NB - 1) as b:
                dve_main(dve, att=b, moe=b - 1, front=b + 1)
                dve_turn(dve, post=b, end=b - 1, top=b + 1)
            dve_main(dve, att=NB - 1, moe=NB - 2)
            dve_turn(dve, post=NB - 1, end=NB - 2)
            dve_main(dve, moe=NB - 1)
            dve_turn(dve, end=NB - 1)

        def pool_rstd(pool, b, side, done, at, steps, after):
            pool.wait_ge(steps, count(steps, b, after))
            nc.gpsimd.tensor_tensor(rt[:, side, 2, :], mv[:, side, :, 1], eps[:, :], ALU.add).then_inc(done, 1)
            pool.wait_ge(done, count(done, b, at + 1))
            nc.gpsimd.tensor_tensor(rt[:, side, 3, :], rt[:, side, 2, :], mhalf[:, :], ALU.pow).then_inc(done, 1)

        def pool_rms(pool, b, side, done, at, steps, after):
            pool.wait_ge(steps, count(steps, b, after))
            nc.gpsimd.tensor_tensor(rt[:, side, 0, :], mv[:, side, :, 0], mv[:, side, :, 0],
                                    ALU.mult).then_inc(done, 1)
            pool.wait_ge(done, count(done, b, at + 1))
            nc.gpsimd.tensor_tensor(rt[:, side, 1, :], rt[:, side, 0, :], mv[:, side, :, 1],
                                    ALU.add).then_inc(done, 1)
            pool.wait_ge(done, count(done, b, at + 2))
            nc.gpsimd.tensor_tensor(rt[:, side, 2, :], rt[:, side, 1, :], eps[:, :], ALU.add).then_inc(done, 1)
            pool.wait_ge(done, count(done, b, at + 3))
            nc.gpsimd.tensor_tensor(rt[:, side, 3, :], rt[:, side, 2, :], mhalf[:, :], ALU.pow).then_inc(done, 1)

        def pool_add(pool, b, k):
            src, dst = ((rot, qf), (rotk, kf))[k]
            pool.wait_ge(rope_mul, count(rope_mul, b, 2 * k + 2))
            pool.wait_ge(part_act, count(part_act, b, 0))
            pool.wait_ge(part_pool, count(part_pool, b, 0))
            nc.gpsimd.tensor_tensor(dst[:, :], src[:, 0, :], src[:, 1, :], ALU.add).then_inc(rope_add, 1)

        def pool_part(pool, b, k):
            src, parts, rem = ((qf, qp, rot), (kf, kp, rotk))[k // 2]
            if k % 2 == 0:
                pool.wait_ge(part_act, count(part_act, b, 1 if k == 0 else 2))
                pool.wait_ge(rope_add, count(rope_add, b, k // 2 + 1))
                nc.gpsimd.tensor_tensor(rem[:, 0, :], src[:, :], parts[:, 0, :],
                                        ALU.subtract).then_inc(part_pool, 1)
            else:
                pool.wait_ge(part_act, count(part_act, b, 3 if k == 1 else 4))
                nc.gpsimd.tensor_tensor(parts[:, 2, :], rem[:, 0, :], parts[:, 1, :],
                                        ALU.subtract).then_inc(part_pool, 1)

        def pool_nm(pool, b):
            pool.wait_ge(nm_act, count(nm_act, b, 2))
            pool.wait_ge(m_written, count(m_written, b, 0))
            nc.gpsimd.tensor_tensor(nm[:, 2, :], nmr[:, :], nm[:, 1, :], ALU.subtract).then_inc(nm_pool, 1)

        def pool_main(pool, front=None):
            if front is not None:
                pool_rstd(pool, front, 0, in_rstd, 0, in_step, 8)
                pool_rms(pool, front, 0, in_rstd, 2, in_step, 20)
                pool_add(pool, front, 0)
                pool_add(pool, front, 1)
                for k in (0, 2, 1, 3):
                    pool_part(pool, front, k)

        def pool_turn(pool, post=None, end=None, top=None):
            if post is not None:
                pool_rms(pool, post, 1, post_rstd, 0, post_step, 8)
            if end is not None:
                pool_rstd(pool, end, 2, end_rstd, 0, end_step, 8)
            if top is not None:
                pool_nm(pool, top)

        @block.gpsimd
        def _(pool):
            for s, per in credited["gpsimd"]:
                pool.sem_inc(s, per)
            nc.gpsimd.memset(mhalf[:, :], -0.5).then_inc(consts, 1)
            nc.gpsimd.memset(eps[:, :], EPS).then_inc(consts, 1)
            nc.gpsimd.memset(k9[:, :, :], 1.0).then_inc(consts, 1)
            nc.gpsimd.memset(wrep[:, :, :, :], 0.0).then_inc(consts, 1)
            nc.gpsimd.memset(vpad[:, :, :, :], 0.0).then_inc(consts, 1)
            pool.wait_ge(consts, 5)
            for c in range(TC):
                for gi in range(2):
                    a = vpad_diag(c, gi)
                    ones = bass.AP(tensor=a.tensor, offset=a.offset + 64, ap=[list(x) for x in a.ap])
                    last = nc.gpsimd.memset(ones, 1.0)
            last.then_inc(consts, 1)
            pool.wait_ge(loaded, n_weights)
            nc.gpsimd.tensor_copy(identb[:, :], ident[:, :]).then_inc(casts, 1)
            nc.gpsimd.tensor_copy(mask[:, :, :], mask32[:, :, :]).then_inc(casts, 1)
            nc.gpsimd.tensor_copy(sel[:, :, :], sel32[:, :, :]).then_inc(casts, 1)
            pool_main(pool, front=0)
            pool_turn(pool, top=0)
            pool_main(pool, front=1)
            pool_turn(pool, post=0, top=1)
            with pool.Fori(1, NB - 1) as b:
                pool_main(pool, front=b + 1)
                pool_turn(pool, post=b, end=b - 1, top=b + 1)
            pool_turn(pool, post=NB - 1, end=NB - 2)
            pool_turn(pool, end=NB - 1)


def program(nc, x, out, scratch, w_mamba, w_ffn):
    with ExitStack() as sems:
        mamba_phase(nc, sems, x, scratch["x1"], scratch["c"], w_mamba)
        ffn_phase(nc, sems, scratch["x1"], out, scratch["q"], scratch["k"], scratch["m"], w_ffn)


def lay_out_mamba(v):
    def both(name):
        return [np.asarray(v[f"L0_attn_{d}_{name}"]) for d in "fb"]

    win, taps, wx_in, wdt_in = both("Win"), both("convw"), both("Wx"), both("Wdt")
    wx = np.zeros((P, NDIR, NH2, P), np.float32)
    wdt = np.zeros((P, NDIR, DI), np.float32)
    for d in range(NDIR):
        for h in range(NH2):
            t = wx_in[d].T[h * P:(h + 1) * P]
            for part in range(3):
                wx[:, d, h, 32 * part:32 * part + 2 * NS] = t[:, DTR:]
            wx[:, d, h, DT_ROW:DT_ROW + DTR] = t[:, :DTR]
        wdt[DT_ROW:DT_ROW + DTR, d] = wdt_in[d].T
    sel = np.zeros((SPLIT_ROWS, NS, P), np.float32)
    for n in range(NS):
        sel[n::32, n, :] = 1
    return {
        "ident": np.eye(P, dtype=np.float32),
        "win_u": np.stack([a[:DI].T for a in win], 1),
        "win_z": np.stack([a[DI:].T for a in win], 1),
        "tap_w": np.broadcast_to(np.stack([a[:, 0, :].T for a in taps])[None], (P, NDIR, NTAP, DI)),
        "wx": wx,
        "wdt": wdt,
        "wout": np.stack([a.T.reshape(NH2, P, DM).transpose(1, 0, 2) for a in both("Wout")], 1),
        "col": np.stack([np.stack([a.reshape(NH2, P).T for a in c], -1)
                         for c in zip(both("convb"), both("bdt"), both("D"))], 1),
        "alog": np.stack([a.reshape(NH2, P, NS).transpose(1, 0, 2) for a in both("Alog")], 1),
        "ncol": np.stack([np.asarray(v["L0_attn_norm_g"]), np.asarray(v["L0_attn_norm_b"])], 1),
        "sel": sel,
    }


def lay_out_ffn(v):
    def get(name):
        return np.asarray(v["L0_ffn_" + name])

    def swapped(a):
        return a.reshape(-1, 2, HD // 2, DM)[:, ::-1].reshape(a.shape)

    i = np.arange(P)
    causal = np.where(i[None, :] > i[:, None], np.float32(-1e30), np.float32(0))
    inv = np.float32(1) / np.power(np.float32(10000), np.arange(0, HD, 2, dtype=np.float32) / np.float32(HD))
    angle = np.arange(SEQ, dtype=np.float32)[:, None] * inv.astype(np.float32)[None]
    angle = np.concatenate([angle, angle], -1)
    sign = np.where(np.arange(HD) < HD // 2, -1, 1).astype(np.float32)
    wqkv = get("wqkv")
    q, k, value = wqkv[:NHEAD * HD], wqkv[NHEAD * HD:(NHEAD + NKV) * HD], wqkv[(NHEAD + NKV) * HD:]
    sel = np.zeros((SPLIT_ROWS, NE, P), np.float32)
    for e in range(NE):
        sel[e::32, e, :] = 1
    return {
        "ident": np.eye(P, dtype=np.float32),
        "mask": np.stack([causal, causal.T], 1),
        "trig": np.stack([np.tile(np.cos(angle).T, (NHEAD, 1)),
                          np.tile(np.sin(angle).T * sign[:, None], (NHEAD, 1))], 1).astype(np.float32),
        "wq": np.stack([q.T, swapped(q).T], 1),
        "wk": np.concatenate([k.T, swapped(k).T], 1),
        "wv": value.T,
        "wo": get("wo").T,
        "gate": get("gate_w").T,
        "lnw": np.stack([get("ln1_w"), get("ln2_w")], 1),
        "tri": np.broadcast_to(np.tril(np.ones((NE, NE), np.float32), -1)[None], (P, NE, NE)),
        "sel_e": sel,
        "w13": get("w13").transpose(2, 0, 1),
        "w2": get("w2").transpose(2, 0, 1).reshape(NF, P, NE, DM).transpose(1, 2, 0, 3),
    }


def kernel(**inputs):
    import concourse.bacc as bacc
    from concourse.bass_utils import run_bass_kernel_spmd

    nc = bacc.Bacc("TRN2", target_bir_lowering=False, num_devices=1)
    arrays = {}

    def given(prefix, parts):
        aps = {}
        for name, a in parts.items():
            arrays[prefix + name] = np.ascontiguousarray(a)
            aps[name] = nc.dram_tensor(prefix + name, a.shape, F32, kind="ExternalInput").ap()
        return aps

    x = given("in_", {"x": np.asarray(inputs["L0_attn_x"])})["x"]
    w_mamba = given("mamba_", lay_out_mamba(inputs))
    w_ffn = given("ffn_", lay_out_ffn(inputs))
    out = nc.dram_tensor("out", (NB, SEQ, DM), F32, kind="ExternalOutput").ap()
    scratch = {
        "x1": nc.dram_tensor("x1_scratch", (NB, SEQ, DM), F32, kind="Internal").ap(),
        "c": nc.dram_tensor("c_scratch", (NDIR, NS, SEQ), F32, kind="Internal").ap(),
        "q": nc.dram_tensor("q_scratch", (3, HD, NHEAD, SEQ), BF16, kind="Internal").ap(),
        "k": nc.dram_tensor("k_scratch", (3, HD, NKV, SEQ), BF16, kind="Internal").ap(),
        "m": nc.dram_tensor("m_scratch", (3, NHEAD, SEQ), BF16, kind="Internal").ap(),
    }
    program(nc, x, out, scratch, w_mamba, w_ffn)
    r = run_bass_kernel_spmd(nc, [arrays], core_ids=[0])
    return r.results[0]["out"]
```

```python
from contextlib import ExitStack

import numpy as np

import concourse.bass as bass
from concourse import mybir

ALU = mybir.AluOpType
ACT = mybir.ActivationFunctionType
F32 = mybir.dt.float32
BF16 = mybir.dt.bfloat16
F16 = mybir.dt.float16

P = 128
NB = 8
SEQ = 512
DM = 128
TC = SEQ // P
DI = 256
NH2 = DI // P
NS = 16
NTAP = 4
DTR = 8
NDIR = 2
STEPS = NS * NH2
EPS = 1e-5
C_FIRST = 4
LAG_Y = 5
SPLIT_ROWS = 3 * 32
DT_ROW = 96


class Counts:

    def __init__(self):
        self.per, self.ahead = {}, {}

    def add(self, sem, per, credited):
        self.per[sem.name], self.ahead[sem.name] = per, per if credited else 0

    def __call__(self, sem, b, c):
        per, ahead = self.per[sem.name], self.ahead[sem.name]
        assert c >= 1 or (ahead and c > -per), (sem.name, c)
        value = b * per + c + ahead
        assert not isinstance(value, int) or value > 0, (sem.name, b, c)
        return value

    def in_register(self, eng, sem, b, c):
        value = self(sem, b, c)
        return value if isinstance(value, int) else eng.to_reg(value)


def is_first(b):
    return isinstance(b, int) and b == 0


def mamba_phase(nc, sems, x, x1, cscr, w):
    with ExitStack() as ctx:
        def sb(name, shape, dt=F32):
            return ctx.enter_context(nc.sbuf_tensor(name, shape, dt))

        def pb(name, shape):
            return ctx.enter_context(nc.psum_tensor(name, shape, F32))

        count = Counts()
        credited = {e: [] for e in ("sync", "tensor", "scalar", "vector", "gpsimd")}

        def sig(name, per, producer=None):
            s = sems.enter_context(nc.semaphore(name))
            count.add(s, per, producer is not None)
            if producer is not None:
                credited[producer].append((s, per))
            return s

        ident = sb("ident", [P, P])
        win_u = sb("win_u", [P, NDIR, DI])
        win_z = sb("win_z", [P, NDIR, DI])
        wu = sb("wu", [P, NDIR, NTAP, DI])
        wx = sb("wx", [P, NDIR, NH2, P])
        wdt = sb("wdt", [P, NDIR, DI])
        wout = sb("wout", [P, NDIR, NH2, DM])
        col = sb("col", [P, NDIR, NH2, 3])
        a_neg = sb("a_neg", [P, NDIR, NH2, NS])
        ncol = sb("ncol", [P, 2])
        sel = sb("sel", [SPLIT_ROWS, NS, P], BF16)
        mhalf = sb("mhalf", [P, TC])
        eps = sb("eps", [P, TC])
        xin = sb("xin", [P, TC, DM])
        xln = sb("xln", [P, TC, DM])
        xres = sb("xres", [P, 2, TC, DM])
        xn = sb("xn", [P, TC, DM])
        stats = sb("stats", [P, 2, TC, 6])
        mv = sb("mv", [P, 2, TC, 2])
        rstd = sb("rstd", [P, 2, 2, TC])
        xpad = sb("xpad", [P, NDIR, NTAP - 1 + SEQ])
        u = sb("u", [P, NH2, SEQ])
        sz = sb("sz", [P, NDIR, TC, DI])
        xd = sb("xd", [P, SEQ])
        st = sb("st", [SPLIT_ROWS, NDIR, SEQ], BF16)
        rem = sb("rem", [SPLIT_ROWS, SEQ])
        mid2 = sb("mid2", [32, SEQ], BF16)
        t_abs = sb("t_abs", [P, SEQ])
        t_ln = sb("t_ln", [P, NH2, SEQ])
        t_relu = sb("t_relu", [P, NH2, SEQ])
        dt = sb("dt", [P, NDIR, NH2, SEQ])
        dtu = sb("dtu", [P, NDIR, NH2, SEQ])
        ud = sb("ud", [P, NH2, SEQ])
        cb = sb("cb", [P, NDIR, NS, SEQ])
        yg = sb("yg", [P, TC, DI])
        ygt = sb("ygt", [P, NDIR, NH2, SEQ])
        res = sb("res", [P, TC, DM])
        x1t = sb("x1t", [P, TC, DM])
        NDA, NHB, NHC = 8, 4, 8
        da = sb("da", [P, NDA, SEQ])
        sel32 = da[0:SPLIT_ROWS, 0:NS * P // SEQ, :].rearrange("r a (n p) -> r (a n) p", p=P)
        hb = sb("hb", [P, NHB, SEQ])
        hc = sb("hc", [P, NHC, SEQ])
        bp = pb("bp", [P, 2, SEQ])
        dbu = pb("dbu", [P, 2, SEQ])
        yp = pb("yp", [P, TC, DI])
        wp = pb("wp", [P, 2, SEQ])

        weights_loaded = sems.enter_context(nc.semaphore("weights_loaded"))
        taps_folded = sems.enter_context(nc.semaphore("taps_folded"))
        sel_cast = sems.enter_context(nc.semaphore("sel_cast"))
        a_ready = sems.enter_context(nc.semaphore("a_ready"))
        consts_set = sems.enter_context(nc.semaphore("consts_set"))

        x_loaded = sig("x_loaded", 16)
        x_kept = sig("x_kept", 32, "sync")
        c_written = sig("c_written", 32, "sync")
        c_first = sig("c_first", 32, "sync")
        c_rest = sig("c_rest", 32, "sync")
        x1_stored = sig("x1_stored", 16, "sync")

        xt_ready = sig("xt_ready", 1, "tensor")
        u_ready = sig("u_ready", 4)
        z_ready = sig("z_ready", 4, "tensor")
        xd_ready = sig("xd_ready", 2, "tensor")
        dtp_ready = sig("dtp_ready", 4, "tensor")
        b_ready = sig("b_ready", NDIR * NS, "tensor")
        y_added = sig("y_added", NDIR * (STEPS + 1), "tensor")
        ygt_ready = sig("ygt_ready", 4, "tensor")
        out_ready = sig("out_ready", 1, "tensor")

        xpad_done = sig("xpad_done", 2)
        silu_done = sig("silu_done", 8)
        xd_done = sig("xd_done", 8, "scalar")
        soft_done = sig("soft_done", 16, "scalar")
        ud_done = sig("ud_done", 4)
        da_done = sig("da_done", NDIR * STEPS, "scalar")
        ygt_done = sig("ygt_done", 4, "scalar")

        ln_step = sig("ln_step", 24, "vector")
        end_step = sig("end_step", 12, "vector")
        part_done = sig("part_done", 2, "gpsimd")
        dt_done = sig("dt_done", 4, "vector")
        dbu_done = sig("dbu_done", NDIR * STEPS, "vector")
        scan_done = sig("scan_done", NDIR * STEPS, "vector")
        yg_done = sig("yg_done", 2, "vector")
        res_done = sig("res_done", 1, "vector")
        x1_done = sig("x1_done", 1, "gpsimd")

        rstd_done = sig("rstd_done", 4)
        end_rstd = sig("end_rstd", 2)
        rem_done = sig("rem_done", 2, "gpsimd")
        hc_done = sig("hc_done", NDIR * STEPS, "gpsimd")

        block = ctx.enter_context(nc.Block())
        weights = ((ident, "ident"), (win_u, "win_u"), (win_z, "win_z"), (wu, "tap_w"), (wx, "wx"),
                   (wdt, "wdt"), (wout, "wout"), (col, "col"), (a_neg, "alog"), (ncol, "ncol"), (sel32, "sel"))
        n_weights = 16 * len(weights)

        def y_count(d, s):
            return (STEPS + 1) * d + s + (2 if s >= 0 else 1)

        def sp_x_load(sp, b, first=False):
            if not first:
                sp.wait_ge(ln_step, count(ln_step, b, 12 - 24))
                sp.wait_ge(x_kept, count(x_kept, b, 0))
            sp.dma_start(xin[:, :, :].rearrange("p (a c) m -> p a c m", a=1),
                         x[bass.ds(b, 1)].rearrange("a (c p) m -> p a c m", p=P)).then_inc(x_loaded, 16)

        def sp_keep(sp, b):
            sp.wait_ge(ln_step, count(ln_step, b, 12))
            sp.wait_ge(x1_done, count(x1_done, b, 0))
            sp.dma_start(xres[:, 0], xin[:, :, :]).then_inc(x_kept, 16)
            sp.dma_start(xres[:, 1], xln[:, :, :]).then_inc(x_kept, 16)

        def sp_c(sp, b, d):
            xd_now = count.in_register(sp, xd_done, b, 4 * d + 2)
            c_before = count.in_register(sp, c_rest, b, 16 * d - 16)
            sp.wait_ge(xd_done, xd_now)
            sp.wait_ge(c_rest, c_before)
            sp.wait_ge(c_first, count(c_first, b, 16 * d - 16))
            sp.dma_start(cscr[d], xd[NS:2 * NS, :]).then_inc(c_written, 16)
            written = count.in_register(sp, c_written, b, 16 * d + 16)
            hc_before = count.in_register(sp, hc_done, b, STEPS * (d - 1))
            sp.wait_ge(c_written, written)
            sp.wait_ge(hc_done, hc_before)
            sp.dma_start(cb[:, d, 0:C_FIRST], cscr[d:d + 1, 0:C_FIRST].to_broadcast([P, C_FIRST, SEQ])
                         ).then_inc(c_first, 16)
            sp.dma_start(cb[:, d, C_FIRST:], cscr[d:d + 1, C_FIRST:].to_broadcast([P, NS - C_FIRST, SEQ])
                         ).then_inc(c_rest, 16)

        def sp_store(sp, b):
            sp.wait_ge(x1_done, count(x1_done, b, 1))
            sp.dma_start(x1[bass.ds(b, 1)].rearrange("a (c p) m -> p a c m", p=P),
                         x1t[:, :, :].rearrange("p (a c) m -> p a c m", a=1)).then_inc(x1_stored, 16)

        @block.sync
        def _(sp):
            for s, per in credited["sync"]:
                sp.sem_inc(s, per)
            sp_x_load(sp, 0, first=True)
            for dst, name in weights:
                sp.dma_start(dst[...], w[name]).then_inc(weights_loaded, 16)
            sp_c(sp, 0, 0)
            sp_keep(sp, 0)
            sp_c(sp, 0, 1)
            with sp.Fori(0, NB - 1) as b:
                sp_x_load(sp, b + 1)
                sp_c(sp, b + 1, 0)
                sp_store(sp, b)
                sp_keep(sp, b + 1)
                sp_c(sp, b + 1, 1)
            sp_store(sp, NB - 1)
            sp.wait_ge(x1_stored, count(x1_stored, NB - 1, 16))

        def pe_xt(pe, b, first=False):
            pe.wait_ge(ln_step, count(ln_step, b, 24))
            if not first:
                pe.wait_ge(ygt_done, count(ygt_done, b - 1, 2))
            for c in range(TC):
                last = nc.tensor.transpose(wp[:, 1, c * P:(c + 1) * P], xn[:, c, :], ident[:, :])
            last.then_inc(xt_ready, 1)

        def pe_u(pe, b, d, i, first=False):
            k, j = i // NTAP, i % NTAP
            h = k ^ d
            if i == 0:
                pe.wait_ge(xpad_done, count(xpad_done, b, 2))
                if d:
                    pe.wait_ge(ygt_done, count(ygt_done, b, 0))
                elif not first:
                    pe.wait_ge(ygt_done, count(ygt_done, b - 1, 2))
            if i == NTAP and d:
                pe.wait_ge(res_done, count(res_done, b, 0))
            last = nc.tensor.matmul(wp[:, h, :], wu[:, d, j, h * P:(h + 1) * P], xpad[:, d, j:j + SEQ],
                                    start=(j == 0), stop=(j == NTAP - 1))
            if j == NTAP - 1:
                last.then_inc(u_ready, 1)

        def pe_z(pe, b, d, k):
            pe.wait_ge(silu_done, count(silu_done, b, 4 * d + k + 1))
            h = k ^ d
            for c in (2 * h, 2 * h + 1):
                last = nc.tensor.matmul(wp[:, h, (c % 2) * DI:(c % 2 + 1) * DI],
                                        xpad[:, d, NTAP - 1 + c * P:NTAP - 1 + (c + 1) * P], win_z[:, d, :],
                                        start=True, stop=True)
            last.then_inc(z_ready, 1)

        def pe_xd(pe, b, d):
            pe.wait_ge(silu_done, count(silu_done, b, 4 * d + 3))
            for h in range(NH2):
                last = nc.tensor.matmul(wp[:, d, :], wx[:, d, h, :], u[:, h, :], start=(h == 0), stop=(h == 1))
            last.then_inc(xd_ready, 1)

        def pe_dt(pe, b, d, h):
            if h == 0:
                pe.wait_ge(silu_done, count(silu_done, b, 4 * d + 4))
                pe.wait_ge(xd_done, count(xd_done, b, 4 * d + 2))
            nc.tensor.matmul(wp[:, 1 - (h ^ d), :], wdt[:, d, h * P:(h + 1) * P], xd[:, :],
                             start=True, stop=True).then_inc(dtp_ready, 1)

        def pe_b(pe, b, d, n):
            if n == 0:
                pe.wait_ge(part_done, count(part_done, b, d + 1))
                pe.wait_ge(xd_done, count(xd_done, b, 4 * d + 3))
            pe.wait_ge(dbu_done, count(dbu_done, b, STEPS * d + 2 * (n - 1)))
            nc.tensor.matmul(bp[:, n % 2, :], sel[:, n, :], st[:, d, :], start=True, stop=True).then_inc(b_ready, 1)

        def pe_y(pe, b, d, s):
            if s < 0:
                pe.wait_ge(ud_done, count(ud_done, b, 2 * d + 2))
                pe.wait_ge(yg_done, count(yg_done, b, d))
            else:
                pe.wait_ge(hc_done, count(hc_done, b, STEPS * d + s + 1))
            for h in (range(NH2) if s < 0 else (s % 2,)):
                src = ud[:, h, :] if s < 0 else hc[:, s % NHC, :]
                for c in range(TC):
                    last = nc.tensor.matmul(yp[:, c, h * P:(h + 1) * P], src[:, c * P:(c + 1) * P], ident[:, :],
                                            is_transpose=True, start=(s < 0 and h == 0 and c % 2 == 0),
                                            stop=(s == STEPS - 1), skip_group_check=True)
            last.then_inc(y_added, 1)

        def pe_ygt(pe, b, d, last_unit=False):
            pe.wait_ge(yg_done, count(yg_done, b, d + 1))
            if last_unit:
                pe.wait_ge(ygt_done, count(ygt_done, b, 2))
                pe.wait_ge(res_done, count(res_done, b, 0))
            elif d:
                pe.wait_ge(soft_done, count(soft_done, b + 1, 8))
            else:
                pe.wait_ge(soft_done, count(soft_done, b, 16))
            for h in range(NH2):
                for c in range(TC):
                    last = nc.tensor.transpose(wp[:, h, c * P:(c + 1) * P], yg[:, c, h * P:(h + 1) * P], ident[:, :])
                last.then_inc(ygt_ready, 1)

        def pe_out(pe, b, c):
            pe.wait_ge(ygt_done, count(ygt_done, b, 4))
            for k in range(NDIR * NH2):
                last = nc.tensor.matmul(wp[:, 0, c * P:(c + 1) * P], ygt[:, k // 2, k % 2, c * P:(c + 1) * P],
                                        wout[:, k // 2, k % 2, :], start=(k == 0), stop=(k == 3))
            if c == TC - 1:
                last.then_inc(out_ready, 1)

        def pe_unit(pe, b, d, front=None, tail=None, after=None):
            for s in range(STEPS):
                if s % 2 == 1 and s // 2 + 1 < NS:
                    pe_b(pe, b, d, s // 2 + 1)
                if s == STEPS - 1 and after:
                    pe_b(pe, *after, 0)
                if tail and s == 0:
                    pe_y(pe, *tail, STEPS - LAG_Y)
                if tail and s < LAG_Y - 1:
                    pe_y(pe, *tail, STEPS - LAG_Y + 1 + s)
                if s == LAG_Y + 2:
                    pe_y(pe, b, d, -1)
                    pe_y(pe, b, d, 0)
                    pe_y(pe, b, d, 1)
                if s >= LAG_Y + 2:
                    pe_y(pe, b, d, s - LAG_Y)
                if tail and s == 7:
                    pe_ygt(pe, *tail)
                if tail and tail[1] == 1 and s in (10, 11, 12, 13):
                    pe_out(pe, tail[0], s - 10)
                if front:
                    if s == 10 and front[1] == 0:
                        pe_xt(pe, front[0])
                    for i in range(NH2 * NTAP):
                        if s == (12, 13, 14, 15, 15, 16, 17, 18)[i]:
                            pe_u(pe, *front, i)
                    if s in (19, 20):
                        pe_z(pe, *front, s - 19)
                    if s == 21:
                        pe_xd(pe, *front)
                    if s in (24, 25):
                        pe_dt(pe, *front, s - 24)
            if not after:
                for s in range(STEPS - LAG_Y, STEPS):
                    pe_y(pe, b, d, s)

        @block.tensor
        def _(pe):
            for s, per in credited["tensor"]:
                pe.sem_inc(s, per)
            pe.wait_ge(weights_loaded, n_weights)
            pe.wait_ge(taps_folded, NDIR)
            pe_xt(pe, 0, first=True)
            for i in range(NH2 * NTAP):
                pe_u(pe, 0, 0, i, first=True)
            pe_z(pe, 0, 0, 0)
            pe_z(pe, 0, 0, 1)
            pe_xd(pe, 0, 0)
            pe_dt(pe, 0, 0, 0)
            pe_dt(pe, 0, 0, 1)
            pe.wait_ge(sel_cast, 1)
            pe_b(pe, 0, 0, 0)
            pe_unit(pe, 0, 0, front=(0, 1), after=(0, 1))
            with pe.Fori(0, NB - 1) as b:
                pe_unit(pe, b, 1, front=(b + 1, 0), tail=(b, 0), after=(b + 1, 0))
                pe_unit(pe, b + 1, 0, front=(b + 1, 1), tail=(b, 1), after=(b + 1, 1))
            pe_unit(pe, NB - 1, 1, tail=(NB - 1, 0))
            pe_ygt(pe, NB - 1, 1, last_unit=True)
            for c in range(TC):
                pe_out(pe, NB - 1, c)

        def act_xpad(act, b, r):
            if r == 0:
                act.wait_ge(xt_ready, count(xt_ready, b, 1))
                act.wait_ge(z_ready, count(z_ready, b, 0))
            out = xpad[:, r, NTAP - 1:]
            nc.scalar.activation(out[:, ::-1] if r else out, wp[:, 1, :], ACT.Identity,
                                 bias=ncol[:, 1:2], scale=ncol[:, 0:1]).then_inc(xpad_done, 1)

        def act_silu_u(act, b, d, k):
            h = k ^ d
            act.wait_ge(u_ready, count(u_ready, b, 2 * d + k + 1))
            if k == 0:
                act.wait_ge(xd_ready, count(xd_ready, b, d))
                act.wait_ge(dt_done, count(dt_done, b, 2 * d))
                if d:
                    act.wait_ge(ud_done, count(ud_done, b, 2))
                elif not is_first(b):
                    act.wait_ge(ud_done, count(ud_done, b - 1, 4))
            nc.scalar.activation(u[:, h, :], wp[:, h, :], ACT.Silu, bias=col[:, d, h, 0:1]).then_inc(silu_done, 1)

        def act_silu_z(act, b, d, k):
            act.wait_ge(z_ready, count(z_ready, b, 2 * d + k + 1))
            if k == 0:
                act.wait_ge(yg_done, count(yg_done, b, d - 1))
            h = k ^ d
            nc.scalar.activation(sz[:, d, 2 * h:2 * h + 2, :], wp[:, h, :].rearrange("p (c n) -> p c n", c=2),
                                 ACT.Silu).then_inc(silu_done, 1)

        def act_xd(act, b, d, k):
            if k == 0:
                act.wait_ge(xd_ready, count(xd_ready, b, d + 1))
                act.wait_ge(b_ready, count(b_ready, b, NS * (d - 1)))
                nc.scalar.activation(st[:, d, :], wp[0:SPLIT_ROWS, d, :], ACT.Copy).then_inc(xd_done, 1)
            elif k == 1:
                act.wait_ge(c_written, count(c_written, b, 16 * d))
                act.wait_ge(dtp_ready, count(dtp_ready, b, 2 * d))
                act.wait_ge(rem_done, count(rem_done, b, d))
                nc.scalar.activation(xd[:, :], wp[:, d, :], ACT.Copy).then_inc(xd_done, 1)
            elif k == 2:
                act.wait_ge(rem_done, count(rem_done, b, d + 1))
                act.wait_ge(part_done, count(part_done, b, d))
                nc.scalar.activation(st[32:64, d, :], rem[32:64, :], ACT.Copy).then_inc(xd_done, 1)
            else:
                nc.scalar.activation(mid2[:, :], rem[0:32, :], ACT.Copy).then_inc(xd_done, 1)

        def act_soft(act, b, d, h, k):
            n = 8 * d + 4 * h
            bias = col[:, d, h, 1:2]
            if k == 0:
                act.wait_ge(dtp_ready, count(dtp_ready, b, 2 * d + h + 1))
                if h == 0:
                    act.wait_ge(dt_done, count(dt_done, b, 2 * d))
                act.wait_ge(soft_done, count(soft_done, b, n))
                nc.scalar.activation(t_abs[:, :], wp[:, 1 - (h ^ d), :], ACT.Abs, bias=bias).then_inc(soft_done, 1)
            elif k == 1:
                nc.scalar.activation(t_relu[:, h, :], wp[:, 1 - (h ^ d), :], ACT.Relu, bias=bias).then_inc(soft_done, 1)
            elif k == 2:
                act.wait_ge(soft_done, count(soft_done, b, n + 1))
                nc.scalar.activation(t_abs[:, :], t_abs[:, :], ACT.Exp, scale=-1.0).then_inc(soft_done, 1)
            else:
                act.wait_ge(soft_done, count(soft_done, b, n + 3))
                nc.scalar.activation(t_ln[:, h, :], t_abs[:, :], ACT.Ln, bias=1.0).then_inc(soft_done, 1)

        def act_ud(act, b, d, h):
            if h == 0:
                act.wait_ge(y_added, count(y_added, b, y_count(d - 1, 0)))
            nc.scalar.activation(ud[:, h, :], u[:, h, :], ACT.Copy, scale=col[:, d, h, 2:3]).then_inc(ud_done, 1)

        def act_da(act, b, d, s):
            n, h = s // 2, s % 2
            if s == 0:
                act.wait_ge(dt_done, count(dt_done, b, 2 * d + 1))
            act.wait_ge(scan_done, count(scan_done, b, STEPS * d + s + 1 - NDA))
            nc.scalar.activation(da[:, s % NDA, :], dt[:, d, h, :], ACT.Exp,
                                 scale=a_neg[:, d, h, n:n + 1]).then_inc(da_done, 1)

        def act_ygt(act, b, d, h):
            act.wait_ge(ygt_ready, count(ygt_ready, b, 2 * d + h + 1))
            if h == 0:
                act.wait_ge(out_ready, count(out_ready, b, 0))
            out = ygt[:, d, h, :]
            nc.scalar.activation(out[:, ::-1] if d else out, wp[:, h, :], ACT.Copy).then_inc(ygt_done, 1)

        def act_front(act, b, d, at, first=False):
            if at == 16 and d == 0:
                act_xpad(act, b, 0)
            if at == 17 and d == 0:
                act_xpad(act, b, 1)
            if at == 25:
                act_silu_u(act, b, d, 0)
                act_silu_u(act, b, d, 1)
                act_silu_z(act, b, d, 0)
                act_silu_z(act, b, d, 1)
                act.preload_act_table_set("natural_log_exp_and_others")
            if at in (27, 30):
                act_xd(act, b, d, 0 if at == 27 else 2)
                act_xd(act, b, d, 1 if at == 27 else 3)
            if at == STEPS - 1:
                for h in range(NH2):
                    for k in range(4):
                        act_soft(act, b, d, h, k)
                for h in range(NH2):
                    act_ud(act, b, d, h)

        def act_unit(act, b, d, front=None, tail=None):
            for s in range(STEPS):
                act_da(act, b, d, s)
                if tail and s in (14, 15):
                    act_ygt(act, *tail, s - 14)
                if front:
                    act_front(act, *front, s)

        @block.scalar
        def _(act):
            for s, per in credited["scalar"]:
                act.sem_inc(s, per)
            act.preload_act_table_set("natural_log_exp_and_others")
            act.wait_ge(weights_loaded, n_weights)
            nc.scalar.activation(a_neg[...], a_neg[...], ACT.Exp).then_inc(a_ready, 1)
            act.wait_ge(a_ready, 1)
            nc.scalar.activation(a_neg[...], a_neg[...], ACT.Copy, scale=-1.0).then_inc(a_ready, 1)
            nc.scalar.activation(sel[:, :, :], sel32, ACT.Copy).then_inc(sel_cast, 1)
            for at in range(16, STEPS):
                act_front(act, 0, 0, at)
            act.wait_ge(a_ready, 2)
            act.wait_ge(sel_cast, 1)
            act_unit(act, 0, 0, front=(0, 1))
            with act.Fori(0, NB - 1) as b:
                act_unit(act, b, 1, front=(b + 1, 0), tail=(b, 0))
                act_unit(act, b + 1, 0, front=(b + 1, 1), tail=(b, 1))
            act_unit(act, NB - 1, 1, tail=(NB - 1, 0))
            act_ygt(act, NB - 1, 1, 0)
            act_ygt(act, NB - 1, 1, 1)

        def dve_ln(dve, b, k):
            base, part = 12 * (k // 3), k % 3
            src, dst = (xin, xln) if k < 3 else (xln, xn)
            if k == 0:
                dve.wait_ge(x_loaded, count(x_loaded, b, 16))
                dve.wait_ge(ln_step, count(ln_step, b, 0))
            if k == 3:
                dve.wait_ge(ln_step, count(ln_step, b, 12))
            if part == 2:
                dve.wait_ge(rstd_done, count(rstd_done, b, 2 * (k // 3) + 2))
                if k == 2:
                    dve.wait_ge(x_kept, count(x_kept, b, 0))
                else:
                    dve.wait_ge(xt_ready, count(xt_ready, b, 0))
            for c in range(TC):
                if part == 0:
                    i = nc.vector.bn_stats(stats[:, 0, c, :], src[:, c, :])
                elif part == 1:
                    i = nc.vector.bn_aggr(mv[:, 0, c, :], stats[:, 0, c, :])
                else:
                    i = nc.vector.tensor_scalar(dst[:, c, :], src[:, c, :], mv[:, 0, c, 0:1], rstd[:, 0, 1, c:c + 1],
                                                ALU.subtract, ALU.mult)
                i.then_inc(ln_step, 1)

        def dve_ln_stats_wait(dve, b, k):
            dve.wait_ge(ln_step, count(ln_step, b, 12 * (k // 3) + 4))

        def dve_dt(dve, b, d, k):
            if k == 0:
                dve.wait_ge(soft_done, count(soft_done, b, 8 * d + 8))
                dve.wait_ge(da_done, count(da_done, b, STEPS * (d - 1)))
                nc.vector.tensor_tensor(dt[:, d], t_ln[:, :, :], t_relu[:, :, :], ALU.add).then_inc(dt_done, 1)
            else:
                dve.wait_ge(dt_done, count(dt_done, b, 2 * d + 1))
                dve.wait_ge(dbu_done, count(dbu_done, b, STEPS * (d - 1)))
                nc.vector.tensor_tensor(dtu[:, d], dt[:, d], u[:, :, :], ALU.mult).then_inc(dt_done, 1)

        def dve_dbu(dve, b, d, s):
            n, h = s // 2, s % 2
            if s == 0:
                dve.wait_ge(dt_done, count(dt_done, b, 2 * d + 2))
            if h == 0:
                dve.wait_ge(b_ready, count(b_ready, b, NS * d + n + 1))
            dve.wait_ge(scan_done, count(scan_done, b, STEPS * d + s - 1))
            nc.vector.tensor_tensor(dbu[:, s % 2, :], dtu[:, d, h, :], bp[:, n % 2, :],
                                    ALU.mult).then_inc(dbu_done, 1)

        def dve_scan(dve, b, d, s):
            dve.wait_ge(dbu_done, count(dbu_done, b, STEPS * d + s + 1))
            dve.wait_ge(da_done, count(da_done, b, STEPS * d + s + 1))
            dve.wait_ge(hc_done, count(hc_done, b, STEPS * d + s + 1 - NHB))
            nc.vector.tensor_tensor_scan(hb[:, s % NHB, :], da[:, s % NDA, :], dbu[:, s % 2, :], 0.0,
                                         ALU.mult, ALU.add).then_inc(scan_done, 1)

        def dve_yg(dve, b, d):
            dve.wait_ge(y_added, count(y_added, b, y_count(d, STEPS - 1)))
            dve.wait_ge(silu_done, count(silu_done, b, 4 * d + 4))
            dve.wait_ge(ygt_ready, count(ygt_ready, b, 2 * d))
            nc.vector.tensor_tensor(yg[:, :, :], yp[:, :, :], sz[:, d], ALU.mult).then_inc(yg_done, 1)

        def dve_end(dve, b, k):
            if k == 0:
                dve.wait_ge(out_ready, count(out_ready, b, 1))
                dve.wait_ge(x_kept, count(x_kept, b, 32))
                dve.wait_ge(end_step, count(end_step, b, 0))
                nc.vector.tensor_tensor(res[:, :, :], wp[:, 0, :].rearrange("p (c m) -> p c m", c=TC), xres[:, 1],
                                        ALU.add).then_inc(res_done, 1)
            else:
                if k == 1:
                    dve.wait_ge(res_done, count(res_done, b, 1))
                if k == 3:
                    dve.wait_ge(end_rstd, count(end_rstd, b, 2))
                    dve.wait_ge(x1_stored, count(x1_stored, b, 0))
                for c in range(TC):
                    if k == 1:
                        i = nc.vector.bn_stats(stats[:, 1, c, :], res[:, c, :])
                    elif k == 2:
                        i = nc.vector.bn_aggr(mv[:, 1, c, :], stats[:, 1, c, :])
                    else:
                        i = nc.vector.tensor_scalar(x1t[:, c, :], res[:, c, :], mv[:, 1, c, 0:1],
                                                    rstd[:, 1, 1, c:c + 1], ALU.subtract, ALU.mult)
                    i.then_inc(end_step, 1)

        def dve_unit(dve, b, d, front=None, tail=None):
            dve_dbu(dve, b, d, 0)
            dve_dbu(dve, b, d, 1)
            for s in range(STEPS):
                if front and front[1] == 0 and s in (2, 6):
                    dve_ln_stats_wait(dve, front[0], {2: 1, 6: 4}[s])
                if tail and tail[1] == 1 and s == 16:
                    dve.wait_ge(end_step, count(end_step, tail[0], 4))
                dve_scan(dve, b, d, s)
                if s % 2 == 1 and s + 1 < STEPS:
                    dve_dbu(dve, b, d, s + 1)
                    dve_dbu(dve, b, d, s + 2)
                if tail and s == LAG_Y - 1:
                    dve_yg(dve, *tail)
                if tail and tail[1] == 1 and s in (14, 15, 16, 18):
                    dve_end(dve, tail[0], {14: 0, 15: 1, 16: 2, 18: 3}[s])
                if front and front[1] == 0 and s in (1, 2, 4, 5, 6, 8):
                    dve_ln(dve, front[0], {1: 0, 2: 1, 4: 2, 5: 3, 6: 4, 8: 5}[s])
                if front and s in (29, 30):
                    dve_dt(dve, *front, s - 29)

        @block.vector
        def _(dve):
            for s, per in credited["vector"]:
                dve.sem_inc(s, per)
            for k in range(6):
                if k % 3 == 1:
                    dve_ln_stats_wait(dve, 0, k)
                dve_ln(dve, 0, k)
            dve.wait_ge(weights_loaded, n_weights)
            for d in range(NDIR):
                nc.vector.tensor_tensor(wu[:, d], win_u[:, d:d + 1, :].to_broadcast([P, NTAP, DI]), wu[:, d],
                                        ALU.mult).then_inc(taps_folded, 1)
            dve_dt(dve, 0, 0, 0)
            dve_dt(dve, 0, 0, 1)
            dve_unit(dve, 0, 0, front=(0, 1))
            with dve.Fori(0, NB - 1) as b:
                dve_unit(dve, b, 1, front=(b + 1, 0), tail=(b, 0))
                dve_unit(dve, b + 1, 0, front=(b + 1, 1), tail=(b, 1))
            dve_unit(dve, NB - 1, 1, tail=(NB - 1, 0))
            dve_yg(dve, NB - 1, 1)
            for k in range(4):
                if k == 2:
                    dve.wait_ge(end_step, count(end_step, NB - 1, 4))
                dve_end(dve, NB - 1, k)

        def pool_rstd(pool, b, k, done, steps, after):
            pool.wait_ge(steps, count(steps, b, after))
            side = 0 if done is rstd_done else 1
            nc.gpsimd.tensor_tensor(rstd[:, side, 0, :], mv[:, side, :, 1], eps[:, :], ALU.add).then_inc(done, 1)
            pool.wait_ge(done, count(done, b, 2 * k + 1))
            nc.gpsimd.tensor_tensor(rstd[:, side, 1, :], rstd[:, side, 0, :], mhalf[:, :], ALU.pow).then_inc(done, 1)

        def pool_rem(pool, b, d):
            pool.wait_ge(xd_done, count(xd_done, b, 4 * d + 2))
            pool.wait_ge(part_done, count(part_done, b, d))
            nc.gpsimd.tensor_tensor(rem[:, :], xd[0:SPLIT_ROWS, :], st[:, d, :],
                                    ALU.subtract).then_inc(rem_done, 1)

        def pool_part(pool, b, d):
            pool.wait_ge(xd_done, count(xd_done, b, 4 * d + 4))
            nc.gpsimd.tensor_tensor(st[0:32, d, :], rem[0:32, :], mid2[:, :], ALU.subtract).then_inc(part_done, 1)

        def pool_x1(pool, b):
            pool.wait_ge(end_step, count(end_step, b, 12))
            nc.gpsimd.tensor_tensor(x1t[:, :, :], x1t[:, :, :], xres[:, 0], ALU.add).then_inc(x1_done, 1)

        def pool_hc(pool, b, d, s):
            if s == 0:
                pool.wait_ge(c_first, count(c_first, b, 16 * d + 16))
            if s == NH2 * C_FIRST:
                pool.wait_ge(c_rest, count(c_rest, b, 16 * d + 16))
            pool.wait_ge(scan_done, count(scan_done, b, STEPS * d + s + 1))
            pool.wait_ge(y_added, count(y_added, b, y_count(d, s - NHC)))
            nc.gpsimd.tensor_tensor(hc[:, s % NHC, :], hb[:, s % NHB, :], cb[:, d, s // 2, :],
                                    ALU.mult).then_inc(hc_done, 1)

        def pool_unit(pool, b, d, front=None, tail=None):
            for s in range(STEPS):
                if front and front[1] == 0 and s == 3:
                    pool_rstd(pool, front[0], 0, rstd_done, ln_step, 8)
                if front and front[1] == 0 and s == 7:
                    pool_rstd(pool, front[0], 1, rstd_done, ln_step, 20)
                if tail and tail[1] == 1 and s == 16:
                    pool_rstd(pool, tail[0], 0, end_rstd, end_step, 8)
                if tail and tail[1] == 1 and s == 18:
                    pool_x1(pool, tail[0])
                if front and s == 23:
                    pool_rem(pool, *front)
                if front and s == 26:
                    pool_part(pool, *front)
                pool_hc(pool, b, d, s)

        @block.gpsimd
        def _(pool):
            for s, per in credited["gpsimd"]:
                pool.sem_inc(s, per)
            nc.gpsimd.memset(mhalf[:, :], -0.5).then_inc(consts_set, 1)
            nc.gpsimd.memset(eps[:, :], EPS).then_inc(consts_set, 1)
            nc.gpsimd.memset(xpad[:, :, 0:NTAP - 1], 0.0).then_inc(consts_set, 1)
            pool.wait_ge(consts_set, 3)
            pool_rstd(pool, 0, 0, rstd_done, ln_step, 8)
            pool_rstd(pool, 0, 1, rstd_done, ln_step, 20)
            pool_rem(pool, 0, 0)
            pool_part(pool, 0, 0)
            pool_unit(pool, 0, 0, front=(0, 1))
            with pool.Fori(0, NB - 1) as b:
                pool_unit(pool, b, 1, front=(b + 1, 0), tail=(b, 0))
                pool_unit(pool, b + 1, 0, front=(b + 1, 1), tail=(b, 1))
            pool_unit(pool, NB - 1, 1, tail=(NB - 1, 0))
            pool_rstd(pool, NB - 1, 0, end_rstd, end_step, 8)
            pool_x1(pool, NB - 1)


NHEAD, NKV, HD = 16, 4, 8
GH = NHEAD // NKV
NE, FF = 8, 256
NF = FF // P
PART_ROWS = 9 * HD
QK_ROWS = PART_ROWS + 3
SCALE = HD ** -0.5
PAIRS = NHEAD // 2
PAIR_TILES = (((0, 0, 0),), ((0, 1, 0), (0, 3, 384)), ((0, 2, 0), (1, 2, 256)), ((1, 0, 0),), ((1, 1, 0), (1, 3, 384)))
NPT = len(PAIR_TILES)
ST_TILES = PAIRS * NPT
GROUP_TILES = ST_TILES // NKV
LAG = 4
LIFT = 3.9
MAX_TILES = [(c, h, n) for g in range(NKV) for c, n in ((0, 4), (1, 2), (2, 1), (3, 1))
             for h in range(GH * g, GH * (g + 1), n)]
MT = len(MAX_TILES)
SLOTS = 5 * NE
EARLY_SLOTS = 7
MAIN_END = 24
MAIN_SLOTS = {2 * (k - EARLY_SLOTS) + 4: k for k in range(EARLY_SLOTS, MAIN_END)}
TURN_SLOTS = {(k - MAIN_END) * 34 // (SLOTS - MAIN_END): k for k in range(MAIN_END, SLOTS)}


def ffn_phase(nc, sems, x1, out, qscr, kscr, w):
    with ExitStack() as ctx:
        def sb(name, shape, dt=F32):
            return ctx.enter_context(nc.sbuf_tensor(name, shape, dt))

        def pb(name, shape):
            return ctx.enter_context(nc.psum_tensor(name, shape, F32))

        count = Counts()
        credited = {e: [] for e in ("sync", "tensor", "scalar", "vector", "gpsimd")}

        def sig(name, per, producer=None):
            s = sems.enter_context(nc.semaphore(name))
            count.add(s, per, producer is not None)
            if producer is not None:
                credited[producer].append((s, per))
            return s

        ident = sb("ident2", [P, P])
        identb = sb("identb", [P, P], BF16)
        mask32 = sb("mask32", [P, 2, P])
        mask = sb("mask", [P, 2, P], BF16)
        trig = sb("trig", [P, 2, SEQ])
        wq = sb("wq", [P, 2, P])
        wk = sb("wk", [P, 2 * NKV * HD])
        wv = sb("wv", [P, NKV * HD])
        wo = sb("wo", [P, DM])
        gate = sb("gate", [P, NE])
        w13 = sb("w13", [P, NE, 2 * FF])
        w2 = sb("w2", [P, NE, NF, DM])
        lnw = sb("lnw", [P, 2])
        tri = sb("tri", [P, NE, NE])
        sel32 = sb("sel32e", [SPLIT_ROWS, NE, P])
        sel = sb("sel_e", [SPLIT_ROWS, NE, P], BF16)
        mhalf = sb("mhalf2", [P, TC])
        lift = sb("lift", [P, 1])
        eps = sb("eps2", [P, TC])
        xa = sb("xa", [P, TC, DM])
        h0 = sb("h0", [P, TC, DM])
        hres = sb("hres", [P, TC, DM])
        hn = sb("hn", [P, TC, DM])
        stats = sb("stats2", [P, 3, TC, 6])
        mv = sb("mv2", [P, 3, TC, 2])
        rt = sb("rt", [P, 3, 4, TC])
        ht = sb("ht", [P, SEQ])
        rot = sb("rot", [P, 2, SEQ])
        qf = sb("qf", [P, SEQ])
        rotk = sb("rotk", [NKV * HD, 2, SEQ])
        kf = sb("kf", [NKV * HD, SEQ])
        qp = sb("qp", [P, 3, SEQ], BF16)
        kp = sb("kp", [NKV * HD, 3, SEQ], BF16)
        vst = sb("vst", [P, TC, NKV, HD])
        vr = sb("vr", [P, TC, NKV, HD])
        vb = sb("vb", [P, 3, TC, NKV, HD], BF16)
        vpad = sb("vpad", [P, TC, NHEAD, P], BF16)
        q9 = sb("q9", [QK_ROWS, NHEAD, SEQ], BF16)
        k9 = sb("k9", [QK_ROWS, NKV, SEQ], BF16)
        mx = sb("mx", [P, TC, NHEAD])
        nm = sb("nm", [NHEAD, 3, SEQ], BF16)
        nmr = sb("nmr", [NHEAD, SEQ])
        NPR = 6
        pt = sb("pt", [P, NPR, SEQ])
        pp = sb("pp", [P, NPR, 2, SEQ], F16)
        osum = sb("osum", [P, SEQ])
        den = sb("den", [P, SEQ])
        rec = sb("rec", [P, SEQ])
        ot = sb("ot", [P, SEQ])
        x2 = sb("x2", [P, TC, DM])
        h2n = sb("h2n", [P, TC, DM])
        h2tn = sb("h2tn", [P, SEQ])
        lg = sb("lg", [P, TC, NE])
        lmax = sb("lmax", [P, TC])
        ex = sb("ex", [P, TC, NE])
        gtm = sb("gtm", [P, TC, NE, NE])
        eqm = sb("eqm", [P, TC, NE, NE])
        rank = sb("rank", [P, TC, NE])
        wsum = sb("wsum", [P, 2, TC])
        wrep = sb("wrep", [P, TC, 3, 32])
        wstn = sb("wstn", [SPLIT_ROWS, SEQ], BF16)
        wrem = sb("wrem", [SPLIT_ROWS, SEQ])
        wmid = sb("wmid", [SPLIT_ROWS, SEQ], BF16)
        h2t = sb("h2t", [P, SEQ])
        wst = sb("wst", [SPLIT_ROWS, SEQ], BF16)
        x2e = sb("x2e", [P, TC, DM])
        h2e = sb("h2e", [P, 2, SEQ])
        th = sb("th", [P, 2, SEQ])
        ga = sb("ga", [P, 2, SEQ])
        g = sb("g", [P, 2, SEQ])
        ots = sb("ots", [P, SEQ])
        ye = sb("ye", [P, TC, DM])
        xr = sb("xr", [P, TC, DM])
        yo = sb("yo", [P, TC, DM])
        sp_ = pb("scores", [P, 2, SEQ])
        og = pb("og", [P, SEQ])
        pa = pb("pa", [P, SEQ])
        pbk = pb("pbk", [P, SEQ])
        po = pb("po", [P, SEQ])
        m0 = pb("m0", [P, SEQ])
        m1 = pb("m1", [P, SEQ])

        rest_loaded = sems.enter_context(nc.semaphore("weights2_rest_loaded"))
        loaded = sems.enter_context(nc.semaphore("weights2_loaded"))
        consts = sems.enter_context(nc.semaphore("consts2_set"))
        casts = sems.enter_context(nc.semaphore("casts2_done"))

        xa_loaded = sig("xa_loaded", 16)
        qk_written = sig("qk_written", 96, "sync")
        qk_loaded = sig("qk_loaded", 64, "sync")
        qk_last = sig("qk_last", 64, "sync")
        m_loaded = sig("m_loaded", 48, "sync")
        xr_loaded = sig("xr_loaded", 16)
        out_stored = sig("out_stored", 16, "sync")

        ht_ready = sig("ht_ready", 1, "tensor")
        proj_ready = sig("proj_ready", 4, "tensor")
        max_ready = sig("max_ready", MT, "tensor")
        nm_ready = sig("nm_ready", 1)
        st_ready = sig("st_ready", ST_TILES, "tensor")
        pv_done = sig("pv_done", ST_TILES, "tensor")
        wo_ready = sig("wo_ready", 1, "tensor")
        x2t_ready = sig("x2t_ready", 1, "tensor")
        gate_ready = sig("gate_ready", 1)
        wt_ready = sig("wt_ready", 1, "tensor")
        wbc_ready = sig("wbc_ready", NE, "tensor")
        a_ready = sig("a_ready2", NE * NF, "tensor")
        b_ready = sig("b_ready2", NE * NF, "tensor")
        down_done = sig("down_done", NE * NF, "tensor")
        ot_ready = sig("ot_ready", 1, "tensor")

        ht_done = sig("ht_done", 1)
        part_act = sig("part_act", 4, "scalar")
        v_done = sig("v_done", 3, "scalar")
        exp_done = sig("exp_done", ST_TILES, "scalar")
        den_done = sig("den_done", 2 * NKV, "scalar")
        moe_in = sig("moe_in", 3, "scalar")
        nm_act = sig("nm_act", 2, "scalar")
        th_done = sig("th_done", NE * NF, "scalar")
        h2t_done = sig("h2t_done", 1, "scalar")
        ex_done = sig("ex_done", 1)
        wpart_act = sig("wpart_act", 3, "scalar")
        ots_done = sig("ots_done", 1, "scalar")

        in_step = sig("in_step", 24, "vector")
        rope_mul = sig("rope_mul", 4, "vector")
        max_done = sig("max_done", MT, "vector")
        nm_rem = sig("nm_rem", 2, "vector")
        og_add = sig("og_add", 2 * NKV, "vector")
        og_fin = sig("og_fin", 2 * TC, "vector")
        x2_done = sig("x2_done", 1, "vector")
        post_step = sig("post_step", 8, "vector")
        gate_step = sig("gate_step", 12, "vector")
        wpart_dve = sig("wpart_dve", 2, "vector")
        h2e_done = sig("h2e_done", NE, "vector")
        ga_done = sig("ga_done", NE * NF, "vector")
        g_done = sig("g_done", NE * NF, "vector")
        ye_done = sig("ye_done", 1, "vector")
        end_step = sig("end_step2", 8, "vector")
        out_done = sig("out_done", 3, "gpsimd")

        in_rstd = sig("in_rstd", 6, "gpsimd")
        post_rstd = sig("post_rstd", 4, "gpsimd")
        h2n_done = sig("h2n_done", 1, "gpsimd")
        end_rstd = sig("end_rstd2", 2, "gpsimd")
        rope_add = sig("rope_add", 2, "gpsimd")
        part_pool = sig("part_pool", 4, "gpsimd")
        kept = sig("kept", 1, "scalar")
        vpad_done = sig("vpad_done", 3, "scalar")
        v_rest = sig("v_rest", 2, "gpsimd")
        split_done = sig("split_done", ST_TILES, "gpsimd")

        block = ctx.enter_context(nc.Block())
        first_weights = ((ident, "ident"), (lnw, "lnw"), (wq, "wq"), (wk, "wk"), (trig, "trig"), (wv, "wv"),
                         (mask32, "mask"))
        rest_weights = ((wo, "wo"), (gate, "gate"), (tri, "tri"), (sel32, "sel_e"), (w13, "w13"), (w2, "w2"))
        n_first, n_rest = 16 * len(first_weights), 16 * len(rest_weights)

        def rows(t, b):
            return t[bass.ds(b, 1)].rearrange("a (c p) m -> p a c m", p=P)

        def flat(t):
            return t[:, :, :].rearrange("p (a c) m -> p a c m", a=1)

        def sp_xa(sp, b, first=False):
            if not first:
                sp.wait_ge(in_step, count(in_step, b, -12))
            sp.dma_start(flat(xa), rows(x1, b)).then_inc(xa_loaded, 16)

        def sp_xr(sp, b):
            sp.wait_ge(out_done, count(out_done, b, 0))
            sp.dma_start(flat(xr), rows(x1, b)).then_inc(xr_loaded, 16)

        def sp_parts_out(sp, b):
            sp.wait_ge(part_act, count(part_act, b, 4))
            sp.wait_ge(part_pool, count(part_pool, b, 4))
            sp.wait_ge(qk_loaded, count(qk_loaded, b, 0))
            sp.wait_ge(qk_last, count(qk_last, b, 0))
            for a in range(3):
                sp.dma_start(qscr[a].rearrange("d h s -> h d s"), qp[:, a, :]).then_inc(qk_written, 16)
                sp.dma_start(kscr[a].rearrange("d h s -> h d s"), kp[:, a, :]).then_inc(qk_written, 16)

        def sp_parts_in(sp, b):
            sp.wait_ge(qk_written, count(qk_written, b, 96))
            for g0, g1, done in ((0, NKV - 1, qk_loaded), (NKV - 1, NKV, qk_last)):
                sp.wait_ge(st_ready, count(st_ready, b, GROUP_TILES * g1 - ST_TILES))
                h0_, h1 = GH * g0, GH * g1
                for a in range(3):
                    sp.dma_start(q9[a * 3 * HD:(a + 1) * 3 * HD, h0_:h1].rearrange("r h s -> r (h s)"),
                                 qscr[a:a + 1, :, h0_:h1].rearrange("a d h s -> a d (h s)")
                                 .to_broadcast([3, HD, (h1 - h0_) * SEQ])).then_inc(done, 16)
                sp.dma_start(k9[0:PART_ROWS, g0:g1].rearrange("r h s -> r (h s)"),
                             kscr[:, :, g0:g1].rearrange("b d h s -> b d (h s)").rearrange("b d n -> (b d) n")
                             .unsqueeze(0).to_broadcast([3, 3 * HD, (g1 - g0) * SEQ])).then_inc(done, 16)

        def sp_max(sp, b):
            scores_before = count.in_register(sp, st_ready, b, 0)
            part0, part1 = count.in_register(sp, nm_act, b, 1), count.in_register(sp, nm_act, b, 2)
            part2 = count.in_register(sp, nm_rem, b, 2)

            def row(a):
                return q9[PART_ROWS + a:PART_ROWS + a + 1].rearrange("r h s -> r (h s)")

            sp.wait_ge(st_ready, scores_before)
            sp.wait_ge(nm_act, part0)
            sp.dma_start(row(0), nm[:, 0, :]).then_inc(m_loaded, 16)
            sp.wait_ge(nm_act, part1)
            sp.dma_start(row(1), nm[:, 1, :]).then_inc(m_loaded, 16)
            sp.wait_ge(nm_rem, part2)
            sp.dma_start(row(2), nm[:, 2, :]).then_inc(m_loaded, 16)

        def sp_out(sp, b):
            sp.wait_ge(out_done, count(out_done, b, 3))
            sp.dma_start(rows(out, b), flat(yo)).then_inc(out_stored, 16)

        @block.sync
        def _(sp):
            for s, per in credited["sync"]:
                sp.sem_inc(s, per)
            sp_xa(sp, 0, first=True)
            for dst, name in first_weights:
                sp.dma_start(dst[...], w[name]).then_inc(loaded, 16)
            for dst, name in rest_weights:
                sp.dma_start(dst[...], w[name]).then_inc(rest_loaded, 16)
            sp_parts_out(sp, 0)
            sp.wait_ge(consts, 4)
            sp_parts_in(sp, 0)
            sp_max(sp, 0)
            sp_xa(sp, 1)
            sp_parts_out(sp, 1)
            sp_parts_in(sp, 1)
            sp_max(sp, 1)
            with sp.Fori(1, NB - 1) as b:
                sp_xa(sp, b + 1)
                sp_xr(sp, b - 1)
                sp_parts_out(sp, b + 1)
                sp_parts_in(sp, b + 1)
                sp_out(sp, b - 1)
                sp_max(sp, b + 1)
            sp_xr(sp, NB - 2)
            sp_out(sp, NB - 2)
            sp_xr(sp, NB - 1)
            sp_out(sp, NB - 1)
            sp.wait_ge(out_stored, count(out_stored, NB - 1, 16))

        def pe_ht(pe, b):
            pe.wait_ge(in_step, count(in_step, b, 24))
            if not is_first(b):
                pe.wait_ge(wpart_act, count(wpart_act, b - 1, 0))
                pe.wait_ge(wpart_dve, count(wpart_dve, b - 1, 0))
            for c in range(TC):
                last = nc.tensor.transpose(m0[:, c * P:(c + 1) * P], hn[:, c, :], ident[:, :])
            last.then_inc(ht_ready, 1)

        def pe_proj(pe, b, k):
            if k == 0:
                pe.wait_ge(ht_done, count(ht_done, b, 1))
                nc.tensor.matmul(m0[:, :], wq[:, 0, :], ht[:, :], start=True, stop=True).then_inc(proj_ready, 1)
            elif k == 1:
                pe.wait_ge(rope_mul, count(rope_mul, b, 1))
                nc.tensor.matmul(m0[:, :], wq[:, 1, :], ht[:, :], start=True, stop=True).then_inc(proj_ready, 1)
            elif k == 2:
                pe.wait_ge(rope_mul, count(rope_mul, b, 2))
                nc.tensor.matmul(m0[0:64, :], wk[:, :], ht[:, :], start=True, stop=True).then_inc(proj_ready, 1)
            else:
                pe.wait_ge(rope_mul, count(rope_mul, b, 4))
                for c in range(TC):
                    last = nc.tensor.matmul(m0[:, c * 32:(c + 1) * 32], ht[:, c * P:(c + 1) * P], wv[:, :],
                                            start=True, stop=True)
                last.then_inc(proj_ready, 1)

        def pe_max(pe, b, t):
            c, h0_, n = MAX_TILES[t]
            if t == 0:
                pe.wait_ge(qk_loaded, count(qk_loaded, b, 64))
                pe.wait_ge(exp_done, count(exp_done, b, 0))
            if t == MT // NKV * (NKV - 1):
                pe.wait_ge(qk_last, count(qk_last, b, 64))
            if t >= 2:
                pe.wait_ge(max_done, count(max_done, b, t - 1))
            width = (c + 1) * P
            for i in range(n):
                at = i * width
                nc.tensor.matmul(sp_[:, t % 2, at + c * P:at + width], identb[:, :], mask[:, 0, :],
                                 start=(i == 0), stop=False, skip_group_check=True)
                last = nc.tensor.matmul(sp_[:, t % 2, at:at + width],
                                        q9[0:PART_ROWS, h0_ + i, c * P:(c + 1) * P],
                                        k9[0:PART_ROWS, (h0_ + i) // 4, 0:width],
                                        start=False, stop=True, skip_group_check=True)
            last.then_inc(max_ready, 1)

        def pe_nm(pe, b):
            pe.wait_ge(max_done, count(max_done, b, MT))
            pe.wait_ge(og_add, count(og_add, b, 0))
            pe.wait_ge(den_done, count(den_done, b, 0))
            for c in range(TC):
                last = nc.tensor.transpose(og[0:NHEAD, c * P:(c + 1) * P], mx[:, c, :], ident[:, :])
            last.then_inc(nm_ready, 1)

        def pieces(t):
            i, j = t // NPT, t % NPT
            return [(2 * i + hh, kc, at) for hh, kc, at in PAIR_TILES[j]]

        def pe_st(pe, b, t):
            if t == 0:
                pe.wait_ge(m_loaded, count(m_loaded, b, 48))
                pe.wait_ge(max_done, count(max_done, b, MT))
            if t >= 2:
                pe.wait_ge(exp_done, count(exp_done, b, t - 1))
            for i, (h, kc, at) in enumerate(pieces(t)):
                nc.tensor.matmul(sp_[:, t % 2, at:at + P], identb[:, :], mask[:, 1, :],
                                 start=(i == 0), stop=False, skip_group_check=True)
                last = nc.tensor.matmul(sp_[:, t % 2, at:at + SEQ - kc * P],
                                        k9[:, h // 4, kc * P:(kc + 1) * P], q9[:, h, kc * P:],
                                        start=False, stop=True, skip_group_check=True)
            last.then_inc(st_ready, 1)

        def pe_pv(pe, b, t):
            pe.wait_ge(split_done, count(split_done, b, t + 1))
            if t == 0:
                pe.wait_ge(vpad_done, count(vpad_done, b, 3))
            if t % GROUP_TILES == 0:
                group = t // GROUP_TILES
                pe.wait_ge(og_add, count(og_add, b, 2 * group))
                pe.wait_ge(den_done, count(den_done, b, 2 * group))
            ps = pieces(t)
            for i, (h, kc, at) in enumerate(ps):
                for part in range(2):
                    first = t % GROUP_TILES == 0 and part == 0
                    final = t % GROUP_TILES == GROUP_TILES - 1 and i == len(ps) - 1 and part == 1
                    last = nc.tensor.matmul(og[:, kc * P:], vpad[:, kc, h, :],
                                            pp[:, t % NPR, part, at:at + SEQ - kc * P],
                                            start=first, stop=final, skip_group_check=True)
            last.then_inc(pv_done, 1)

        def pe_wo(pe, b, final=False):
            pe.wait_ge(og_fin, count(og_fin, b, 2 * TC))
            if final:
                pe.wait_ge(wpart_act, count(wpart_act, b, 0))
                pe.wait_ge(wpart_dve, count(wpart_dve, b, 0))
            else:
                pe.wait_ge(v_done, count(v_done, b + 1, 2))
            for c in range(TC):
                last = nc.tensor.matmul(m0[:, c * P:(c + 1) * P], ot[:, c * P:(c + 1) * P], wo[:, :],
                                        start=True, stop=True)
            last.then_inc(wo_ready, 1)

        def pe_x2t(pe, b):
            pe.wait_ge(h2n_done, count(h2n_done, b, 1))
            pe.wait_ge(x2_done, count(x2_done, b, 1))
            for c in range(TC):
                last = nc.tensor.transpose(m0[:, c * P:(c + 1) * P], h2n[:, c, :], ident[:, :])
            last.then_inc(x2t_ready, 1)

        def pe_gate(pe, b):
            pe.wait_ge(h2t_done, count(h2t_done, b, 1))
            for c in range(TC):
                last = nc.tensor.matmul(m0[:, c * NE:(c + 1) * NE], h2tn[:, c * P:(c + 1) * P], gate[:, :],
                                        start=True, stop=True)
            last.then_inc(gate_ready, 1)

        def pe_wt(pe, b):
            pe.wait_ge(gate_step, count(gate_step, b, 12))
            for c in range(TC):
                last = nc.tensor.transpose(m0[0:SPLIT_ROWS, c * P:(c + 1) * P],
                                           wrep[:, c, :, :].rearrange("p a b -> p (a b)"), ident[:, :])
            last.then_inc(wt_ready, 1)

        def pe_wbc(pe, b, e):
            if e == 0:
                pe.wait_ge(moe_in, count(moe_in, b, 2))
                pe.wait_ge(ye_done, count(ye_done, b, 0))
            else:
                pe.wait_ge(h2e_done, count(h2e_done, b, e))
            nc.tensor.matmul(m1[:, :], sel[:, e, :], wst[:, :], start=True, stop=True).then_inc(wbc_ready, 1)

        def pe_a(pe, b, e, f):
            n = NF * e + f
            pe.wait_ge(ga_done, count(ga_done, b, n))
            if n == 0:
                pe.wait_ge(moe_in, count(moe_in, b, 1))
            nc.tensor.matmul(pa[:, :], w13[:, e, f * P:(f + 1) * P], h2t[:, :],
                             start=True, stop=True).then_inc(a_ready, 1)

        def pe_bm(pe, b, e, f):
            pe.wait_ge(g_done, count(g_done, b, NF * e + f))
            pe.wait_ge(h2e_done, count(h2e_done, b, e + 1))
            nc.tensor.matmul(pbk[:, :], w13[:, e, FF + f * P:FF + (f + 1) * P], h2e[:, e % 2, :],
                             start=True, stop=True).then_inc(b_ready, 1)

        def pe_down(pe, b, n):
            pe.wait_ge(g_done, count(g_done, b, n + 1))
            if n == 0:
                pe.wait_ge(ots_done, count(ots_done, b, 0))
            nc.tensor.matmul(po[:, :], w2[:, n // NF, n % NF, :], g[:, n % 2, :], start=(n == 0),
                             stop=(n == NE * NF - 1), skip_group_check=True).then_inc(down_done, 1)

        def pe_ot(pe, b):
            pe.wait_ge(ots_done, count(ots_done, b, 1))
            pe.wait_ge(h2e_done, count(h2e_done, b, NE))
            for c in range(TC):
                last = nc.tensor.transpose(m1[:, c * P:(c + 1) * P], ots[:, c * P:(c + 1) * P], ident[:, :])
            last.then_inc(ot_ready, 1)

        def pe_moe(pe, b, slot):
            i, j = slot // 5, slot % 5
            if j == 0:
                pe_a(pe, b, i, 0)
                if i == 0:
                    pe_wbc(pe, b, 0)
            if j == 1:
                pe_bm(pe, b, i, 0)
                if i > 0:
                    pe_down(pe, b, 2 * i - 1)
            if j == 2:
                if i + 1 < NE:
                    pe_wbc(pe, b, i + 1)
                pe_a(pe, b, i, 1)
            if j == 3:
                pe_bm(pe, b, i, 1)
            if j == 4:
                pe_down(pe, b, 2 * i)

        def pe_main(pe, att=None, moe=None, front=None):
            if moe is not None:
                for slot in range(EARLY_SLOTS):
                    pe_moe(pe, moe, slot)
            for t in range(ST_TILES):
                if att is not None:
                    pe_st(pe, att, t)
                if moe is not None and t in MAIN_SLOTS:
                    pe_moe(pe, moe, MAIN_SLOTS[t])
                if front is not None:
                    if t == 9:
                        pe_ht(pe, front)
                    if t in (12, 14, 16, 19):
                        pe_proj(pe, front, (12, 14, 16, 19).index(t))
                if att is not None and t >= LAG and (t - LAG) % GROUP_TILES != 0:
                    if (t - LAG) % GROUP_TILES == 1:
                        pe_pv(pe, att, t - LAG - 1)
                    pe_pv(pe, att, t - LAG)
            if att is not None:
                for t in range(ST_TILES - LAG, ST_TILES):
                    pe_pv(pe, att, t)

        def pe_turn(pe, post=None, end=None, top=None):
            for t in range(MT):
                if top is not None:
                    pe_max(pe, top, t)
                if end is not None:
                    if t in TURN_SLOTS:
                        pe_moe(pe, end, TURN_SLOTS[t])
                    if t == 34:
                        pe_down(pe, end, NE * NF - 1)
                    if t == 37:
                        pe_ot(pe, end)
                if post is not None:
                    if t == 7:
                        pe_wo(pe, post, final=top is None)
                    if t == 16:
                        pe_x2t(pe, post)
                    if t == 18:
                        pe_gate(pe, post)
                    if t == 35:
                        pe_wt(pe, post)
            if top is not None:
                pe_nm(pe, top)

        @block.tensor
        def _(pe):
            for s, per in credited["tensor"]:
                pe.sem_inc(s, per)
            pe.wait_ge(loaded, n_first)
            pe_ht(pe, 0)
            for k in range(4):
                pe_proj(pe, 0, k)
            pe.wait_ge(casts, 2)
            pe_turn(pe, top=0)
            pe_main(pe, att=0, front=1)
            pe.wait_ge(rest_loaded, n_rest)
            pe.wait_ge(casts, 3)
            pe_turn(pe, post=0, top=1)
            with pe.Fori(1, NB - 1) as b:
                pe_main(pe, att=b, moe=b - 1, front=b + 1)
                pe_turn(pe, post=b, end=b - 1, top=b + 1)
            pe_main(pe, att=NB - 1, moe=NB - 2)
            pe_turn(pe, post=NB - 1, end=NB - 2)
            pe_main(pe, moe=NB - 1)
            pe_turn(pe, end=NB - 1)

        def vpad_diag(column):
            a = vpad[:, :, :, column:column + HD].rearrange("p c (g r) d -> p (c g) r d", r=GH)
            ap = [list(x) for x in a.ap]
            ap[2][0] = P + HD
            return bass.AP(tensor=a.tensor, offset=a.offset, ap=ap)

        def act_keep(act, b):
            act.wait_ge(in_step, count(in_step, b, 24))
            act.wait_ge(x2_done, count(x2_done, b, 0))
            nc.scalar.activation(hres[:, :, :], h0[:, :, :], ACT.Copy).then_inc(kept, 1)

        def act_vpad(act, b):
            act.wait_ge(v_done, count(v_done, b, 1))
            act.wait_ge(pv_done, count(pv_done, b, 0))
            act.wait_ge(v_rest, count(v_rest, b, 2))
            for part in range(3):
                v_all = vb[:, part].rearrange("p c g d -> p (c g) d").unsqueeze(2).to_broadcast([P, TC * NKV, GH, HD])
                nc.scalar.activation(vpad_diag(32 * part), v_all, ACT.Copy).then_inc(vpad_done, 1)

        def act_den(act, b, group):
            act.wait_ge(pv_done, count(pv_done, b, GROUP_TILES * (group + 1)))
            act.wait_ge(og_fin, count(og_fin, b, 0))
            rows32 = slice(32 * group, 32 * group + 32)
            nc.scalar.activation(osum[rows32, :], og[64:96, :], ACT.Copy).then_inc(den_done, 1)
            nc.scalar.activation(den[rows32, :], og[96:128, :], ACT.Copy).then_inc(den_done, 1)

        def act_moe_in(act, b, k):
            if k == 0:
                act.wait_ge(h2t_done, count(h2t_done, b, 1))
                act.wait_ge(a_ready, count(a_ready, b, 0))
                act.wait_ge(h2e_done, count(h2e_done, b, 0))
                nc.scalar.activation(h2t[:, :], h2tn[:, :], ACT.Copy).then_inc(moe_in, 1)
            elif k == 1:
                act.wait_ge(wpart_act, count(wpart_act, b, 3))
                act.wait_ge(wpart_dve, count(wpart_dve, b, 2))
                act.wait_ge(wbc_ready, count(wbc_ready, b, 0))
                nc.scalar.activation(wst[:, :], wstn[:, :], ACT.Copy).then_inc(moe_in, 1)
            else:
                act.wait_ge(x2_done, count(x2_done, b, 1))
                act.wait_ge(ye_done, count(ye_done, b, 0))
                nc.scalar.activation(x2e[:, :, :], x2[:, :, :], ACT.Copy).then_inc(moe_in, 1)

        def act_ht(act, b):
            act.wait_ge(ht_ready, count(ht_ready, b, 1))
            act.wait_ge(proj_ready, count(proj_ready, b, 0))
            nc.scalar.activation(ht[:, :], m0[:, :], ACT.Copy, scale=lnw[:, 0:1]).then_inc(ht_done, 1)

        def act_v(act, b, k):
            if k == 0:
                act.wait_ge(proj_ready, count(proj_ready, b, 4))
                act.wait_ge(vpad_done, count(vpad_done, b, 0))
                act.wait_ge(v_rest, count(v_rest, b, 0))
                v_in = m0[:, 0:TC * NKV * HD]
                nc.scalar.activation(vst[:, :, :, :].rearrange("p c h d -> p (c h d)"), v_in,
                                     ACT.Copy).then_inc(v_done, 1)
                nc.scalar.activation(vb[:, 0].rearrange("p c h d -> p (c h d)"), v_in,
                                     ACT.Copy).then_inc(v_done, 1)
            else:
                act.wait_ge(v_rest, count(v_rest, b, 1))
                nc.scalar.activation(vb[:, 1], vr[:, :, :, :], ACT.Copy).then_inc(v_done, 1)

        def act_part(act, b, k):
            src, first, rem = ((qf, qp, rot), (kf, kp, rotk))[k // 2]
            if k % 2 == 0:
                act.wait_ge(rope_add, count(rope_add, b, k // 2 + 1))
                act.wait_ge(qk_written, count(qk_written, b, 0))
                act.wait_ge(part_pool, count(part_pool, b, 0))
                nc.scalar.activation(first[:, 0, :], src[:, :], ACT.Copy).then_inc(part_act, 1)
            else:
                act.wait_ge(part_pool, count(part_pool, b, k // 2 + 1))
                nc.scalar.activation(first[:, 1, :], rem[:, 0, :], ACT.Copy).then_inc(part_act, 1)

        def act_exp(act, b, t):
            act.wait_ge(st_ready, count(st_ready, b, t + 1))
            act.wait_ge(pv_done, count(pv_done, b, t + 1 - NPR))
            width = sum(SEQ - kc * P for _, kc, _ in pieces(t))
            scores_in = sp_[:, t % 2, 0:width]
            nc.scalar.activation(pp[:, t % NPR, 0, 0:width], scores_in, ACT.Exp, bias=lift[:, :], scale=SCALE)
            nc.scalar.activation(pt[:, t % NPR, 0:width], scores_in, ACT.Exp, bias=lift[:, :],
                                 scale=SCALE).then_inc(exp_done, 1)

        def act_nm(act, b, k):
            if k == 0:
                act.wait_ge(nm_ready, count(nm_ready, b, 1))
                act.wait_ge(m_loaded, count(m_loaded, b, 0))
                nc.scalar.activation(nm[:, 0, :], og[0:NHEAD, :], ACT.Copy, scale=-1.0).then_inc(nm_act, 1)
            else:
                act.wait_ge(nm_rem, count(nm_rem, b, 1))
                nc.scalar.activation(nm[:, 1, :], nmr[:, :], ACT.Copy).then_inc(nm_act, 1)

        def act_th(act, b, n):
            act.wait_ge(a_ready, count(a_ready, b, n + 1))
            act.wait_ge(ga_done, count(ga_done, b, n - 1))
            nc.scalar.activation(th[:, n % 2, :], pa[:, :], ACT.Tanh, scale=0.5).then_inc(th_done, 1)

        def act_h2t(act, b):
            act.wait_ge(x2t_ready, count(x2t_ready, b, 1))
            act.wait_ge(moe_in, count(moe_in, b, 0))
            nc.scalar.activation(h2tn[:, :], m0[:, :], ACT.Copy, scale=lnw[:, 1:2]).then_inc(h2t_done, 1)

        def act_ex(act, b):
            act.wait_ge(gate_step, count(gate_step, b, 3))
            nc.scalar.activation(ex[:, :, :], ex[:, :, :], ACT.Exp).then_inc(ex_done, 1)

        def act_wpart(act, b, k):
            if k == 0:
                act.wait_ge(wt_ready, count(wt_ready, b, 1))
                act.wait_ge(moe_in, count(moe_in, b, 0))
                nc.scalar.activation(wstn[:, :], m0[0:SPLIT_ROWS, :], ACT.Copy).then_inc(wpart_act, 1)
            elif k == 1:
                act.wait_ge(wpart_dve, count(wpart_dve, b, 1))
                nc.scalar.activation(wstn[32:64, :], wrem[32:64, :], ACT.Copy).then_inc(wpart_act, 1)
            else:
                nc.scalar.activation(wmid[64:96, :], wrem[64:96, :], ACT.Copy).then_inc(wpart_act, 1)

        def act_ots(act, b):
            act.wait_ge(down_done, count(down_done, b, NE * NF))
            act.wait_ge(ot_ready, count(ot_ready, b, 0))
            nc.scalar.activation(ots[:, :], po[:, :], ACT.Copy).then_inc(ots_done, 1)

        def act_moe(act, b, slot):
            if slot % 5 in (1, 3):
                act_th(act, b, 2 * (slot // 5) + slot % 5 // 2)

        def act_main(act, att=None, moe=None, front=None):
            if moe is not None:
                for slot in range(EARLY_SLOTS):
                    act_moe(act, moe, slot)
            for t in range(ST_TILES):
                if att is not None:
                    if t in (14, 24, 34):
                        act_den(act, att, (t - 14) // 10)
                    act_exp(act, att, t)
                if moe is not None and t in MAIN_SLOTS:
                    act_moe(act, moe, MAIN_SLOTS[t])
                if front is not None:
                    if t == 10:
                        act_ht(act, front)
                    if t in (18, 20, 22, 24):
                        act_part(act, front, (0, 2, 1, 3)[(t - 18) // 2])
                    if t in (21, 27):
                        act_v(act, front, (t - 21) // 6)

        def act_turn(act, post=None, end=None, top=None):
            if post is not None:
                act_den(act, post, NKV - 1)
            for t in range(MT):
                if end is not None:
                    if t in TURN_SLOTS:
                        act_moe(act, end, TURN_SLOTS[t])
                    if t == 36:
                        act_ots(act, end)
                if top is not None:
                    if t == 13:
                        act_keep(act, top)
                    if t == 17:
                        act_vpad(act, top)
                if post is not None:
                    if t == 16:
                        act_h2t(act, post)
                    if t == 23:
                        act_ex(act, post)
                    if t == 36:
                        act_wpart(act, post, 0)
                    if t == 38:
                        act_wpart(act, post, 1)
                        act_wpart(act, post, 2)
                    if t in (37, 41):
                        act_moe_in(act, post, (t - 37) // 4)
            if top is not None:
                act_nm(act, top, 0)
                act_nm(act, top, 1)
            if post is not None:
                act_moe_in(act, post, 2)

        @block.scalar
        def _(act):
            for s, per in credited["scalar"]:
                act.sem_inc(s, per)
            act.wait_ge(loaded, n_first)
            act_ht(act, 0)
            for k in (0, 2, 1, 3):
                act_part(act, 0, k)
            act_v(act, 0, 0)
            act_v(act, 0, 1)
            act.wait_ge(consts, 7)
            act_turn(act, top=0)
            act_main(act, att=0, front=1)
            act_turn(act, post=0, top=1)
            with act.Fori(1, NB - 1) as b:
                act_main(act, att=b, moe=b - 1, front=b + 1)
                act_turn(act, post=b, end=b - 1, top=b + 1)
            act_main(act, att=NB - 1, moe=NB - 2)
            act_turn(act, post=NB - 1, end=NB - 2)
            act_main(act, moe=NB - 1)
            act_turn(act, end=NB - 1)

        def dve_stats(side, src, sem):
            for c in range(TC):
                nc.vector.bn_stats(stats[:, side, c, :], src[:, c, :]).then_inc(sem, 1)

        def dve_aggr(side, sem):
            for c in range(TC):
                nc.vector.bn_aggr(mv[:, side, c, :], stats[:, side, c, :]).then_inc(sem, 1)

        def dve_norm(side, dst, src, sem, rms):
            for c in range(TC):
                r = rt[:, side, 3, c:c + 1]
                if rms:
                    nc.vector.tensor_scalar(dst[:, c, :], src[:, c, :], r, None, ALU.mult).then_inc(sem, 1)
                else:
                    nc.vector.tensor_scalar(dst[:, c, :], src[:, c, :], mv[:, side, c, 0:1], r,
                                            ALU.subtract, ALU.mult).then_inc(sem, 1)

        def dve_in(dve, b, k):
            s = in_step
            if k == 0:
                dve.wait_ge(xa_loaded, count(xa_loaded, b, 16))
                dve.wait_ge(s, count(s, b, 0))
                dve_stats(0, xa, s)
            elif k == 1:
                dve_aggr(0, s)
            elif k == 2:
                dve.wait_ge(in_rstd, count(in_rstd, b, 2))
                dve.wait_ge(kept, count(kept, b, 0))
                dve_norm(0, h0, xa, s, False)
            elif k == 3:
                dve.wait_ge(s, count(s, b, 12))
                dve_stats(0, h0, s)
            elif k == 4:
                dve_aggr(0, s)
            else:
                dve.wait_ge(in_rstd, count(in_rstd, b, 6))
                dve.wait_ge(ht_ready, count(ht_ready, b, 0))
                dve_norm(0, hn, h0, s, True)

        def dve_rope(dve, b, k):
            dve.wait_ge(proj_ready, count(proj_ready, b, (1, 2, 3, 3)[k]))
            if k == 0:
                dve.wait_ge(rope_add, count(rope_add, b, 0))
                dve.wait_ge(part_act, count(part_act, b, 0))
                dve.wait_ge(part_pool, count(part_pool, b, 0))
            if k < 2:
                nc.vector.tensor_tensor(rot[:, k, :], m0[:, :], trig[:, k, :], ALU.mult).then_inc(rope_mul, 1)
            else:
                at = 32 * (k - 2)
                nc.vector.tensor_tensor(rotk[:, k - 2, :], m0[at:at + 32, :], trig[0:32, k - 2, :],
                                        ALU.mult).then_inc(rope_mul, 1)

        def dve_max(dve, b, t):
            c, h, n = MAX_TILES[t]
            dve.wait_ge(max_ready, count(max_ready, b, t + 1))
            if t == 0:
                dve.wait_ge(nm_act, count(nm_act, b, 0))
            nc.vector.reduce_max(mx[:, c, h:h + n],
                                 sp_[:, t % 2, 0:n * (c + 1) * P].rearrange("p (n k) -> p n k", n=n),
                                 mybir.AxisListType.X).then_inc(max_done, 1)

        def dve_nm(dve, b):
            dve.wait_ge(nm_act, count(nm_act, b, 1))
            dve.wait_ge(nm_rem, count(nm_rem, b, 0))
            nc.vector.scalar_tensor_tensor(nmr[:, :], og[0:NHEAD, :], -1.0, nm[:, 0, :],
                                           ALU.mult, ALU.subtract).then_inc(nm_rem, 1)
            dve.wait_ge(nm_act, count(nm_act, b, 2))
            dve.wait_ge(m_loaded, count(m_loaded, b, 0))
            nc.vector.tensor_tensor(nm[:, 2, :], nmr[:, :], nm[:, 1, :], ALU.subtract).then_inc(nm_rem, 1)

        def dve_og(dve, b, group):
            rows32 = slice(32 * group, 32 * group + 32)
            dve.wait_ge(den_done, count(den_done, b, 2 * group + 1))
            nc.vector.tensor_tensor(osum[rows32, :], osum[rows32, :], og[32:64, :], ALU.add).then_inc(og_add, 1)
            dve.wait_ge(og_add, count(og_add, b, 2 * group + 1))
            nc.vector.tensor_tensor(osum[rows32, :], osum[rows32, :], og[0:32, :], ALU.add).then_inc(og_add, 1)

        def dve_og_fin(dve, b, c):
            cols = slice(c * P, (c + 1) * P)
            if c == 0:
                dve.wait_ge(den_done, count(den_done, b, 2 * NKV))
                dve.wait_ge(wo_ready, count(wo_ready, b, 0))
            nc.vector.reciprocal(rec[:, cols], den[:, cols]).then_inc(og_fin, 1)
            dve.wait_ge(og_fin, count(og_fin, b, 2 * c + 1))
            nc.vector.tensor_tensor(ot[:, cols], osum[:, cols], rec[:, cols], ALU.mult).then_inc(og_fin, 1)

        def dve_post(dve, b, k):
            if k == 0:
                dve.wait_ge(wo_ready, count(wo_ready, b, 1))
                dve.wait_ge(kept, count(kept, b, 1))
                dve.wait_ge(moe_in, count(moe_in, b, 0))
                dve.wait_ge(post_step, count(post_step, b, 0))
                nc.vector.tensor_tensor(x2[:, :, :], m0[:, :].rearrange("p (c m) -> p c m", c=TC), hres[:, :, :],
                                        ALU.add).then_inc(x2_done, 1)
            elif k == 1:
                dve.wait_ge(x2_done, count(x2_done, b, 1))
                dve_stats(1, x2, post_step)
            else:
                dve_aggr(1, post_step)

        def over(a, axis):
            return a[:, :, :].unsqueeze(axis).to_broadcast([P, TC, NE, NE])

        def dve_gate(dve, b, k):
            s = gate_step
            v = nc.vector
            if k == 0:
                dve.wait_ge(gate_ready, count(gate_ready, b, 1))
                dve.wait_ge(s, count(s, b, 0))
                i = v.tensor_copy(lg[:, :, :].rearrange("p c e -> p (c e)"), m0[:, 0:TC * NE])
            else:
                dve.wait_ge(s, count(s, b, k))
            if k == 1:
                i = v.reduce_max(lmax[:, :], lg[:, :, :], mybir.AxisListType.X)
            if k == 2:
                i = v.tensor_tensor(ex[:, :, :], lg[:, :, :], lmax[:, :].unsqueeze(2).to_broadcast([P, TC, NE]),
                                    ALU.subtract)
            if k == 3:
                i = v.tensor_tensor(gtm[:, :, :, :], over(lg, 2), over(lg, 3), ALU.is_gt)
            if k == 4:
                i = v.tensor_tensor(eqm[:, :, :, :], over(lg, 2), over(lg, 3), ALU.is_equal)
            if k == 5:
                i = v.tensor_tensor(eqm[:, :, :, :], eqm[:, :, :, :],
                                    tri[:, :, :].unsqueeze(1).to_broadcast([P, TC, NE, NE]), ALU.mult)
            if k == 6:
                i = v.tensor_tensor(gtm[:, :, :, :], gtm[:, :, :, :], eqm[:, :, :, :], ALU.add)
            if k == 7:
                i = v.reduce_sum(rank[:, :, :], gtm[:, :, :, :], mybir.AxisListType.X)
            if k == 8:
                dve.wait_ge(ex_done, count(ex_done, b, 1))
                i = v.scalar_tensor_tensor(rank[:, :, :], rank[:, :, :], 1.5, ex[:, :, :], ALU.is_lt, ALU.mult)
            if k == 9:
                i = v.reduce_sum(wsum[:, 0, :], rank[:, :, :], mybir.AxisListType.X)
            if k == 10:
                i = v.reciprocal(wsum[:, 1, :], wsum[:, 0, :])
            if k == 11:
                dve.wait_ge(wt_ready, count(wt_ready, b, 0))
                i = v.tensor_tensor(wrep[:, :, :, 0:NE], rank[:, :, :].unsqueeze(2).to_broadcast([P, TC, 3, NE]),
                                    wsum[:, 1, :].unsqueeze(2).unsqueeze(3).to_broadcast([P, TC, 3, NE]), ALU.mult)
            i.then_inc(s, 1)

        def dve_wpart(dve, b, k):
            if k == 0:
                dve.wait_ge(wpart_act, count(wpart_act, b, 1))
                dve.wait_ge(wpart_dve, count(wpart_dve, b, 0))
                nc.vector.tensor_tensor(wrem[:, :], m0[0:SPLIT_ROWS, :], wstn[:, :],
                                        ALU.subtract).then_inc(wpart_dve, 1)
            else:
                dve.wait_ge(wpart_act, count(wpart_act, b, 3))
                nc.vector.tensor_tensor(wstn[64:96, :], wrem[64:96, :], wmid[64:96, :],
                                        ALU.subtract).then_inc(wpart_dve, 1)

        def dve_h2e(dve, b, e):
            dve.wait_ge(wbc_ready, count(wbc_ready, b, e + 1))
            dve.wait_ge(b_ready, count(b_ready, b, NF * (e - 1)))
            nc.vector.tensor_tensor(h2e[:, e % 2, :], h2t[:, :], m1[:, :], ALU.mult).then_inc(h2e_done, 1)

        def dve_ga(dve, b, n):
            dve.wait_ge(th_done, count(th_done, b, n + 1))
            dve.wait_ge(g_done, count(g_done, b, n - 1))
            nc.vector.scalar_tensor_tensor(ga[:, n % 2, :], th[:, n % 2, :], 1.0, pa[:, :],
                                           ALU.add, ALU.mult).then_inc(ga_done, 1)

        def dve_g(dve, b, n):
            dve.wait_ge(b_ready, count(b_ready, b, n + 1))
            dve.wait_ge(ga_done, count(ga_done, b, n + 1))
            dve.wait_ge(down_done, count(down_done, b, n - 1))
            nc.vector.scalar_tensor_tensor(g[:, n % 2, :], ga[:, n % 2, :], 0.5, pbk[:, :],
                                           ALU.mult, ALU.mult).then_inc(g_done, 1)

        def dve_end(dve, b, k):
            if k == 0:
                dve.wait_ge(ot_ready, count(ot_ready, b, 1))
                dve.wait_ge(out_done, count(out_done, b, 0))
                dve.wait_ge(moe_in, count(moe_in, b, 3))
                dve.wait_ge(end_step, count(end_step, b, 0))
                nc.vector.tensor_tensor(ye[:, :, :], m1[:, :].rearrange("p (c m) -> p c m", c=TC), x2e[:, :, :],
                                        ALU.add).then_inc(ye_done, 1)
            elif k == 1:
                dve.wait_ge(ye_done, count(ye_done, b, 1))
                dve_stats(2, ye, end_step)
            else:
                dve_aggr(2, end_step)

        def dve_moe(dve, b, slot):
            i, j = slot // 5, slot % 5
            if j == 1:
                dve_ga(dve, b, 2 * i)
            if j == 2:
                dve_g(dve, b, 2 * i)
                if i + 1 < NE:
                    dve_h2e(dve, b, i + 1)
            if j == 3:
                dve_ga(dve, b, 2 * i + 1)
            if j == 4:
                dve_g(dve, b, 2 * i + 1)

        def dve_main(dve, att=None, moe=None, front=None):
            if moe is not None:
                dve_h2e(dve, moe, 0)
            for slot in range(EARLY_SLOTS):
                if front is not None and slot == EARLY_SLOTS - 1:
                    dve.wait_ge(in_step, count(in_step, front, 4))
                if moe is not None:
                    dve_moe(dve, moe, slot)
                if front is not None and slot >= EARLY_SLOTS - 2:
                    dve_in(dve, front, slot - EARLY_SLOTS + 2)
            for t in range(ST_TILES):
                if front is not None and t == 4:
                    dve.wait_ge(in_step, count(in_step, front, 16))
                if att is not None and t in (14, 24, 34):
                    dve_og(dve, att, (t - 14) // 10)
                if moe is not None and t in MAIN_SLOTS:
                    dve_moe(dve, moe, MAIN_SLOTS[t])
                if front is not None:
                    if t in (1, 2, 4, 6):
                        dve_in(dve, front, {1: 2, 2: 3, 4: 4, 6: 5}[t])
                    if t in (13, 15, 17, 18):
                        dve_rope(dve, front, (13, 15, 17, 18).index(t))

        def dve_turn(dve, post=None, end=None, top=None):
            for t in range(MT):
                if post is not None and t == 9:
                    dve.wait_ge(post_step, count(post_step, post, 4))
                if end is not None and t == 40:
                    dve.wait_ge(end_step, count(end_step, end, 4))
                if top is not None:
                    dve_max(dve, top, t)
                if end is not None:
                    if t in TURN_SLOTS:
                        dve_moe(dve, end, TURN_SLOTS[t])
                    if t in (38, 39, 40):
                        dve_end(dve, end, t - 38)
                if post is not None:
                    if t == 0:
                        dve_og(dve, post, NKV - 1)
                    if 1 <= t <= TC:
                        dve_og_fin(dve, post, t - 1)
                    if t == 8:
                        dve_post(dve, post, 0)
                        dve_post(dve, post, 1)
                    if t == 9:
                        dve_post(dve, post, 2)
                    if 19 <= t < 31:
                        dve_gate(dve, post, t - 19)
                    if t in (37, 39):
                        dve_wpart(dve, post, (t - 37) // 2)
            if top is not None:
                dve_nm(dve, top)

        @block.vector
        def _(dve):
            for s, per in credited["vector"]:
                dve.sem_inc(s, per)
            for k in range(6):
                if k in (1, 4):
                    dve.wait_ge(in_step, count(in_step, 0, {1: 4, 4: 16}[k]))
                dve_in(dve, 0, k)
            dve.wait_ge(loaded, n_first)
            for k in range(4):
                dve_rope(dve, 0, k)
            dve_turn(dve, top=0)
            dve.wait_ge(consts, 7)
            dve_main(dve, att=0, front=1)
            dve.wait_ge(rest_loaded, n_rest)
            dve_turn(dve, post=0, top=1)
            with dve.Fori(1, NB - 1) as b:
                dve_main(dve, att=b, moe=b - 1, front=b + 1)
                dve_turn(dve, post=b, end=b - 1, top=b + 1)
            dve_main(dve, att=NB - 1, moe=NB - 2)
            dve_turn(dve, post=NB - 1, end=NB - 2)
            dve_main(dve, moe=NB - 1)
            dve_turn(dve, end=NB - 1)

        def pool_rstd(pool, b, side, done, at, steps, after):
            pool.wait_ge(steps, count(steps, b, after))
            nc.gpsimd.tensor_tensor(rt[:, side, 2, :], mv[:, side, :, 1], eps[:, :], ALU.add).then_inc(done, 1)
            pool.wait_ge(done, count(done, b, at + 1))
            nc.gpsimd.tensor_tensor(rt[:, side, 3, :], rt[:, side, 2, :], mhalf[:, :], ALU.pow).then_inc(done, 1)

        def pool_rms(pool, b, side, done, at, steps, after):
            pool.wait_ge(steps, count(steps, b, after))
            nc.gpsimd.tensor_tensor(rt[:, side, 0, :], mv[:, side, :, 0], mv[:, side, :, 0],
                                    ALU.mult).then_inc(done, 1)
            pool.wait_ge(done, count(done, b, at + 1))
            nc.gpsimd.tensor_tensor(rt[:, side, 1, :], rt[:, side, 0, :], mv[:, side, :, 1],
                                    ALU.add).then_inc(done, 1)
            pool.wait_ge(done, count(done, b, at + 2))
            nc.gpsimd.tensor_tensor(rt[:, side, 2, :], rt[:, side, 1, :], eps[:, :], ALU.add).then_inc(done, 1)
            pool.wait_ge(done, count(done, b, at + 3))
            nc.gpsimd.tensor_tensor(rt[:, side, 3, :], rt[:, side, 2, :], mhalf[:, :], ALU.pow).then_inc(done, 1)

        def pool_add(pool, b, k):
            src, dst = ((rot, qf), (rotk, kf))[k]
            pool.wait_ge(rope_mul, count(rope_mul, b, 2 * k + 2))
            pool.wait_ge(part_act, count(part_act, b, 0))
            pool.wait_ge(part_pool, count(part_pool, b, 0))
            nc.gpsimd.tensor_tensor(dst[:, :], src[:, 0, :], src[:, 1, :], ALU.add).then_inc(rope_add, 1)

        def pool_part(pool, b, k):
            src, parts, rem = ((qf, qp, rot), (kf, kp, rotk))[k // 2]
            if k % 2 == 0:
                pool.wait_ge(part_act, count(part_act, b, 1 if k == 0 else 2))
                pool.wait_ge(rope_add, count(rope_add, b, k // 2 + 1))
                nc.gpsimd.tensor_tensor(rem[:, 0, :], src[:, :], parts[:, 0, :],
                                        ALU.subtract).then_inc(part_pool, 1)
            else:
                pool.wait_ge(part_act, count(part_act, b, 3 if k == 1 else 4))
                nc.gpsimd.tensor_tensor(parts[:, 2, :], rem[:, 0, :], parts[:, 1, :],
                                        ALU.subtract).then_inc(part_pool, 1)

        def pool_h2n(pool, b):
            pool.wait_ge(post_rstd, count(post_rstd, b, 4))
            pool.wait_ge(x2t_ready, count(x2t_ready, b, 0))
            r = rt[:, 1, 3, :].unsqueeze(2).to_broadcast([P, TC, DM])
            nc.gpsimd.tensor_tensor(h2n[:, :, :], x2[:, :, :], r, ALU.mult).then_inc(h2n_done, 1)

        def pool_out(pool, b):
            mean = mv[:, 2, :, 0:1].to_broadcast([P, TC, DM])
            r = rt[:, 2, 3, :].unsqueeze(2).to_broadcast([P, TC, DM])
            pool.wait_ge(end_rstd, count(end_rstd, b, 2))
            pool.wait_ge(out_stored, count(out_stored, b, 0))
            nc.gpsimd.tensor_tensor(yo[:, :, :], ye[:, :, :], mean, ALU.subtract).then_inc(out_done, 1)
            pool.wait_ge(out_done, count(out_done, b, 1))
            nc.gpsimd.tensor_tensor(yo[:, :, :], yo[:, :, :], r, ALU.mult).then_inc(out_done, 1)
            pool.wait_ge(out_done, count(out_done, b, 2))
            pool.wait_ge(xr_loaded, count(xr_loaded, b, 16))
            nc.gpsimd.tensor_tensor(yo[:, :, :], yo[:, :, :], xr[:, :, :], ALU.add).then_inc(out_done, 1)

        def pool_v(pool, b, k):
            if k == 0:
                pool.wait_ge(v_done, count(v_done, b, 2))
                pool.wait_ge(v_rest, count(v_rest, b, 0))
                nc.gpsimd.tensor_tensor(vr[:, :, :, :], vst[:, :, :, :], vb[:, 0], ALU.subtract).then_inc(v_rest, 1)
            else:
                pool.wait_ge(v_done, count(v_done, b, 3))
                nc.gpsimd.tensor_tensor(vb[:, 2], vr[:, :, :, :], vb[:, 1], ALU.subtract).then_inc(v_rest, 1)

        def pool_split(pool, b, t):
            width = sum(SEQ - kc * P for _, kc, _ in pieces(t))
            pool.wait_ge(exp_done, count(exp_done, b, t + 1))
            nc.gpsimd.tensor_tensor(pp[:, t % NPR, 1, 0:width], pt[:, t % NPR, 0:width], pp[:, t % NPR, 0, 0:width],
                                    ALU.subtract).then_inc(split_done, 1)

        def pool_main(pool, att=None, front=None, norms=True):
            if front is not None and norms:
                pool_rstd(pool, front, 0, in_rstd, 0, in_step, 8)
            for t in range(ST_TILES):
                if att is not None:
                    pool_split(pool, att, t)
                if front is not None and norms and t == 3:
                    pool_rms(pool, front, 0, in_rstd, 2, in_step, 20)
                if front is not None:
                    if t in (15, 17):
                        pool_add(pool, front, (t - 15) // 2)
                    if t in (19, 21, 23, 25):
                        pool_part(pool, front, (0, 2, 1, 3)[(t - 19) // 2])
                    if t in (24, 29):
                        pool_v(pool, front, (t - 24) // 5)

        def pool_turn(pool, post=None, end=None, top=None):
            if post is not None:
                pool_rms(pool, post, 1, post_rstd, 0, post_step, 8)
                pool_h2n(pool, post)
            if end is not None:
                pool_rstd(pool, end, 2, end_rstd, 0, end_step, 8)
            if end is not None:
                pool_out(pool, end)

        @block.gpsimd
        def _(pool):
            for s, per in credited["gpsimd"]:
                pool.sem_inc(s, per)
            nc.gpsimd.memset(mhalf[:, :], -0.5).then_inc(consts, 1)
            nc.gpsimd.memset(eps[:, :], EPS).then_inc(consts, 1)
            nc.gpsimd.memset(lift[:, :], LIFT).then_inc(consts, 1)
            pool.wait_ge(consts, 3)
            pool_rstd(pool, 0, 0, in_rstd, 0, in_step, 8)
            nc.gpsimd.memset(k9[:, :, :], 1.0).then_inc(consts, 1)
            pool_rms(pool, 0, 0, in_rstd, 2, in_step, 20)
            pool.wait_ge(loaded, n_first)
            nc.gpsimd.tensor_copy(identb[:, :], ident[:, :]).then_inc(casts, 1)
            nc.gpsimd.tensor_copy(mask[:, :, :], mask32[:, :, :]).then_inc(casts, 1)
            pool_main(pool, front=0, norms=False)
            nc.gpsimd.memset(wrep[:, :, :, :], 0.0).then_inc(consts, 1)
            nc.gpsimd.memset(vpad[:, :, :, :], 0.0).then_inc(consts, 1)
            pool.wait_ge(consts, 6)
            nc.gpsimd.memset(vpad_diag(96), 1.0).then_inc(consts, 1)
            pool.wait_ge(rest_loaded, n_rest)
            nc.gpsimd.tensor_copy(sel[:, :, :], sel32[:, :, :]).then_inc(casts, 1)
            pool_turn(pool, top=0)
            pool_main(pool, att=0, front=1)
            pool_turn(pool, post=0, top=1)
            with pool.Fori(1, NB - 1) as b:
                pool_main(pool, att=b, front=b + 1)
                pool_turn(pool, post=b, end=b - 1, top=b + 1)
            pool_main(pool, att=NB - 1)
            pool_turn(pool, post=NB - 1, end=NB - 2)
            pool_turn(pool, end=NB - 1)


def program(nc, x, out, scratch, w_mamba, w_ffn):
    with ExitStack() as sems:
        mamba_phase(nc, sems, x, scratch["x1"], scratch["c"], w_mamba)
        ffn_phase(nc, sems, scratch["x1"], out, scratch["q"], scratch["k"], w_ffn)


def lay_out_mamba(v):
    def both(name):
        return [np.asarray(v[f"L0_attn_{d}_{name}"]) for d in "fb"]

    win, taps, wx_in, wdt_in = both("Win"), both("convw"), both("Wx"), both("Wdt")
    wx = np.zeros((P, NDIR, NH2, P), np.float32)
    wdt = np.zeros((P, NDIR, DI), np.float32)
    for d in range(NDIR):
        for h in range(NH2):
            t = wx_in[d].T[h * P:(h + 1) * P]
            for part in range(3):
                wx[:, d, h, 32 * part:32 * part + 2 * NS] = t[:, DTR:]
            wx[:, d, h, DT_ROW:DT_ROW + DTR] = t[:, :DTR]
        wdt[DT_ROW:DT_ROW + DTR, d] = wdt_in[d].T
    sel = np.zeros((SPLIT_ROWS, NS, P), np.float32)
    for n in range(NS):
        sel[n::32, n, :] = 1
    return {
        "ident": np.eye(P, dtype=np.float32),
        "win_u": np.stack([a[:DI].T for a in win], 1),
        "win_z": np.stack([a[DI:].T for a in win], 1),
        "tap_w": np.broadcast_to(np.stack([a[:, 0, :].T for a in taps])[None], (P, NDIR, NTAP, DI)),
        "wx": wx,
        "wdt": wdt,
        "wout": np.stack([a.T.reshape(NH2, P, DM).transpose(1, 0, 2) for a in both("Wout")], 1),
        "col": np.stack([np.stack([a.reshape(NH2, P).T for a in c], -1)
                         for c in zip(both("convb"), both("bdt"), both("D"))], 1),
        "alog": np.stack([a.reshape(NH2, P, NS).transpose(1, 0, 2) for a in both("Alog")], 1),
        "ncol": np.stack([np.asarray(v["L0_attn_norm_g"]), np.asarray(v["L0_attn_norm_b"])], 1),
        "sel": sel,
    }


def lay_out_ffn(v):
    def get(name):
        return np.asarray(v["L0_ffn_" + name])

    def swapped(a):
        return a.reshape(-1, 2, HD // 2, DM)[:, ::-1].reshape(a.shape)

    i = np.arange(P)
    causal = np.where(i[None, :] > i[:, None], np.float32(-1e30), np.float32(0))
    inv = np.float32(1) / np.power(np.float32(10000), np.arange(0, HD, 2, dtype=np.float32) / np.float32(HD))
    angle = np.arange(SEQ, dtype=np.float32)[:, None] * inv.astype(np.float32)[None]
    angle = np.concatenate([angle, angle], -1)
    sign = np.where(np.arange(HD) < HD // 2, -1, 1).astype(np.float32)
    wqkv = get("wqkv")
    q, k, value = wqkv[:NHEAD * HD], wqkv[NHEAD * HD:(NHEAD + NKV) * HD], wqkv[(NHEAD + NKV) * HD:]
    sel = np.zeros((SPLIT_ROWS, NE, P), np.float32)
    for e in range(NE):
        sel[e::32, e, :] = 1
    return {
        "ident": np.eye(P, dtype=np.float32),
        "mask": np.stack([causal, causal.T], 1),
        "trig": np.stack([np.tile(np.cos(angle).T, (NHEAD, 1)),
                          np.tile(np.sin(angle).T * sign[:, None], (NHEAD, 1))], 1).astype(np.float32),
        "wq": np.stack([q.T, swapped(q).T], 1),
        "wk": np.concatenate([k.T, swapped(k).T], 1),
        "wv": value.T,
        "wo": get("wo").T,
        "gate": get("gate_w").T,
        "lnw": np.stack([get("ln1_w"), get("ln2_w")], 1),
        "tri": np.broadcast_to(np.tril(np.ones((NE, NE), np.float32), -1)[None], (P, NE, NE)),
        "sel_e": sel,
        "w13": get("w13").transpose(2, 0, 1),
        "w2": get("w2").transpose(2, 0, 1).reshape(NF, P, NE, DM).transpose(1, 2, 0, 3),
    }


def kernel(**inputs):
    import concourse.bacc as bacc
    from concourse.bass_utils import run_bass_kernel_spmd

    nc = bacc.Bacc("TRN2", target_bir_lowering=False, num_devices=1)
    arrays = {}

    def given(prefix, parts):
        aps = {}
        for name, a in parts.items():
            arrays[prefix + name] = np.ascontiguousarray(a)
            aps[name] = nc.dram_tensor(prefix + name, a.shape, F32, kind="ExternalInput").ap()
        return aps

    x = given("in_", {"x": np.asarray(inputs["L0_attn_x"])})["x"]
    w_mamba = given("mamba_", lay_out_mamba(inputs))
    w_ffn = given("ffn_", lay_out_ffn(inputs))
    out = nc.dram_tensor("out", (NB, SEQ, DM), F32, kind="ExternalOutput").ap()
    scratch = {
        "x1": nc.dram_tensor("x1_scratch", (NB, SEQ, DM), F32, kind="Internal").ap(),
        "c": nc.dram_tensor("c_scratch", (NDIR, NS, SEQ), F32, kind="Internal").ap(),
        "q": nc.dram_tensor("q_scratch", (3, HD, NHEAD, SEQ), BF16, kind="Internal").ap(),
        "k": nc.dram_tensor("k_scratch", (3, HD, NKV, SEQ), BF16, kind="Internal").ap(),
    }
    program(nc, x, out, scratch, w_mamba, w_ffn)
    r = run_bass_kernel_spmd(nc, [arrays], core_ids=[0])
    return r.results[0]["out"]
```
